# Optimizing a Trainium2 kernel written in Bass

```python
import numpy as np
import jax
import jax.numpy as jnp

def _softmax(x, axis=-1):
    return jax.nn.softmax(x, axis=axis)

def _gelu(x):
    return jax.nn.gelu(x, approximate=True)

def _silu(x):
    return jax.nn.silu(x)

def _sigmoid(x):
    return jax.nn.sigmoid(x)

def _layernorm(x, axis=-1, eps=1e-05):
    m = jnp.mean(x, axis=axis, keepdims=True)
    v = jnp.var(x, axis=axis, keepdims=True)
    return (x - m) / jnp.sqrt(v + eps)

def _scatter_add(tgt, idx, src, axis=0):
    return tgt.at[idx].add(src)

def _segment_sum(src, seg, n):
    return jax.ops.segment_sum(src, seg, n)
kernel_name = 'mk_recurrent_d2_jaxref_r8_82a54f'

def setup_inputs(seed: int=0):
    np.random.seed(seed)
    _w = jnp.asarray

    def _L0_attn_setup():
        import jax, jax.numpy as jnp
        import numpy as np
        D_MODEL = 512
        NUM_HEADS = 32
        NUM_KV_HEADS = 8
        HEAD_DIM = D_MODEL // NUM_HEADS
        GROUP = NUM_HEADS // NUM_KV_HEADS
        NEG = -1000000000.0
        key = jax.random.key(seed)
        ks = jax.random.split(key, 9)
        B, S = (2, 256)
        s = 0.02
        x = jax.random.normal(ks[0], (B, S, D_MODEL), dtype=jnp.float32)
        Wq = jax.random.normal(ks[1], (D_MODEL, D_MODEL), dtype=jnp.float32) * s
        bq = jax.random.normal(ks[2], (D_MODEL,), dtype=jnp.float32) * s
        Wk = jax.random.normal(ks[3], (D_MODEL, NUM_KV_HEADS * HEAD_DIM), dtype=jnp.float32) * s
        bk = jax.random.normal(ks[4], (NUM_KV_HEADS * HEAD_DIM,), dtype=jnp.float32) * s
        Wv = jax.random.normal(ks[5], (D_MODEL, NUM_KV_HEADS * HEAD_DIM), dtype=jnp.float32) * s
        bv = jax.random.normal(ks[6], (NUM_KV_HEADS * HEAD_DIM,), dtype=jnp.float32) * s
        Wo = jax.random.normal(ks[7], (D_MODEL, D_MODEL), dtype=jnp.float32) * s
        bo = jax.random.normal(ks[8], (D_MODEL,), dtype=jnp.float32) * s
        return {'x': x, 'Wq': Wq, 'bq': bq, 'Wk': Wk, 'bk': bk, 'Wv': Wv, 'bv': bv, 'Wo': Wo, 'bo': bo}
    _L0_attn_in = _L0_attn_setup()

    def _L0_ffn_setup():
        import jax, jax.numpy as jnp
        import numpy as np
        D_MODEL = 512
        D_FF = 1376
        key = jax.random.key(seed)
        k1, k2, k3, k4 = jax.random.split(key, 4)
        x = jax.random.normal(k1, (2, 256, D_MODEL), dtype=jnp.float32)
        W_gate = jax.random.normal(k2, (D_FF, D_MODEL), dtype=jnp.float32) * D_MODEL ** (-0.5)
        W_up = jax.random.normal(k3, (D_FF, D_MODEL), dtype=jnp.float32) * D_MODEL ** (-0.5)
        W_down = jax.random.normal(k4, (D_MODEL, D_FF), dtype=jnp.float32) * D_FF ** (-0.5)
        return {'x': x, 'W_gate': W_gate, 'W_up': W_up, 'W_down': W_down}
    _L0_ffn_in = _L0_ffn_setup()

    def _L1_attn_setup():
        import jax, jax.numpy as jnp
        import numpy as np
        DEPTH, DIM, DFF, VOCAB = (4, 64, 256, 512)
        EPS = 1e-05

        def layernorm(x, w, b):
            mu = jnp.mean(x, axis=-1, keepdims=True)
            var = jnp.mean((x - mu) ** 2, axis=-1, keepdims=True)
            return (x - mu) * jax.lax.rsqrt(var + EPS) * w + b

        def sconv(x, phazor_c, last_conv_c):
            B, L, D = x.shape
            r = jnp.abs(phazor_c)
            p = jnp.tanh(r) * jnp.exp(1j * jnp.angle(phazor_c))
            prog = p[None, :] ** jnp.arange(L, dtype=jnp.float32)[:, None]
            filt_fft = jnp.fft.fft(prog, n=2 * L, axis=0)
            x_fft = jnp.fft.fft(x.astype(jnp.complex64), n=2 * L, axis=1)
            conv = jnp.fft.ifft(filt_fft[None] * x_fft, axis=1)[:, :L]
            conv = conv + last_conv_c[None, None, :] * prog[None] * p[None, None, :]
            return conv.real.astype(x.dtype)

        def _forward(x, Win, bin, ln1_w, ln1_b, phz_re, phz_im, lc_re, lc_im, sc_lin, ln2_w, ln2_b, W1, b1, W2, b2, lnl_w, lnl_b, Wout, bout):
            h = jnp.einsum('blv,dv->bld', x, Win) + bin

            def body(h, p):
                l1w, l1b, pr, pi, lr, li, scl, l2w, l2b, w1, b1_, w2, b2_ = p
                y = jax.nn.silu(layernorm(h, l1w, l1b))
                y = sconv(y, pr + 1j * pi, lr + 1j * li)
                h = h + y * scl
                y = layernorm(h, l2w, l2b)
                y = jax.nn.silu(jnp.einsum('bld,fd->blf', y, w1) + b1_)
                y = jnp.einsum('blf,df->bld', y, w2) + b2_
                return (h + y, None)
            xs = (ln1_w, ln1_b, phz_re, phz_im, lc_re, lc_im, sc_lin, ln2_w, ln2_b, W1, b1, W2, b2)
            h, _ = jax.lax.scan(body, h, xs)
            h = layernorm(h, lnl_w, lnl_b)
            return jnp.einsum('bld,vd->blv', h, Wout) + bout
        key = jax.random.key(seed)
        ks = jax.random.split(key, 20)
        f32 = jnp.float32
        inp = {}
        inp['x'] = jax.random.normal(ks[0], (2, 512, VOCAB), dtype=f32)
        inp['Win'] = jax.random.normal(ks[1], (DIM, VOCAB), dtype=f32) * VOCAB ** (-0.5)
        inp['bin'] = jnp.zeros((DIM,), f32)
        inp['ln1_w'] = jnp.ones((DEPTH, DIM), f32)
        inp['ln1_b'] = jnp.zeros((DEPTH, DIM), f32)
        ang = 2 * np.pi * jnp.arange(DIM, dtype=f32) / DIM
        mag = jnp.abs(jax.random.normal(ks[2], (DEPTH, DIM), dtype=f32))
        inp['phz_re'] = mag * jnp.cos(ang)[None]
        inp['phz_im'] = mag * jnp.sin(ang)[None]
        inp['lc_re'] = jax.random.normal(ks[3], (DEPTH, DIM), dtype=f32)
        inp['lc_im'] = jax.random.normal(ks[4], (DEPTH, DIM), dtype=f32)
        inp['sc_lin'] = jnp.ones((DEPTH, DIM), f32)
        inp['ln2_w'] = jnp.ones((DEPTH, DIM), f32)
        inp['ln2_b'] = jnp.zeros((DEPTH, DIM), f32)
        inp['W1'] = jax.random.normal(ks[5], (DEPTH, DFF, DIM), dtype=f32) * DIM ** (-0.5)
        inp['b1'] = jnp.zeros((DEPTH, DFF), f32)
        inp['W2'] = jax.random.normal(ks[6], (DEPTH, DIM, DFF), dtype=f32) * DFF ** (-0.5)
        inp['b2'] = jnp.zeros((DEPTH, DIM), f32)
        inp['lnl_w'] = jnp.ones((DIM,), f32)
        inp['lnl_b'] = jnp.zeros((DIM,), f32)
        inp['Wout'] = jax.random.normal(ks[7], (VOCAB, DIM), dtype=f32) * DIM ** (-0.5)
        inp['bout'] = jnp.zeros((VOCAB,), f32)
        return inp
    _L1_attn_in = _L1_attn_setup()

    def _L1_ffn_setup():
        import jax, jax.numpy as jnp
        import numpy as np
        H = 512
        I = 1376
        R = 32
        NLEV = 16
        Q_ZERO = 7.5
        Q_STEP = 0.005
        LR_SCALE = 0.02

        def _qlinear(x, q, scale, A, Bm):
            w = (q.astype(jnp.float32) - Q_ZERO) * (scale * Q_STEP)[:, None]
            y = jnp.einsum('bsh,oh->bso', x, w)
            return y + LR_SCALE * (x @ A @ Bm)
        key = jax.random.key(seed)
        ks = jax.random.split(key, 13)
        B, S = (2, 256)
        inp = {'x': jax.random.normal(ks[0], (B, S, H), jnp.float32), 'gate_q': jax.random.randint(ks[1], (I, H), 0, NLEV, jnp.int32), 'gate_scale': jax.random.uniform(ks[2], (I,), jnp.float32), 'gate_A': jax.random.normal(ks[3], (H, R), jnp.float32), 'gate_B': jax.random.normal(ks[4], (R, I), jnp.float32), 'up_q': jax.random.randint(ks[5], (I, H), 0, NLEV, jnp.int32), 'up_scale': jax.random.uniform(ks[6], (I,), jnp.float32), 'up_A': jax.random.normal(ks[7], (H, R), jnp.float32), 'up_B': jax.random.normal(ks[8], (R, I), jnp.float32), 'down_q': jax.random.randint(ks[9], (H, I), 0, NLEV, jnp.int32), 'down_scale': jax.random.uniform(ks[10], (H,), jnp.float32), 'down_A': jax.random.normal(ks[11], (I, R), jnp.float32), 'down_B': jax.random.normal(ks[12], (R, H), jnp.float32)}
        return inp
    _L1_ffn_in = _L1_ffn_setup()
    _d = {'L0_attn_x': _L0_attn_in['x'], 'L0_attn_Wq': _L0_attn_in['Wq'], 'L0_attn_bq': _L0_attn_in['bq'], 'L0_attn_Wk': _L0_attn_in['Wk'], 'L0_attn_bk': _L0_attn_in['bk'], 'L0_attn_Wv': _L0_attn_in['Wv'], 'L0_attn_bv': _L0_attn_in['bv'], 'L0_attn_Wo': _L0_attn_in['Wo'], 'L0_attn_bo': _L0_attn_in['bo'], 'L0_ffn_W_gate': _L0_ffn_in['W_gate'], 'L0_ffn_W_up': _L0_ffn_in['W_up'], 'L0_ffn_W_down': _L0_ffn_in['W_down'], 'L1_attn_Win': _L1_attn_in['Win'], 'L1_attn_bin': _L1_attn_in['bin'], 'L1_attn_ln1_w': _L1_attn_in['ln1_w'], 'L1_attn_ln1_b': _L1_attn_in['ln1_b'], 'L1_attn_phz_re': _L1_attn_in['phz_re'], 'L1_attn_phz_im': _L1_attn_in['phz_im'], 'L1_attn_lc_re': _L1_attn_in['lc_re'], 'L1_attn_lc_im': _L1_attn_in['lc_im'], 'L1_attn_sc_lin': _L1_attn_in['sc_lin'], 'L1_attn_ln2_w': _L1_attn_in['ln2_w'], 'L1_attn_ln2_b': _L1_attn_in['ln2_b'], 'L1_attn_W1': _L1_attn_in['W1'], 'L1_attn_b1': _L1_attn_in['b1'], 'L1_attn_W2': _L1_attn_in['W2'], 'L1_attn_b2': _L1_attn_in['b2'], 'L1_attn_lnl_w': _L1_attn_in['lnl_w'], 'L1_attn_lnl_b': _L1_attn_in['lnl_b'], 'L1_attn_Wout': _L1_attn_in['Wout'], 'L1_attn_bout': _L1_attn_in['bout'], 'L1_ffn_gate_q': _L1_ffn_in['gate_q'], 'L1_ffn_gate_scale': _L1_ffn_in['gate_scale'], 'L1_ffn_gate_A': _L1_ffn_in['gate_A'], 'L1_ffn_gate_B': _L1_ffn_in['gate_B'], 'L1_ffn_up_q': _L1_ffn_in['up_q'], 'L1_ffn_up_scale': _L1_ffn_in['up_scale'], 'L1_ffn_up_A': _L1_ffn_in['up_A'], 'L1_ffn_up_B': _L1_ffn_in['up_B'], 'L1_ffn_down_q': _L1_ffn_in['down_q'], 'L1_ffn_down_scale': _L1_ffn_in['down_scale'], 'L1_ffn_down_A': _L1_ffn_in['down_A'], 'L1_ffn_down_B': _L1_ffn_in['down_B']}
    _x0 = _d['L0_attn_x']
    _d['L0_attn_x'] = jax.random.normal(jax.random.fold_in(jax.random.key(seed), 1), (4, 256, 512), dtype=_x0.dtype)
    del _x0
    return _d

def reference(L0_attn_x, L0_attn_Wq, L0_attn_bq, L0_attn_Wk, L0_attn_bk, L0_attn_Wv, L0_attn_bv, L0_attn_Wo, L0_attn_bo, L0_ffn_W_gate, L0_ffn_W_up, L0_ffn_W_down, L1_attn_Win, L1_attn_bin, L1_attn_ln1_w, L1_attn_ln1_b, L1_attn_phz_re, L1_attn_phz_im, L1_attn_lc_re, L1_attn_lc_im, L1_attn_sc_lin, L1_attn_ln2_w, L1_attn_ln2_b, L1_attn_W1, L1_attn_b1, L1_attn_W2, L1_attn_b2, L1_attn_lnl_w, L1_attn_lnl_b, L1_attn_Wout, L1_attn_bout, L1_ffn_gate_q, L1_ffn_gate_scale, L1_ffn_gate_A, L1_ffn_gate_B, L1_ffn_up_q, L1_ffn_up_scale, L1_ffn_up_A, L1_ffn_up_B, L1_ffn_down_q, L1_ffn_down_scale, L1_ffn_down_A, L1_ffn_down_B):

    def _L0_attn_ref(x, Wq, bq, Wk, bk, Wv, bv, Wo, bo):
        import jax, jax.numpy as jnp
        import numpy as np
        D_MODEL = 512
        NUM_HEADS = 32
        NUM_KV_HEADS = 8
        HEAD_DIM = D_MODEL // NUM_HEADS
        GROUP = NUM_HEADS // NUM_KV_HEADS
        NEG = -1000000000.0
        B, S, _ = x.shape
        q = (x @ Wq + bq).reshape(B, S, NUM_HEADS, HEAD_DIM).transpose(0, 2, 1, 3)
        k = (x @ Wk + bk).reshape(B, S, NUM_KV_HEADS, HEAD_DIM).transpose(0, 2, 1, 3)
        v = (x @ Wv + bv).reshape(B, S, NUM_KV_HEADS, HEAD_DIM).transpose(0, 2, 1, 3)
        k = jnp.repeat(k, GROUP, axis=1)
        v = jnp.repeat(v, GROUP, axis=1)
        scores = jnp.einsum('bhqd,bhkd->bhqk', q, k) / jnp.sqrt(jnp.asarray(HEAD_DIM, dtype=jnp.float32))
        causal = jnp.tril(jnp.ones((S, S), dtype=bool))
        scores = jnp.where(causal, scores, NEG)
        p = jax.nn.softmax(scores, axis=-1)
        out = jnp.einsum('bhqk,bhkd->bhqd', p, v)
        out = out.transpose(0, 2, 1, 3).reshape(B, S, D_MODEL)
        return out @ Wo + bo

    def _L0_ffn_ref(x, W_gate, W_up, W_down):
        import jax, jax.numpy as jnp
        import numpy as np
        D_MODEL = 512
        D_FF = 1376
        out_shape = x.shape[:-1] + (W_down.shape[0],)
        xf = x.reshape(-1, x.shape[-1])
        up = jnp.einsum('td,fd->tf', xf, W_up)
        gate = jax.nn.silu(jnp.einsum('td,fd->tf', xf, W_gate))
        h = gate * up
        y = jnp.einsum('tf,df->td', h, W_down)
        return y.reshape(out_shape)

    def _L1_attn_ref(x, Win, bin, ln1_w, ln1_b, phz_re, phz_im, lc_re, lc_im, sc_lin, ln2_w, ln2_b, W1, b1, W2, b2, lnl_w, lnl_b, Wout, bout):
        import jax, jax.numpy as jnp
        import numpy as np
        DEPTH, DIM, DFF, VOCAB = (4, 64, 256, 512)
        EPS = 1e-05

        def layernorm(x, w, b):
            mu = jnp.mean(x, axis=-1, keepdims=True)
            var = jnp.mean((x - mu) ** 2, axis=-1, keepdims=True)
            return (x - mu) * jax.lax.rsqrt(var + EPS) * w + b

        def sconv(x, phazor_c, last_conv_c):
            B, L, D = x.shape
            r = jnp.abs(phazor_c)
            p = jnp.tanh(r) * jnp.exp(1j * jnp.angle(phazor_c))
            prog = p[None, :] ** jnp.arange(L, dtype=jnp.float32)[:, None]
            filt_fft = jnp.fft.fft(prog, n=2 * L, axis=0)
            x_fft = jnp.fft.fft(x.astype(jnp.complex64), n=2 * L, axis=1)
            conv = jnp.fft.ifft(filt_fft[None] * x_fft, axis=1)[:, :L]
            conv = conv + last_conv_c[None, None, :] * prog[None] * p[None, None, :]
            return conv.real.astype(x.dtype)

        def _forward(x, Win, bin, ln1_w, ln1_b, phz_re, phz_im, lc_re, lc_im, sc_lin, ln2_w, ln2_b, W1, b1, W2, b2, lnl_w, lnl_b, Wout, bout):
            h = jnp.einsum('blv,dv->bld', x, Win) + bin

            def body(h, p):
                l1w, l1b, pr, pi, lr, li, scl, l2w, l2b, w1, b1_, w2, b2_ = p
                y = jax.nn.silu(layernorm(h, l1w, l1b))
                y = sconv(y, pr + 1j * pi, lr + 1j * li)
                h = h + y * scl
                y = layernorm(h, l2w, l2b)
                y = jax.nn.silu(jnp.einsum('bld,fd->blf', y, w1) + b1_)
                y = jnp.einsum('blf,df->bld', y, w2) + b2_
                return (h + y, None)
            xs = (ln1_w, ln1_b, phz_re, phz_im, lc_re, lc_im, sc_lin, ln2_w, ln2_b, W1, b1, W2, b2)
            h, _ = jax.lax.scan(body, h, xs)
            h = layernorm(h, lnl_w, lnl_b)
            return jnp.einsum('bld,vd->blv', h, Wout) + bout
        return _forward(x, Win, bin, ln1_w, ln1_b, phz_re, phz_im, lc_re, lc_im, sc_lin, ln2_w, ln2_b, W1, b1, W2, b2, lnl_w, lnl_b, Wout, bout)

    def _L1_ffn_ref(x, gate_q, gate_scale, gate_A, gate_B, up_q, up_scale, up_A, up_B, down_q, down_scale, down_A, down_B):
        import jax, jax.numpy as jnp
        import numpy as np
        H = 512
        I = 1376
        R = 32
        NLEV = 16
        Q_ZERO = 7.5
        Q_STEP = 0.005
        LR_SCALE = 0.02

        def _qlinear(x, q, scale, A, Bm):
            w = (q.astype(jnp.float32) - Q_ZERO) * (scale * Q_STEP)[:, None]
            y = jnp.einsum('bsh,oh->bso', x, w)
            return y + LR_SCALE * (x @ A @ Bm)
        g = _qlinear(x, gate_q, gate_scale, gate_A, gate_B)
        u = _qlinear(x, up_q, up_scale, up_A, up_B)
        h = jax.nn.silu(g) * u
        return _qlinear(h, down_q, down_scale, down_A, down_B)
    x = L0_attn_x
    xn = _layernorm(x, axis=-1)
    s = _L0_attn_ref(xn, L0_attn_Wq, L0_attn_bq, L0_attn_Wk, L0_attn_bk, L0_attn_Wv, L0_attn_bv, L0_attn_Wo, L0_attn_bo)
    g = _silu(_L0_ffn_ref(xn, L0_ffn_W_gate, L0_ffn_W_up, L0_ffn_W_down))
    x = x + s * g
    xn = _layernorm(x, axis=-1)
    s = _L1_attn_ref(xn, L1_attn_Win, L1_attn_bin, L1_attn_ln1_w, L1_attn_ln1_b, L1_attn_phz_re, L1_attn_phz_im, L1_attn_lc_re, L1_attn_lc_im, L1_attn_sc_lin, L1_attn_ln2_w, L1_attn_ln2_b, L1_attn_W1, L1_attn_b1, L1_attn_W2, L1_attn_b2, L1_attn_lnl_w, L1_attn_lnl_b, L1_attn_Wout, L1_attn_bout)
    g = _silu(_L1_ffn_ref(xn, L1_ffn_gate_q, L1_ffn_gate_scale, L1_ffn_gate_A, L1_ffn_gate_B, L1_ffn_up_q, L1_ffn_up_scale, L1_ffn_up_A, L1_ffn_up_B, L1_ffn_down_q, L1_ffn_down_scale, L1_ffn_down_A, L1_ffn_down_B))
    x = x + s * g
    return x

_drawn_inputs = setup_inputs


def setup_inputs(seed=0):
    import zlib

    import numpy as np

    out = dict(_drawn_inputs(seed))
    spreads = {'L1_attn_bin': (0.0, 0.1),
     'L1_attn_ln1_w': (1.0, 0.2),
     'L1_attn_ln1_b': (0.0, 0.1),
     'L1_attn_sc_lin': (1.0, 0.2),
     'L1_attn_ln2_w': (1.0, 0.2),
     'L1_attn_ln2_b': (0.0, 0.1),
     'L1_attn_b1': (0.0, 0.1),
     'L1_attn_b2': (0.0, 0.1),
     'L1_attn_lnl_w': (1.0, 0.2),
     'L1_attn_lnl_b': (0.0, 0.1),
     'L1_attn_bout': (0.0, 0.1)}
    factors = {'L0_attn_Wq': 8.0,
     'L0_attn_bq': 8.0,
     'L0_attn_Wk': 8.0,
     'L0_attn_bk': 8.0,
     'L0_attn_bv': 6.529,
     'L0_attn_bo': 3.426}
    for name, (base, spread) in spreads.items():
        noise = np.random.default_rng([zlib.crc32(name.encode()), seed]).standard_normal(out[name].shape)
        drawn = base * np.exp(spread * noise) if base else spread * noise
        out[name] = jnp.asarray(drawn.astype(out[name].dtype))
    for name, factor in factors.items():
        out[name] = (out[name] * factor).astype(out[name].dtype)
    return out
```

```python
from contextlib import ExitStack

import concourse.bass as bass
from concourse import mybir

F32 = mybir.dt.float32
F32R = mybir.dt.float32r
BF16 = mybir.dt.bfloat16
I32 = mybir.dt.int32
ALU = mybir.AluOpType
ACT = mybir.ActivationFunctionType
AX_X = mybir.AxisListType.X

P = 128
TOK = 1024
SEQ = 256
D = 512
KD = D // P
NT = TOK // P
HALF = 512
NKV = 8
GRP = 4
DH = 16
F = 1376
NF = 11
FW = [P] * (NF - 1) + [F - (NF - 1) * P]
DEPTH = 4
CH = 64
RANK = 32
LRR = 3 * RANK
SW = 1312
RW = 1056
EPS = 1e-5
MASKED = -1e30

COLS = {}
_at = 0
for _name, _n in (("bq", 4), ("bk", 1), ("ln1_w", 4), ("ln1_b", 4), ("scl", 4), ("ln2_w", 4), ("ln2_b", 4),
                  ("b2", 4), ("b1", 8), ("lnl_w", 1), ("lnl_b", 1), ("bin", 1), ("lc_a", 4), ("lc_b", 4),
                  ("ph_re", 4), ("ph_im", 4), ("gate_s", NF), ("up_s", NF)):
    COLS[_name] = (_at, _at + _n)
    _at += _n
NCOLS = _at


def weight_chunks():
    chunks = [("qkv", 0), ("qkv", 1), ("qkv", 2), ("wo", 0), ("wo", 1)]
    chunks += [("gu0", i) for i in range(NF)] + [("dn0", i) for i in range(6)]
    chunks += [("win", 0), ("lra", 0)]
    for _ in range(2):
        chunks += [("gu1", i) for i in range(NF)] + [("lrd", 0), ("lrb", 0)] + [("dn1", i) for i in range(6)]
    return chunks


CHUNKS = weight_chunks()
IN_RING = ("wo", "gu0", "dn0", "lra", "gu1", "lrd", "dn1")
N_STAGE = 2
N_RING = 2


def chunk_place(kind, index, half=0):
    seen = -1
    ring = 0
    for c, (k, i) in enumerate(CHUNKS):
        if (k, i) == (kind, index):
            seen += 1
            if seen == half:
                return c, ring
        ring += k in IN_RING
    raise ValueError(kind)


def chunk_dmas(kind):
    return {"qkv": 1, "gu1": 2}.get(kind, 1)


def stage_value(c):
    return 16 * sum(chunk_dmas(CHUNKS[x][0]) + (CHUNKS[x] == ("qkv", 2)) for x in range(c % N_STAGE, c + 1, N_STAGE))


LN_STEPS = ("mean", "var", "rstd")
SSM_STEPS = [(l, s) for l in range(DEPTH) for s in
             ("mean1", "var1", "rstd1", "sel", "comb", "mean2", "var2", "rstd2", "w1a", "w1b", "w2")]
SSM_STEPS += [(DEPTH, s) for s in ("mean1", "var1", "rstd1")]


def layer1_order():
    order = [("lowrank", 0, 0)]
    n = 0
    for half in range(2):
        for i in range(NF):
            for kind in ("gate", "up"):
                order.append((kind, half, i))
                if n < len(SSM_STEPS):
                    order.append(("ssm", n, 0))
                    n += 1
        order.append(("flush", half, 0))
        order.append(("rd", half, 0))
        for i in range(6):
            order.append(("dn", half, i))
            if n < len(SSM_STEPS):
                order.append(("ssm", n, 0))
                n += 1
        if half == 1:
            order.append(("wout", 0, 0))
        order.append(("fin", half, 0))
    assert n == len(SSM_STEPS)
    return order


ORDER1 = layer1_order()


def build(nc, A):
    ctx = ExitStack()
    with ctx:
        def common(name, shape, dt=F32):
            return ctx.enter_context(nc.sbuf_tensor(name, shape, dt))

        def sem(name):
            return ctx.enter_context(nc.semaphore(name))

        x = common("x_sb", [P, NT, D])
        xnT = common("xnT", [P, 2, KD, TOK], F32R)
        s_sb = common("s_sb", [P, NT, D])
        stage = common("stage", [P, N_STAGE, SW])
        ring = common("ring", [P, N_RING, 2, RW], F32R)
        xn = common("xn", [P, 2, D])
        ident = common("ident", [P, P])
        cols = common("cols", [P, NCOLS])
        row_b = common("row_b", [P, D])
        bn6 = common("bn6", [P, NT, 6])
        mv = common("mv", [P, NT, 2])
        ve = common("ve", [P, NT])
        rstd = common("rstd", [P, NT])
        nhalf = common("nhalf", [P, 8])
        PS = ctx.enter_context(nc.psum_tensor("PS", [P, 8, 512], F32))

        with ExitStack() as scope:
            def att(name, shape, dt=F32):
                return scope.enter_context(nc.sbuf_tensor(name, shape, dt))

            wqkv = att("wqkv", [P, 2, KD, 768], F32R)
            qs = att("qs", [P, 4, GRP, HALF], F32R)
            ks = att("ks", [P, 4, HALF], F32R)
            v_sb = att("v_sb", [P, NT, NKV, DH + 1])
            probs = att("probs", [P, 6, GRP * P])
            proj = att("proj", [P, HALF])
            proj_hl = att("proj_hl", [P, 2, 2, HALF], F32R)
            att_tok = att("att_tok", [P, 2, D])
            attT = att("attT", [P, 2, KD, P], F32R)
            max_hl = att("max_hl", [32, 2, SEQ], F32R)
            negmax = att("negmax", [P, 4, 2, 32])
            maskA = att("maskA", [P, 4, P], BF16)
            maskB = att("maskB", [P, 2, SEQ], BF16)
            identb = att("identb", [P, P], BF16)
            bv_b = att("bv_b", [P, P])
            bq4 = att("bq4", [P, 4])
            rden = att("rden", [P, 8])
        def late(name, shape, dt=F32):
            return ctx.enter_context(nc.sbuf_tensor(name, shape, dt))

        rot = late("rot", [P, DEPTH, SEQ])
        decay = late("decay", [P, DEPTH])
        first = late("first", [P, DEPTH])
        win_hl = late("win_hl", [P, 2, KD, 3 * CH], F32R)
        with ExitStack() as scope:
            def ff0(name, shape, dt=F32):
                return scope.enter_context(nc.sbuf_tensor(name, shape, dt))

            hid0 = ff0("hid0", [P, 2, NF, TOK], F32R)
            sg0 = ff0("sg0", [P, 2, HALF])
            ht0 = ff0("ht0", [P, 2, HALF])
            rotb = ff0("rotb", [P, DEPTH, SEQ // 2])
            cs = ff0("cs", [P, 12, DEPTH])
        rtmp = xn[:].rearrange("p a (l t) -> p a l t", l=DEPTH)
        hid1 = late("hid1", [P, 2, NF, HALF], F32R)
        lrx = late("lrx", [LRR, 2, TOK], F32R)
        lrh = late("lrh", [LRR, HALF], F32R)
        lrdb = late("lrdb", [LRR, D], F32R)
        dscale_b = late("dscale_b", [P, D])
        ssmw = late("ssmw", [P, DEPTH * 256 + DEPTH * 2 * CH + D])
        gs = late("gs", [P, 2, NF])
        e_lr = late("e_lr", [P, 2, HALF])
        e_gu = late("e_gu", [P, 2, HALF])
        e_h = xn[:, 1, :]
        h = late("h", [P, HALF])
        cen = late("cen", [P, HALF])
        tmp1 = late("tmp1", [P, HALF])
        act1 = late("act1", [P, HALF])
        dz = late("dz", [P, 2, HALF])
        sv = late("sv", [P, 2, 2, HALF])
        dmat = xn[:, 0, :]
        sel = late("sel", [P, 2, P])
        comb = late("comb", [P, 2, P])
        bd = late("bd", [P, P])
        bdc = late("bdc", [P, 2])
        tstat = late("tstat", [P, 8])
        trs = late("trs", [P, 8])

        w1v = ssmw[:, 0:DEPTH * 256].rearrange("p (l f) -> p l f", l=DEPTH)
        w2v = ssmw[:, DEPTH * 256:DEPTH * 256 + DEPTH * 2 * CH].rearrange("p (l t c) -> p l t c", l=DEPTH, t=2)
        wov = ssmw[:, DEPTH * 256 + DEPTH * 2 * CH:]

        def col(name, i=0, n=1):
            return cols[:, COLS[name][0] + i:COLS[name][0] + i + n]

        q_bounce = nc.dram_tensor("q_bounce", [2, 5, P, TOK], F32).ap()
        m_bounce = nc.dram_tensor("m_bounce", [2, 4, 32, SEQ], F32).ap()

        x_loaded = [sem(f"x_loaded{t}") for t in range(NT)]
        cols_loaded = sem("cols_loaded")
        bv_loaded = sem("bv_loaded")
        bo_loaded = sem("bo_loaded")
        late_loaded = sem("late_loaded")
        stage_loaded = [sem(f"stage_loaded{i}") for i in range(N_STAGE)]
        split_done = sem("split_done")
        chunk_used = sem("chunk_used")
        ident_ready = sem("ident_ready")
        consts_ready = sem("consts_ready")
        var_ready = sem("var_ready")
        rstd_ready = sem("rstd_ready")
        xn_ready = sem("xn_ready")
        xt_ready = sem("xt_ready")
        xh_ready = sem("xh_ready")
        xl_ready = sem("xl_ready")
        qkv_ready = sem("qkv_ready")
        proj_ready = sem("proj_ready")
        proj_split = sem("proj_split")
        v_ready = sem("v_ready")
        q_out = [sem(f"q_out{i}") for i in range(2)]
        qs_loaded = [sem(f"qs_loaded{m}") for m in range(4)]
        ks_loaded = sem("ks_loaded")
        s1_ready = sem("s1_ready")
        max_ready = sem("max_ready")
        mt_ready = sem("mt_ready")
        mh_ready = sem("mh_ready")
        ml_ready = sem("ml_ready")
        m_out = sem("m_out")
        m_loaded = [sem(f"m_loaded{i}") for i in range(2)]
        s2_ready = sem("s2_ready")
        exp_ready = sem("exp_ready")
        masked = sem("masked")
        pv_ready = sem("pv_ready")
        att_ready = sem("att_ready")
        at_ready = sem("at_ready")
        ah_ready = sem("ah_ready")
        al_ready = sem("al_ready")
        wo_ready = sem("wo_ready")
        s_ready = sem("s_ready")
        gu_ready = sem("gu_ready")
        gate_used = sem("gate_used")
        up_used = sem("up_used")
        hid_ready = sem("hid_ready")
        dn_ready = sem("dn_ready")
        g_ready = sem("g_ready")
        x1_ready = sem("x1_ready")
        lr_ready = sem("lr_ready")
        lr_copied = sem("lr_copied")
        lr_split = sem("lr_split")
        phasor_scaled = sem("phasor_scaled")
        polar_ready = sem("polar_ready")
        decay_ready = sem("decay_ready")
        rot_ready = sem("rot_ready")
        late_consts = sem("late_consts")
        gsum_ready = sem("gsum_ready")
        silu_ready = sem("silu_ready")
        fsum_ready = sem("fsum_ready")
        fg_ready = sem("fg_ready")
        rd_ready = sem("rd_ready")
        rd_copied = sem("rd_copied")
        rd_split = sem("rd_split")
        h0_ready = sem("h0_ready")
        h_ready = sem("h_ready")
        ln_mean = sem("ln_mean")
        ln_cen = sem("ln_cen")
        ln_sq = sem("ln_sq")
        ln_var = sem("ln_var")
        ln_stat = sem("ln_stat")
        ln_pow = sem("ln_pow")
        ln_spread = sem("ln_spread")
        ln_rstd = sem("ln_rstd")
        ln_norm = sem("ln_norm")
        ln_out = sem("ln_out")
        cv_sel = sem("cv_sel")
        cv_mod = sem("cv_mod")
        cv_comb = sem("cv_comb")
        w1_ready = sem("w1_ready")
        w1_act = sem("w1_act")
        w2_ready = sem("w2_ready")
        lrd_ready = sem("lrd_ready")
        win_ready = sem("win_ready")
        wout_ready = sem("wout_ready")
        out_ready = sem("out_ready")
        stored = sem("stored")
        dve_chain = sem("dve_chain")
        pool_chain = sem("pool_chain")
        act_chain = sem("act_chain")

        block = ctx.enter_context(nc.Block())

        @block.sync
        def _(sp):
            xd = A["x"].rearrange("(t p) d -> t p d", p=P)

            def chunk_load(c):
                kind, i = CHUNKS[c]
                if c >= N_STAGE:
                    sp.wait_ge(split_done, c - N_STAGE + 1)
                slot = stage[:, c % N_STAGE, :]
                done = stage_loaded[c % N_STAGE]
                if kind == "qkv" and i < 2:
                    sp.dma_start(slot[:, 0:1024].rearrange("p (k n) -> p k n", k=KD),
                                 A["wq"].rearrange("(k p) n -> p k n", p=P)[:, :, 256 * i:256 * i + 256]).then_inc(done, 16)
                elif kind == "qkv":
                    v = slot[:, 0:1024].rearrange("p (k n) -> p k n", k=KD)
                    sp.dma_start(v[:, :, 0:128], A["wk"].rearrange("(k p) n -> p k n", p=P)).then_inc(done, 16)
                    sp.dma_start(v[:, :, 128:256], A["wv"].rearrange("(k p) n -> p k n", p=P)).then_inc(done, 16)
                elif kind == "wo":
                    sp.dma_start(slot[:, 0:1024].rearrange("p (k n) -> p k n", k=2),
                                 A["wo"].rearrange("(k p) n -> p k n", p=P)[:, 2 * i:2 * i + 2, :]).then_inc(done, 16)
                elif kind == "gu0":
                    sp.dma_start(slot[:, 0:8 * FW[i]], A["gu0"][:, 1024 * i:1024 * i + 8 * FW[i]]).then_inc(done, 16)
                elif kind == "gu1":
                    sp.dma_start(slot[:, 0:8 * FW[i]].bitcast(I32), A["gu1"][:, 1024 * i:1024 * i + 8 * FW[i]]).then_inc(done, 16)
                    sp.dma_start(slot[0:LRR, 1024:1024 + 2 * FW[i]], A["lrb"][:, 256 * i:256 * i + 2 * FW[i]]).then_inc(done, 16)
                elif kind in ("dn0", "dn1"):
                    w = A[kind]
                    if i < 5:
                        to = slot[:, 0:1024].rearrange("p (k n) -> p k n", k=2)
                        of = w[256 * i:256 * i + 256, :].rearrange("(k p) n -> p k n", p=P)
                    else:
                        to = slot[0:FW[-1], 0:512]
                        of = w[1280:F, :]
                    sp.dma_start(to if kind == "dn0" else to.bitcast(I32), of).then_inc(done, 16)
                elif kind == "win":
                    sp.dma_start(slot[:, 0:256].rearrange("p (k n) -> p k n", k=KD),
                                 A["winT"].rearrange("(k p) n -> p k n", p=P)).then_inc(done, 16)
                elif kind == "lra":
                    sp.dma_start(slot[:, 0:768], A["lra"]).then_inc(done, 16)
                elif kind == "lrd":
                    sp.dma_start(slot[:, 0:1056], A["lrd"]).then_inc(done, 16)
                elif kind == "lrb":
                    sp.dma_start(slot[0:LRR, 0:512], A["lrdb"]).then_inc(done, 16)

            for t in range(2):
                sp.dma_start(x[:, t, :], xd[t]).then_inc(x_loaded[t], 16)
            for c in range(2):
                chunk_load(c)
            for t in range(2, NT):
                sp.dma_start(x[:, t, :], xd[t]).then_inc(x_loaded[t], 16)
            sp.dma_start(cols[:], A["cols"]).then_inc(cols_loaded, 16)
            sp.dma_start(bv_b[:], A["bv"].to_broadcast([P, P])).then_inc(bv_loaded, 16)
            sp.dma_start(row_b[:], A["bo"].to_broadcast([P, D])).then_inc(bo_loaded, 16)
            for c in range(2, 5):
                chunk_load(c)
            for half in range(2):
                t0 = half * HALF
                for u in range(5):
                    n = 5 * half + u
                    sp.wait_ge(proj_split, n + 1)
                    for part in range(2):
                        sp.dma_start(q_bounce[part, u, :, t0:t0 + HALF],
                                     proj_hl[:, n % 2, part, :].bitcast(F32)).then_inc(q_out[n % 2], 16)
                    sp.wait_ge(q_out[n % 2], 32 * (n // 2 + 1))
                    if half == 1 and u == 0:
                        sp.wait_ge(s2_ready, 48)
                    for j in range(2):
                        for row, part in ((0, 0), (1, u < 4 and 0 or 1), (2, u < 4 and 1 or 0)):
                            r0 = 64 * j + DH * row
                            if u < 4:
                                src = q_bounce[part, u, 64 * j:64 * j + 64, t0:t0 + HALF].rearrange("(g r) t -> r g t", r=DH)
                                sp.dma_start(qs[r0:r0 + DH, u, :, :].bitcast(F32), src).then_inc(qs_loaded[u], 16)
                            else:
                                src = q_bounce[part, 4, :, t0:t0 + HALF].rearrange("(m j r) t -> j r m t", j=2, r=DH)[j]
                                if half == 0:
                                    sp.wait_ge(consts_ready, 1)
                                sp.dma_start(ks[r0:r0 + DH, :, :].bitcast(F32), src).then_inc(ks_loaded, 16)
                for bb in range(2):
                    b = 2 * half + bb
                    sp.wait_ge(ml_ready, b + 1)
                    for part in range(2):
                        sp.dma_start(m_bounce[part, b], max_hl[:, part, :].bitcast(F32)).then_inc(m_out, 16)
                    sp.wait_ge(m_out, 32 * (b + 1))
                    for part in range(2):
                        for j in range(2):
                            src = m_bounce[part, b].rearrange("(o m j g) t -> j o m g t", o=1, j=2, g=GRP)[j]
                            r0 = 64 * j + 3 * DH + part
                            sp.dma_start(qs[r0:r0 + 1, :, :, bb * SEQ:(bb + 1) * SEQ].bitcast(F32), src).then_inc(m_loaded[bb], 16)
            for c in range(5, 22):
                chunk_load(c)
            sp.wait_ge(s_ready, NT)
            sp.wait_ge(dn_ready, NT)
            sp.wait_ge(hid_ready, 2 * NF)
            sp.dma_start(row_b[:], A["bout"].to_broadcast([P, D])).then_inc(late_loaded, 16)
            sp.dma_start(dscale_b[:], A["dscale"].to_broadcast([P, D])).then_inc(late_loaded, 16)
            sp.dma_start(ssmw[:], A["ssmw"]).then_inc(late_loaded, 16)
            for c in range(22, len(CHUNKS)):
                chunk_load(c)
            od = A["out"].rearrange("(t p) d -> t p d", p=P)
            for t in range(NT):
                sp.wait_ge(out_ready, t + 1)
                sp.dma_start(od[t], x[:, t, :]).then_inc(stored, 16)
            sp.wait_ge(stored, 16 * NT)

        @block.gpsimd
        def _(pool):
            chain = [0]

            def link(ins):
                chain[0] += 1
                ins.then_inc(pool_chain, 1)
                pool.wait_ge(pool_chain, chain[0])

            signals = {}

            def signal(ins, done):
                signals[done.name] = signals.get(done.name, 0) + 1
                ins.then_inc(done, 1)
                pool.wait_ge(done, signals[done.name])

            def split(dst_hi, dst_lo, src, wait=True):
                link(pool.tensor_copy(dst_hi, src))
                return pool.tensor_tensor(dst_lo, src, dst_hi.bitcast(F32), ALU.subtract)

            def last_use(c):
                before = [x for x in range(c) if CHUNKS[x][0] in IN_RING][-N_RING]
                kind, i = CHUNKS[before]
                half = CHUNKS[:before].count(CHUNKS[before])
                if kind == "wo":
                    return wo_ready, NT
                if kind == "gu0":
                    return gu_ready, 2 * i + 2
                if kind == "gu1":
                    return gu_ready, 2 * NF + NF * half + i + 1
                if kind == "lra":
                    return lr_ready, 4
                if kind == "lrd":
                    return rd_ready, half + 1
                if i == 5:
                    return dn_ready, NT if kind == "dn0" else NT + 4 * half + 4
                return chunk_used, i + 1 if kind == "dn0" else 5 + 5 * half + i + 1

            def chunk_split(c):
                kind, i = CHUNKS[c]
                slot = stage[:, c % N_STAGE, :]
                pool.wait_ge(stage_loaded[c % N_STAGE], stage_value(c))
                rc = sum(k in IN_RING for k, _ in CHUNKS[:c])
                w = ring[:, rc % N_RING, :, :]
                if kind in IN_RING and rc >= N_RING:
                    pool.wait_ge(*last_use(c))
                if kind == "qkv":
                    to = wqkv[:, :, :, 256 * i:256 * i + 256]
                    of = slot[:, 0:1024].rearrange("p (k n) -> p k n", k=KD)
                    signal(split(to[:, 0], to[:, 1], of), split_done)
                elif kind in ("wo", "gu0", "dn0", "lra", "lrd"):
                    n = {"wo": 1024, "gu0": 8 * FW[i % NF], "dn0": 1024, "lra": 768, "lrd": 1056}[kind]
                    rows = P
                    if kind == "dn0" and i == 5:
                        n, rows = 512, FW[-1]
                    signal(split(w[0:rows, 0, 0:n], w[0:rows, 1, 0:n], slot[0:rows, 0:n]), split_done)
                elif kind == "win":
                    link(pool.memset(win_hl[:].bitcast(F32), 0.0))
                    of = slot[:, 0:256].rearrange("p (k n) -> p k n", k=KD)
                    signal(split(win_hl[:, 0, :, CH:2 * CH], win_hl[:, 1, :, CH:2 * CH], of), split_done)
                elif kind == "gu1":
                    link(pool.tensor_scalar(w[:, 0, 0:8 * FW[i]], slot[:, 0:8 * FW[i]].bitcast(I32), -7.5, None, ALU.add))
                    of = slot[0:LRR, 1024:1024 + 2 * FW[i]]
                    to = w[0:LRR, 1, 0:2 * FW[i]]
                    link(pool.tensor_copy(to, of))
                    mid = slice(RANK, 2 * RANK)
                    signal(pool.tensor_tensor(to[mid], of[mid], to[mid].bitcast(F32), ALU.subtract), split_done)
                elif kind == "dn1":
                    n, rows = (1024, P) if i < 5 else (512, FW[-1])
                    signal(pool.tensor_scalar(w[0:rows, 0, 0:n], slot[0:rows, 0:n].bitcast(I32), -7.5, None, ALU.add), split_done)
                elif kind == "lrb":
                    of = slot[0:LRR, 0:512]
                    if CHUNKS[:c].count(("lrb", 0)):
                        pool.wait_ge(dn_ready, NT + 4)
                    link(pool.tensor_copy(lrdb[:], of))
                    mid = slice(RANK, 2 * RANK)
                    signal(pool.tensor_tensor(lrdb[mid, :], of[mid], lrdb[mid, :].bitcast(F32), ALU.subtract), split_done)

            def rsqrt_pair(n, g):
                pool.wait_ge(var_ready, 4 * n + g + 1)
                signal(pool.tensor_tensor(rstd[:, 2 * g:2 * g + 2], ve[:, 2 * g:2 * g + 2], nhalf[:, 0:2], ALU.pow), rstd_ready)

            link(pool.memset(nhalf[:], -0.5))
            link(pool.memset(ident[:], 0.0))
            signal(pool.affine_select(out=ident[:], in_=ident[:], compare_op=ALU.not_equal, fill=1.0, base=0,
                               pattern=[[-1, P]], channel_multiplier=1), ident_ready)
            pool.wait_ge(ident_ready, 1)
            for g in range(4):
                rsqrt_pair(0, g)
            for j in range(2):
                link(pool.memset(ks[64 * j + 32:64 * j + 64, :, :].bitcast(F32), 1.0))
            link(pool.memset(v_sb[:], 1.0))
            link(pool.memset(maskA[:], 0.0))
            link(pool.memset(maskB[:], 0.0))
            link(pool.affine_select(out=maskA[:], in_=maskA[:], compare_op=ALU.is_ge, fill=MASKED, base=0,
                                    pattern=[[0, 4], [-1, P]], channel_multiplier=1))
            link(pool.affine_select(out=maskB[:], in_=maskB[:], compare_op=ALU.is_ge, fill=MASKED, base=P,
                                    pattern=[[0, 2], [-1, SEQ]], channel_multiplier=1))
            signal(pool.tensor_copy(identb[:], ident[:]), consts_ready)
            for c in range(5):
                chunk_split(c)
            for i in range(32):
                for c in (0, 2):
                    n = 3 * i + c
                    pool.wait_ge(exp_ready, n + 1)
                    pt = probs[:, n % 6, :].rearrange("p (g q) -> p g q", g=GRP)
                    signal(pool.affine_select(out=pt, in_=pt, compare_op=ALU.is_ge, fill=0.0, base=0,
                                       pattern=[[0, GRP], [1, P]], channel_multiplier=-1), masked)

            def rot_start():
                pool.wait_ge(phasor_scaled, 1)
                link(pool.memset(cs[0:64, 5, :], 1.0))
                link(pool.memset(cs[64:128, 5, :], -1.0))
                link(pool.tensor_tensor(cs[:, 8, :], cs[:, 3, :], nhalf[:, 0:DEPTH], ALU.pow))
                link(pool.tensor_tensor(cs[:, 6, :], cs[:, 0, :], cs[:, 8, :], ALU.mult))
                link(pool.tensor_tensor(cs[:, 7, :], cs[:, 1, :], cs[:, 8, :], ALU.mult))
                link(pool.tensor_tensor(cs[:, 9, :], cs[:, 3, :], cs[:, 8, :], ALU.mult))
                signal(pool.tensor_tensor(cs[:, 4, :], cs[:, 9, :], cs[:, 2, :], ALU.mult), polar_ready)
                link(pool.tensor_tensor(cs[:, 10, :], cs[:, 6, :], cs[:, 5, :], ALU.mult))
                link(pool.tensor_tensor(cs[:, 10, :], cs[:, 10, :], col("lc_a", 0, 4), ALU.mult))
                link(pool.tensor_tensor(cs[:, 11, :], cs[:, 7, :], col("lc_b", 0, 4), ALU.mult))
                link(pool.tensor_tensor(cs[:, 10, :], cs[:, 10, :], cs[:, 11, :], ALU.subtract))
                pool.wait_ge(decay_ready, 1)
                link(pool.tensor_tensor(first[:], cs[:, 10, :], decay[:], ALU.mult))
                link(pool.memset(rot[0:64, :, 0:1], 1.0))
                link(pool.memset(rot[64:128, :, 0:1], 0.0))
                link(pool.memset(rotb[0:64, :, 0:1], 0.0))
                link(pool.memset(rotb[64:128, :, 0:1], 1.0))

            def rot_step(k):
                n = 1 << k
                c = cs[:, 6, :].unsqueeze(2).to_broadcast([P, DEPTH, n])
                s = cs[:, 7, :].unsqueeze(2).to_broadcast([P, DEPTH, n])
                a, b = rot[:, :, 0:n], rotb[:, :, 0:n]
                link(pool.tensor_tensor(rtmp[:, 0, :, 0:n], a, c, ALU.mult))
                link(pool.tensor_tensor(rtmp[:, 1, :, 0:n], b, s, ALU.mult))
                if k == 7:
                    signal(pool.tensor_tensor(rot[:, :, n:2 * n], rtmp[:, 0, :, 0:n], rtmp[:, 1, :, 0:n], ALU.add), rot_ready)
                    return
                link(pool.tensor_tensor(rot[:, :, n:2 * n], rtmp[:, 0, :, 0:n], rtmp[:, 1, :, 0:n], ALU.add))
                link(pool.tensor_tensor(rtmp[:, 0, :, 0:n], b, c, ALU.mult))
                link(pool.tensor_tensor(rtmp[:, 1, :, 0:n], a, s, ALU.mult))
                link(pool.tensor_tensor(rotb[:, :, n:2 * n], rtmp[:, 0, :, 0:n], rtmp[:, 1, :, 0:n], ALU.subtract))
                link(pool.tensor_tensor(cs[:, 8, :], cs[:, 6, :], cs[:, 6, :], ALU.mult))
                link(pool.tensor_tensor(cs[:, 9, :], cs[:, 7, :], cs[:, 7, :], ALU.mult))
                link(pool.tensor_tensor(cs[:, 10, :], cs[:, 6, :], cs[:, 7, :], ALU.mult))
                link(pool.tensor_tensor(cs[:, 6, :], cs[:, 8, :], cs[:, 9, :], ALU.subtract))
                link(pool.tensor_tensor(cs[:, 7, :], cs[:, 10, :], cs[:, 10, :], ALU.add))

            for c in range(5, 22):
                chunk_split(c)
                if c == 7:
                    rot_start()
                if 8 <= c < 16:
                    rot_step(c - 8)
            for g in range(4):
                rsqrt_pair(1, g)
            chunk_split(22)
            pool.wait_ge(dn_ready, NT)
            pool.wait_ge(x1_ready, NT)
            link(pool.memset(sel[:], 0.0))
            link(pool.memset(comb[:], 0.0))
            link(pool.memset(bd[:], 0.0))
            link(pool.memset(bdc[:], 0.0))
            for j in range(2):
                r = slice(CH * j, CH * j + CH)
                for i in range(2):
                    link(pool.tensor_copy(sel[r, j, CH * i:CH * i + CH], ident[r, r]))
                link(pool.tensor_tensor(comb[:, j, r], ident[:, 0:CH], ident[:, CH:P], ALU.add))
                link(pool.memset(bd[r, r], 1.0 / CH))
                ins = pool.memset(bdc[r, j:j + 1], 1.0 / CH)
                if j == 0:
                    link(ins)
                else:
                    signal(ins, late_consts)
            c = 23
            for kind, a, i in ORDER1:
                if kind == "ssm":
                    l, step = SSM_STEPS[a]
                    if step in ("var1", "var2"):
                        nth = 2 * l + (step == "var2")
                        pool.wait_ge(ln_stat, nth + 1)
                        signal(pool.tensor_tensor(trs[:], tstat[:], nhalf[:], ALU.pow), ln_pow)
                    continue
                ahead = {"lowrank": 2, "gate": 1, "rd": 3, "dn": 1}.get(kind, 0)
                for _ in range(ahead):
                    if c < len(CHUNKS):
                        chunk_split(c)
                        c += 1
            assert c == len(CHUNKS)

        @block.scalar
        def _(act):
            chain = [0]

            def link(ins):
                chain[0] += 1
                ins.then_inc(act_chain, 1)
                act.wait_ge(act_chain, chain[0])

            def ln_hi(n, t):
                act.wait_ge(xt_ready, NT * n + t + 1)
                act.activation(xnT[:, 0, :, t * P:(t + 1) * P], PS[:, t % 2, :].rearrange("p (k q) -> p k q", k=KD),
                               ACT.Copy).then_inc(xh_ready, 1)

            for t in range(NT):
                ln_hi(0, t)
            for half in range(2):
                for u in range(5):
                    n = 5 * half + u
                    act.wait_ge(qkv_ready, 6 * half + u + 1)
                    if n:
                        act.wait_ge(proj_split, n)
                    if half == 0 and u == 0:
                        act.wait_ge(dve_chain, 1)
                    bank = (6 * half + u) % 2
                    if u < 4:
                        act.activation(proj[:], PS[:, bank, :], ACT.Identity, bias=bq4[:, u:u + 1], scale=0.25).then_inc(proj_ready, 1)
                    else:
                        act.activation(proj[:], PS[:, bank, :], ACT.Identity, bias=col("bk"), scale=1.0).then_inc(proj_ready, 1)
                for bb in range(2):
                    b = 2 * half + bb
                    act.wait_ge(mt_ready, b + 1)
                    if b:
                        act.wait_ge(m_out, 32 * b)
                    act.activation(max_hl[:, 0, :], PS[0:32, 0, 0:SEQ], ACT.Copy).then_inc(mh_ready, 1)
                for bb in range(2):
                    b = 2 * half + bb
                    for kv in range(NKV):
                        i = NKV * b + kv
                        for c in range(3):
                            n = 3 * i + c
                            act.wait_ge(s2_ready, n + 1)
                            if i >= 2:
                                act.wait_ge(pv_ready, i - 1)
                            act.activation(probs[:, n % 6, :], PS[:, 2 + n % 3, :], ACT.Exp).then_inc(exp_ready, 1)
                        if kv == NKV - 1:
                            for qt in range(2):
                                t = 2 * b + qt
                                act.wait_ge(at_ready, t + 1)
                                if t:
                                    act.wait_ge(wo_ready, t)
                                act.activation(attT[:, 0, :, :], PS[:, 7, :].rearrange("p (k q) -> p k q", k=KD), ACT.Copy).then_inc(ah_ready, 1)
            act.wait_ge(polar_ready, 1)
            act.activation(decay[:], cs[:, 4, :], ACT.Tanh).then_inc(decay_ready, 1)
            for job in range(2 * NF):
                i = job // 2
                act.wait_ge(gu_ready, job + 1)
                if job >= 2:
                    act.wait_ge(up_used, job - 1)
                act.activation(sg0[0:FW[i], job % 2, :], PS[0:FW[i], 2 + 2 * (job % 3), :], ACT.Silu).then_inc(gate_used, 1)
            for t in range(NT):
                act.wait_ge(dn_ready, t + 1)
                if t < 2:
                    act.wait_ge(up_used, 2 * NF)
                else:
                    act.wait_ge(x1_ready, t - 1)
                act.activation(sg0[:, t % 2, :], PS[:, t, :], ACT.Silu).then_inc(g_ready, 1)
            for t in range(NT):
                ln_hi(1, t)
            act.wait_ge(win_ready, 1)
            act.activation(h[:], PS[:, 2, :], ACT.Identity, bias=col("bin"), scale=1.0).then_inc(h0_ready, 1)

            def copies(J):
                fw = FW[J % NF]
                act.wait_ge(gu_ready, 2 * NF + J + 1)
                if J:
                    act.wait_ge(up_used, 2 * NF + J)
                for o in range(2):
                    ins = act.activation(e_lr[0:fw, o, :], PS[0:fw, 6 + o, :], ACT.Copy)
                ins.then_inc(lr_copied, 1)

            def silu(J):
                fw = FW[J % NF]
                act.wait_ge(gsum_ready, J + 1)
                if J:
                    act.wait_ge(hid_ready, 2 * NF + J)
                act.activation(e_h[0:fw, :], e_gu[0:fw, 0, :], ACT.Silu).then_inc(silu_ready, 1)

            def model(n):
                l, step = SSM_STEPS[n]
                nth = 2 * l + (step[-1] == "2")
                if step in ("mean1", "mean2"):
                    act.wait_ge(ln_cen, nth + 1)
                    act.activation(tmp1[:], cen[:], ACT.Square).then_inc(ln_sq, 1)
                elif step in ("rstd1", "rstd2"):
                    act.wait_ge(ln_norm, nth + 1)
                    if l == DEPTH:
                        f, w, b = ACT.Identity, col("lnl_w"), col("lnl_b")
                    elif step == "rstd1":
                        f, w, b = ACT.Silu, col("ln1_w", l), col("ln1_b", l)
                    else:
                        f, w, b = ACT.Identity, col("ln2_w", l), col("ln2_b", l)
                    act.activation(act1[:], cen[:], f, bias=b, scale=w).then_inc(ln_out, 1)
                elif step in ("w1a", "w1b"):
                    ft = int(step == "w1b")
                    act.wait_ge(w1_ready, 2 * l + ft + 1)
                    for half in range(2):
                        ins = act.activation(sv[:, ft, half, :], PS[:, half, :], ACT.Silu, bias=col("b1", 2 * l + ft))
                    ins.then_inc(w1_act, 1)

            for kind, a, i in ORDER1:
                J = NF * a + i
                if kind == "lowrank":
                    for o in range(4):
                        act.wait_ge(lr_ready, o + 1)
                        if o >= 2:
                            act.wait_ge(lr_split, o - 1)
                        act.activation(e_lr[0:LRR, o % 2, :], PS[0:LRR, 3 + o, :], ACT.Copy, scale=0.02).then_inc(lr_copied, 1)
                    act.wait_ge(lr_split, 4)
                elif kind == "gate" and i:
                    copies(J - 1)
                elif kind == "up" and i:
                    silu(J - 1)
                elif kind == "flush":
                    copies(NF * a + NF - 1)
                    silu(NF * a + NF - 1)
                elif kind == "ssm":
                    model(a)
                elif kind == "rd":
                    act.wait_ge(rd_ready, a + 1)
                    act.wait_ge(up_used, 2 * NF + NF * (a + 1))
                    act.activation(e_lr[0:LRR, 0, :], PS[0:LRR, 6, :], ACT.Copy, scale=0.02).then_inc(rd_copied, 1)
                elif kind == "fin":
                    for t in range(4):
                        act.wait_ge(fsum_ready, 4 * a + t + 1)
                        if a == 0:
                            act.activation(s_sb[:, t, :], e_gu[:, t % 2, :], ACT.Silu).then_inc(fg_ready, 1)
                        else:
                            if t >= 2:
                                act.wait_ge(out_ready, 4 + t - 1)
                            act.activation(e_lr[:, t % 2, :], e_gu[:, t % 2, :], ACT.Silu).then_inc(fg_ready, 1)

        @block.vector
        def _(dve):
            chain = [0]

            def link(ins):
                chain[0] += 1
                ins.then_inc(dve_chain, 1)
                dve.wait_ge(dve_chain, chain[0])

            dve.wait_ge(cols_loaded, 16)
            link(dve.tensor_scalar(bq4[:], col("bq", 0, 4), 0.25, None, ALU.mult))

            def layernorm(n):
                for g in range(5):
                    if g < 4:
                        for t in (2 * g, 2 * g + 1):
                            if n == 0:
                                dve.wait_ge(x_loaded[t], 16)
                            link(dve.bn_stats(bn6[:, t, :], x[:, t, :]))
                            link(dve.bn_aggr(mv[:, t, :], bn6[:, t, :]))
                        dve.tensor_scalar(ve[:, 2 * g:2 * g + 2], mv[:, 2 * g:2 * g + 2, 1], EPS, None, ALU.add)\
                           .then_inc(var_ready, 1)
                    if g:
                        dve.wait_ge(rstd_ready, 4 * n + g)
                        for t in (2 * g - 2, 2 * g - 1):
                            if NT * n + t >= 2:
                                dve.wait_ge(xt_ready, NT * n + t - 1)
                            dve.tensor_scalar(xn[:, t % 2, :], x[:, t, :], mv[:, t, 0:1], rstd[:, t:t + 1],
                                              ALU.subtract, ALU.mult).then_inc(xn_ready, 1)
                        for t in (2 * g - 2, 2 * g - 1):
                            dve.wait_ge(xh_ready, NT * n + t + 1)
                            o = slice(t * P, (t + 1) * P)
                            dve.tensor_tensor(xnT[:, 1, :, o], PS[:, t % 2, :].rearrange("p (k q) -> p k q", k=KD),
                                              xnT[:, 0, :, o].bitcast(F32), ALU.subtract).then_inc(xl_ready, 1)

            layernorm(0)
            for half in range(2):
                for u in range(6):
                    n = 5 * half + u
                    if u < 5:
                        dve.wait_ge(proj_ready, n + 1)
                        if n >= 2:
                            dve.wait_ge(q_out[n % 2], 32 * (n // 2))
                        link(dve.tensor_copy(proj_hl[:, n % 2, 0, :], proj[:]))
                        dve.tensor_tensor(proj_hl[:, n % 2, 1, :], proj[:], proj_hl[:, n % 2, 0, :].bitcast(F32),
                                          ALU.subtract).then_inc(proj_split, 1)
                    else:
                        dve.wait_ge(qkv_ready, 6 * half + 6)
                        dve.wait_ge(consts_ready, 1)
                        dve.wait_ge(bv_loaded, 16)
                        for q in range(4):
                            ins = dve.tensor_tensor(v_sb[:, 4 * half + q, :, 0:DH],
                                                    PS[:, 1, q * P:(q + 1) * P].rearrange("p (h e) -> p h e", h=NKV),
                                                    bv_b[:].rearrange("p (h e) -> p h e", h=NKV), ALU.add)
                        ins.then_inc(v_ready, 1)
                for bb in range(2):
                    b = 2 * half + bb
                    for kv in range(NKV):
                        i = NKV * b + kv
                        dve.wait_ge(s1_ready, i + 1)
                        o = 2 + 3 * (i % 2)
                        dve.tensor_reduce(negmax[:, b, 0, GRP * kv:GRP * kv + GRP],
                                          PS[:, o, :].rearrange("p (g k) -> p g k", g=GRP), AX_X, ALU.max, negate=True)
                        dve.tensor_reduce(negmax[:, b, 1, GRP * kv:GRP * kv + GRP],
                                          PS[:, o + 1:o + 3, :].rearrange("p o (g k) -> p (o g) k", g=2), AX_X, ALU.max,
                                          negate=True).then_inc(max_ready, 1)
                    dve.wait_ge(mh_ready, b + 1)
                    dve.tensor_tensor(max_hl[:, 1, :], PS[0:32, 0, 0:SEQ], max_hl[:, 0, :].bitcast(F32), ALU.subtract)\
                       .then_inc(ml_ready, 1)
                for bb in range(2):
                    b = 2 * half + bb
                    for kv in range(NKV):
                        i = NKV * b + kv
                        dve.wait_ge(pv_ready, i + 1)
                        if kv == 0 and b:
                            dve.wait_ge(at_ready, 2 * b)
                        if i:
                            dve.wait_ge(att_ready, i)
                        o = PS[:, 5 + i % 2, 0:8 * (DH + 1)].rearrange("p (g e) -> p g e", g=8)
                        link(dve.reciprocal(rden[:], o[:, :, DH]))
                        for qt in range(2):
                            ins = dve.tensor_tensor(
                                att_tok[:, qt, 64 * kv:64 * kv + 64].rearrange("p (g e) -> p g e", g=GRP),
                                o[:, 4 * qt:4 * qt + 4, 0:DH],
                                rden[:, 4 * qt:4 * qt + 4].unsqueeze(2).to_broadcast([P, GRP, DH]), ALU.mult)
                        ins.then_inc(att_ready, 1)
                    for qt in range(2):
                        t = 2 * b + qt
                        dve.wait_ge(ah_ready, t + 1)
                        dve.tensor_tensor(attT[:, 1, :, :], PS[:, 7, :].rearrange("p (k q) -> p k q", k=KD),
                                          attT[:, 0, :, :].bitcast(F32), ALU.subtract).then_inc(al_ready, 1)
                        dve.wait_ge(wo_ready, t + 1)
                        if t == 0:
                            dve.wait_ge(bo_loaded, 16)
                        dve.tensor_tensor(s_sb[:, t, :], PS[:, 1, :], row_b[:], ALU.add).then_inc(s_ready, 1)
            re, im = col("ph_re", 0, 4), col("ph_im", 0, 4)
            dve.wait_ge(s_ready, NT)
            link(dve.tensor_scalar(cs[:, 8, :], re, -1.0, None, ALU.mult))
            link(dve.tensor_scalar(cs[:, 9, :], im, -1.0, None, ALU.mult))
            link(dve.tensor_tensor(cs[:, 8, :], cs[:, 8, :], re, ALU.max))
            link(dve.tensor_tensor(cs[:, 9, :], cs[:, 9, :], im, ALU.max))
            link(dve.tensor_tensor(cs[:, 2, :], cs[:, 8, :], cs[:, 9, :], ALU.max))
            link(dve.tensor_scalar(cs[:, 10, :], cs[:, 2, :], 0.0, None, ALU.is_equal))
            link(dve.tensor_scalar(cs[:, 8, :], cs[:, 2, :], 1.2e-38, None, ALU.max))
            link(dve.reciprocal(cs[:, 9, :], cs[:, 8, :]))
            link(dve.tensor_tensor(cs[:, 0, :], re, cs[:, 9, :], ALU.mult))
            link(dve.tensor_tensor(cs[:, 0, :], cs[:, 0, :], cs[:, 10, :], ALU.add))
            link(dve.tensor_tensor(cs[:, 1, :], im, cs[:, 9, :], ALU.mult))
            link(dve.tensor_tensor(cs[:, 8, :], cs[:, 0, :], cs[:, 0, :], ALU.mult))
            link(dve.tensor_tensor(cs[:, 9, :], cs[:, 1, :], cs[:, 1, :], ALU.mult))
            dve.tensor_tensor(cs[:, 3, :], cs[:, 8, :], cs[:, 9, :], ALU.add).then_inc(phasor_scaled, 1)
            for job in range(2 * NF):
                i, half = job // 2, job % 2
                fw = FW[i]
                hs = slice(half * HALF, (half + 1) * HALF)
                dve.wait_ge(gate_used, job + 1)
                hid = ht0[0:fw, job % 2, :]
                dve.tensor_tensor(hid, sg0[0:fw, job % 2, :], PS[0:fw, 3 + 2 * (job % 3), :], ALU.mult).then_inc(up_used, 1)
                dve.wait_ge(up_used, job + 1)
                link(dve.tensor_copy(hid0[0:fw, 0, i, hs], hid))
                dve.tensor_tensor(hid0[0:fw, 1, i, hs], hid, hid0[0:fw, 0, i, hs].bitcast(F32), ALU.subtract)\
                   .then_inc(hid_ready, 1)
            for t in range(NT):
                dve.wait_ge(g_ready, t + 1)
                link(dve.tensor_tensor(ht0[:, t % 2, :], sg0[:, t % 2, :], s_sb[:, t, :], ALU.mult))
                dve.tensor_tensor(x[:, t, :], x[:, t, :], ht0[:, t % 2, :], ALU.add).then_inc(x1_ready, 1)
            dve.wait_ge(x1_ready, NT)
            dve.wait_ge(rot_ready, 1)
            layernorm(1)
            dve.wait_ge(late_loaded, 48)
            for o, name in ((0, "gate_s"), (1, "up_s")):
                link(dve.tensor_scalar(gs[:, o, :], col(name, 0, NF), 0.005, None, ALU.mult))
            link(dve.tensor_scalar(dscale_b[:], dscale_b[:], 0.005, None, ALU.mult))

            def sums(J):
                i = J % NF
                fw = FW[i]
                dve.wait_ge(lr_copied, 4 + J + 1)
                for o in range(2):
                    dve.scalar_tensor_tensor(e_gu[0:fw, o, :], PS[0:fw, 2 + 2 * (J % 2) + o, :], gs[0:fw, o, i:i + 1],
                                             e_lr[0:fw, o, :], ALU.mult, ALU.add).then_inc((gsum_ready, up_used)[o], 1)

            def hidden(J):
                half, i = J // NF, J % NF
                fw = FW[i]
                if half == 1 and i == 0:
                    dve.wait_ge(dn_ready, NT + 4)
                dve.wait_ge(silu_ready, J + 1)
                dve.wait_ge(up_used, 2 * NF + J + 1)
                hid = e_gu[0:fw, 1, :]
                link(dve.tensor_tensor(hid, hid, e_h[0:fw, :], ALU.mult))
                link(dve.tensor_copy(hid1[0:fw, 0, i, :], hid))
                dve.tensor_tensor(hid1[0:fw, 1, i, :], hid, hid1[0:fw, 0, i, :].bitcast(F32), ALU.subtract).then_inc(hid_ready, 1)
                dve.wait_ge(hid_ready, 2 * NF + J + 1)

            def model(n):
                l, step = SSM_STEPS[n]
                nth = 2 * l + (step[-1] == "2")
                if step in ("mean1", "mean2"):
                    dve.wait_ge(ln_mean, nth + 1)
                    dve.tensor_tensor(cen[:], h[:], PS[:, 0, :], ALU.subtract).then_inc(ln_cen, 1)
                elif step in ("var1", "var2"):
                    dve.wait_ge(ln_var, nth + 1)
                    dve.tensor_scalar(tstat[:], PS[:, 1, 0:8], EPS, None, ALU.add).then_inc(ln_stat, 1)
                    dve.wait_ge(ln_pow, nth + 1)
                    dve.tensor_copy(tmp1[:].rearrange("p (c e) -> p c e", c=8),
                                    trs[:].unsqueeze(2).to_broadcast([P, 8, CH])).then_inc(ln_spread, 1)
                elif step in ("rstd1", "rstd2"):
                    dve.wait_ge(ln_rstd, nth + 1)
                    dve.tensor_tensor(cen[:], cen[:], PS[:, 0, :], ALU.mult).then_inc(ln_norm, 1)
                elif step == "sel":
                    link(dve.tensor_copy(dmat[:], decay[:, l:l + 1].to_broadcast([P, HALF])))
                    link(dve.memset(dmat[:, 0:HALF:SEQ], 0.0))
                    dve.wait_ge(cv_sel, l + 1)
                    r = rot[:, l, :].unsqueeze(1).to_broadcast([P, 2, SEQ])
                    for j in range(2):
                        link(dve.tensor_tensor(dz[:, j, :].rearrange("p (s t) -> p s t", s=2),
                                               PS[:, j, :].rearrange("p (s t) -> p s t", s=2), r, ALU.mult))
                    for j in range(2):
                        link(dve.tensor_scalar(dz[:, j, 0:HALF:SEQ], dz[:, j, 0:HALF:SEQ], first[:, l:l + 1], None, ALU.add))
                    for j in range(2):
                        link(dve.tensor_tensor_scan(sv[:, 0, j, :], dmat[:], dz[:, j, :], 0.0, ALU.mult, ALU.add))
                    for j in range(2):
                        ins = dve.tensor_tensor(dz[:, j, :].rearrange("p (s t) -> p s t", s=2),
                                                sv[:, 0, j, :].rearrange("p (s t) -> p s t", s=2), r, ALU.mult)
                    ins.then_inc(cv_mod, 1)
                elif step == "comb":
                    dve.wait_ge(cv_comb, l + 1)
                    dve.scalar_tensor_tensor(h[:], PS[:, 0, :], col("scl", l), h[:], ALU.mult, ALU.add).then_inc(h_ready, 1)
                    dve.wait_ge(h_ready, 2 * l + 1)
                elif step == "w2":
                    dve.wait_ge(w2_ready, l + 1)
                    dve.scalar_tensor_tensor(h[:], PS[:, 0, :], col("b2", l), h[:], ALU.add, ALU.add).then_inc(h_ready, 1)
                    dve.wait_ge(h_ready, 2 * l + 2)

            def down_sum(n):
                t = n % 4
                dve.wait_ge(lrd_ready, n + 1)
                if n % 4 >= 2:
                    dve.wait_ge(fg_ready, n - 1)
                link(dve.tensor_tensor(e_gu[:, t % 2, :], PS[:, 2 + t, :], dscale_b[:], ALU.mult))
                dve.tensor_tensor(e_gu[:, t % 2, :], e_gu[:, t % 2, :], PS[:, 6 + t % 2, :], ALU.add).then_inc(fsum_ready, 1)

            def gated(n):
                dve.wait_ge(fg_ready, n + 1)
                link(dve.tensor_tensor(s_sb[:, n, :], s_sb[:, n, :], e_lr[:, n % 2, :], ALU.mult))
                dve.tensor_tensor(x[:, n, :], x[:, n, :], s_sb[:, n, :], ALU.add).then_inc(out_ready, 1)

            for kind, a, i in ORDER1:
                J = NF * a + i
                if kind == "lowrank":
                    for o in range(4):
                        dve.wait_ge(lr_copied, o + 1)
                        to = lrx[:, o // 2, (o % 2) * HALF:(o % 2 + 1) * HALF]
                        of = e_lr[0:LRR, o % 2, :]
                        low = slice(2 * RANK, LRR)
                        link(dve.tensor_copy(to, of))
                        dve.tensor_tensor(to[low], of[low], to[low].bitcast(F32), ALU.subtract).then_inc(lr_split, 1)
                elif kind == "gate" and i:
                    sums(J - 1)
                elif kind == "up" and i:
                    hidden(J - 1)
                elif kind == "flush":
                    sums(NF * a + NF - 1)
                    hidden(NF * a + NF - 1)
                elif kind == "ssm":
                    model(a)
                elif kind == "rd":
                    dve.wait_ge(rd_copied, a + 1)
                    if a:
                        dve.wait_ge(lrd_ready, 4)
                    low = slice(2 * RANK, LRR)
                    link(dve.tensor_copy(lrh[:], e_lr[0:LRR, 0, :]))
                    dve.tensor_tensor(lrh[low, :], e_lr[low, 0, :], lrh[low, :].bitcast(F32), ALU.subtract).then_inc(rd_split, 1)
                elif kind == "wout":
                    for t in range(NT):
                        dve.wait_ge(wout_ready, t + 1)
                        if t < 4:
                            link(dve.tensor_tensor(dz[:, 0, :], PS[:, t % 2, :], row_b[:], ALU.add))
                            s_taken = dve.tensor_tensor(dz[:, 1, :], dz[:, 0, :], s_sb[:, t, :], ALU.mult)
                            s_taken.then_inc(s_ready, 1)
                            dve.wait_ge(s_ready, NT + t + 1)
                            dve.tensor_tensor(x[:, t, :], x[:, t, :], dz[:, 1, :], ALU.add).then_inc(out_ready, 1)
                            dve.wait_ge(out_ready, t + 1)
                        else:
                            dve.tensor_tensor(s_sb[:, t, :], PS[:, t % 2, :], row_b[:], ALU.add).then_inc(s_ready, 1)
                            dve.wait_ge(s_ready, NT + t + 1)
                elif kind == "fin":
                    for t in range(5):
                        if t < 4:
                            down_sum(4 * a + t)
                        if t and a:
                            gated(4 * a + t - 1)

        @block.tensor
        def _(pe):
            def products(out, pairs):
                pairs = list(pairs)
                for n, (w, m) in enumerate(pairs):
                    ins = pe.matmul(out, w, m, start=n == 0, stop=n == len(pairs) - 1)
                return ins

            PARTS = ((0, 0), (0, 1), (1, 0))

            def transposes(n):
                for t in range(NT):
                    pe.wait_ge(xn_ready, NT * n + t + 1)
                    if t >= 2:
                        pe.wait_ge(xl_ready, NT * n + t - 1)
                    if n == 1 and t < 2:
                        pe.wait_ge(x1_ready, t + 1)
                    for k in range(KD):
                        ins = pe.transpose(PS[:, t % 2, k * P:(k + 1) * P], xn[:, t % 2, k * P:(k + 1) * P], ident[:])
                    ins.then_inc(xt_ready, 1)

            pe.wait_ge(ident_ready, 1)
            transposes(0)

            def qkv(half):
                tok = slice(half * HALF, (half + 1) * HALF)
                for u in range(6):
                    n = 6 * half + u
                    if half == 0 and u == 0:
                        pe.wait_ge(xl_ready, NT)
                    if u < 5 and n % 6 >= 2:
                        pe.wait_ge(proj_ready, 5 * half + u - 1)
                    if u == 5:
                        pe.wait_ge(proj_ready, 5 * half + 4)
                    if half == 1 and u < 2:
                        pe.wait_ge((ml_ready, s_ready)[u], (2, 4)[u])
                    if half == 0 and u in (0, 2, 4):
                        pe.wait_ge(split_done, u // 2 + 1)
                    if u < 5:
                        products(PS[:, u % 2, :], ((wqkv[:, a, k, u * P:(u + 1) * P], xnT[:, b, k, tok])
                                                   for k in range(KD) for a, b in PARTS)).then_inc(qkv_ready, 1)
                    else:
                        for q in range(4):
                            t = slice((4 * half + q) * P, (4 * half + q + 1) * P)
                            ins = products(PS[:, 1, q * P:(q + 1) * P], ((xnT[:, b, k, t], wqkv[:, a, k, 640:768])
                                                                        for k in range(KD) for a, b in PARTS))
                        ins.then_inc(qkv_ready, 1)

            K1 = 3 * DH
            K2 = K1 + 2

            def score_max(b, kv):
                i, m, r0, t0 = NKV * b + kv, kv // 2, 64 * (kv % 2), (b % 2) * SEQ
                o = 2 + 3 * (i % 2)
                if b % 2 == 0 and kv % 2 == 0:
                    pe.wait_ge(qs_loaded[m], 96 * (b // 2 + 1))
                if b % 2 == 0 and kv == 0:
                    pe.wait_ge(ks_loaded, 96 * (b // 2 + 1))
                if i >= 2:
                    pe.wait_ge(max_ready, i - 1)
                if i == 16:
                    pe.wait_ge(exp_ready, 48)
                    pe.wait_ge(att_ready, 16)
                    pe.wait_ge(al_ready, 4)
                key = ks[r0:r0 + K1, m, t0:t0 + SEQ]
                pe.matmul(PS[:, o, :], identb[:], maskA[:].rearrange("p g k -> p (g k)"), start=True, stop=False)
                for g in range(GRP):
                    pe.matmul(PS[:, o, g * P:(g + 1) * P], qs[r0:r0 + K1, m, g, t0:t0 + P], key[:, 0:P],
                              start=False, stop=g == GRP - 1)
                for d in range(2):
                    pe.matmul(PS[:, o + 1 + d, :], identb[:], maskB[:].rearrange("p g k -> p (g k)"), start=True, stop=False)
                    for g in range(2):
                        ins = pe.matmul(PS[:, o + 1 + d, g * SEQ:(g + 1) * SEQ], qs[r0:r0 + K1, m, 2 * d + g, t0 + P:t0 + SEQ],
                                        key, start=False, stop=g == 1)
                ins.then_inc(s1_ready, 1)

            def max_transposed(b):
                pe.wait_ge(max_ready, NKV * (b + 1))
                if b % 2 == 0:
                    pe.wait_ge(proj_ready, 5 * (b // 2 + 1))
                else:
                    pe.wait_ge(ml_ready, b)
                for qt in range(2):
                    ins = pe.transpose(PS[0:32, 0, qt * P:(qt + 1) * P], negmax[:, b, qt, :], ident[:])
                ins.then_inc(mt_ready, 1)

            def scores(i):
                b, kv = i // NKV, i % NKV
                m, r0, t0 = kv // 2, 64 * (kv % 2), (b % 2) * SEQ
                if kv == 0:
                    pe.wait_ge(m_loaded[b % 2], 64 * (b // 2 + 1))
                if b % 2 == 0 and kv == 0:
                    pe.wait_ge(max_ready, 16 * (b // 2 + 1))
                for c, (kt, qt) in enumerate(((0, 0), (0, 1), (1, 1))):
                    n = 3 * i + c
                    if n >= 3:
                        pe.wait_ge(exp_ready, n - 2)
                    pe.matmul(PS[:, 2 + n % 3, :], ks[r0:r0 + K2, m, t0 + kt * P:t0 + (kt + 1) * P],
                              qs[r0:r0 + K2, m, :, t0 + qt * P:t0 + (qt + 1) * P], start=True, stop=True).then_inc(s2_ready, 1)

            def values(i):
                b, kv = i // NKV, i % NKV
                o = PS[:, 5 + i % 2, 0:8 * (DH + 1)].rearrange("p (g e) -> p g e", g=8)
                if kv == 0 and b % 2 == 0:
                    pe.wait_ge(v_ready, b // 2 + 1)
                if i >= 2:
                    pe.wait_ge(att_ready, i - 1)
                pe.wait_ge(masked, 2 * i + 1)
                for g in range(GRP):
                    pe.matmul(o[:, g, :], probs[:, (3 * i) % 6, g * P:(g + 1) * P], v_sb[:, 2 * b, kv, :], start=True, stop=True)
                pe.wait_ge(exp_ready, 3 * i + 2)
                pe.wait_ge(masked, 2 * i + 2)
                for g in range(GRP):
                    for kt in range(2):
                        ins = pe.matmul(o[:, 4 + g, :], probs[:, (3 * i + 1 + kt) % 6, g * P:(g + 1) * P],
                                        v_sb[:, 2 * b + kt, kv, :], start=kt == 0, stop=kt == 1)
                ins.then_inc(pv_ready, 1)

            def project_out(b):
                pe.wait_ge(att_ready, NKV * (b + 1))
                for qt in range(2):
                    t = 2 * b + qt
                    if t:
                        pe.wait_ge(al_ready, t)
                    for k in range(KD):
                        ins = pe.transpose(PS[:, 7, k * P:(k + 1) * P], att_tok[:, qt, k * P:(k + 1) * P], ident[:])
                    ins.then_inc(at_ready, 1)
                    pe.wait_ge(al_ready, t + 1)
                    pe.wait_ge(split_done, 5)
                    if t % 4 == 0:
                        pe.wait_ge(v_ready, b // 2 + 1)
                    if t:
                        pe.wait_ge(s_ready, t)
                    ins = products(PS[:, 1, :], ((attT[:, a, k, :], ring[:, k // 2, w, (k % 2) * D:(k % 2 + 1) * D])
                                                 for k in range(KD) for a, w in PARTS))
                    ins.then_inc(wo_ready, 1)

            for half in range(2):
                qkv(half)
                for b in (2 * half, 2 * half + 1):
                    for kv in range(NKV):
                        score_max(b, kv)
                    max_transposed(b)
                for i in range(16 * half, 16 * half + 16):
                    if i % 16 == 0:
                        scores(i)
                    if i % 16 < 15:
                        scores(i + 1)
                    values(i)
                    if i % NKV == NKV - 1:
                        project_out(i // NKV)

            used = [2]

            def next_chunk(kind, index, half=0):
                c, rc = chunk_place(kind, index, half)
                assert rc == used[0], (kind, index, rc, used)
                used[0] += 1
                pe.wait_ge(split_done, c + 1)
                return ring[:, rc % N_RING, :, :]

            pe.wait_ge(exp_ready, 96)
            pe.wait_ge(att_ready, 32)
            pe.wait_ge(al_ready, NT)
            for i in range(NF):
                w = next_chunk("gu0", i)
                fw = FW[i]
                for half in range(2):
                    job = 2 * i + half
                    tok = slice(half * HALF, (half + 1) * HALF)
                    if job >= 3:
                        pe.wait_ge(up_used, job - 2)
                    for o in range(2):
                        g0 = 4 * fw * o
                        ins = products(PS[0:fw, 2 + 2 * (job % 3) + o, :],
                                       ((w[:, a, g0 + k * fw:g0 + (k + 1) * fw], xnT[:, b, k, tok])
                                        for k in range(KD) for a, b in PARTS))
                    ins.then_inc(gu_ready, 1)
            pe.wait_ge(up_used, 2 * NF)
            pe.wait_ge(s_ready, NT)
            for i in range(6):
                w = next_chunk("dn0", i)
                for kk in range(2 if i < 5 else 1):
                    k = 2 * i + kk
                    fw = FW[k]
                    pe.wait_ge(hid_ready, 2 * k + 2)
                    for t in range(NT):
                        for n, (a, b) in enumerate(PARTS):
                            ins = pe.matmul(PS[:, t, :], hid0[0:fw, a, k, t * P:(t + 1) * P], w[0:fw, b, kk * D:(kk + 1) * D],
                                            start=k == 0 and n == 0, stop=k == NF - 1 and n == 2)
                        if k == NF - 1:
                            ins.then_inc(dn_ready, 1)
                if i < 5:
                    ins.then_inc(chunk_used, 1)
            transposes(1)

            pe.wait_ge(xl_ready, 2 * NT)
            pe.wait_ge(g_ready, NT)
            pe.wait_ge(split_done, 23)
            products(PS[:, 2, :], ((win_hl[:, a, k, (CH, 0)[half]:(CH, 0)[half] + P], xnT[:, b, k, half * HALF:(half + 1) * HALF])
                                   for half in range(2) for k in range(KD) for a, b in PARTS)).then_inc(win_ready, 1)

            def model(n):
                l, step = SSM_STEPS[n]
                nth = 2 * l + (step[-1] == "2")
                if step in ("mean1", "mean2"):
                    if nth == 0:
                        pe.wait_ge(h0_ready, 1)
                        pe.wait_ge(late_consts, 1)
                    else:
                        pe.wait_ge(h_ready, nth)
                    pe.matmul(PS[:, 0, :], bd[:], h[:], start=True, stop=True).then_inc(ln_mean, 1)
                elif step in ("var1", "var2"):
                    pe.wait_ge(ln_sq, nth + 1)
                    for c in range(4):
                        ins = pe.matmul(PS[:, 1, 2 * c:2 * c + 2], tmp1[:, c * P:(c + 1) * P], bdc[:], start=True, stop=True)
                    ins.then_inc(ln_var, 1)
                elif step in ("rstd1", "rstd2"):
                    pe.wait_ge(ln_spread, nth + 1)
                    for c in range(4):
                        ins = pe.transpose(PS[:, 0, c * P:(c + 1) * P], tmp1[:, c * P:(c + 1) * P], ident[:])
                    ins.then_inc(ln_rstd, 1)
                elif step == "sel":
                    pe.wait_ge(ln_out, nth + 1)
                    for j in range(2):
                        ins = pe.matmul(PS[:, j, :], sel[:, j, :], act1[:], start=True, stop=True)
                    ins.then_inc(cv_sel, 1)
                elif step == "comb":
                    pe.wait_ge(cv_mod, l + 1)
                    products(PS[:, 0, :], ((comb[:, j, :], dz[:, j, :]) for j in range(2))).then_inc(cv_comb, 1)
                elif step in ("w1a", "w1b"):
                    ft = int(step == "w1b")
                    pe.wait_ge(late_loaded, 48)
                    pe.wait_ge(ln_out, 2 * l + 2)
                    if ft:
                        pe.wait_ge(w1_act, 2 * l + 1)
                    for half in range(2):
                        r = slice(CH * half, CH * half + CH)
                        ins = pe.matmul(PS[:, half, :], w1v[r, l, ft * P:(ft + 1) * P], act1[r, :], start=True, stop=True)
                    ins.then_inc(w1_ready, 1)
                elif step == "w2":
                    pe.wait_ge(w1_act, 2 * l + 2)
                    for half in range(2):
                        r = slice(CH * half, CH * half + CH)
                        ins = products(PS[r, 0, :], ((w2v[:, l, ft, :], sv[:, ft, half, :]) for ft in range(2)))
                    ins.then_inc(w2_ready, 1)

            cur = [None]
            for kind, a, i in ORDER1:
                J = NF * a + i
                tok = slice(a * HALF, (a + 1) * HALF)
                if kind == "lowrank":
                    w = next_chunk("lra", 0)
                    for o in range(4):
                        g0 = LRR * KD * (o // 2)
                        ins = products(PS[0:LRR, 3 + o, :], ((w[:, p, g0 + k * LRR:g0 + (k + 1) * LRR],
                                                        xnT[:, q, k, (o % 2) * HALF:(o % 2 + 1) * HALF])
                                                       for k in range(KD) for p, q in PARTS))
                        ins.then_inc(lr_ready, 1)
                    pe.wait_ge(lr_copied, 4)
                    pe.wait_ge(lr_split, 4)
                    pe.wait_ge(h0_ready, 1)
                elif kind in ("gate", "up"):
                    o = int(kind == "up")
                    fw = FW[i]
                    if o == 0:
                        cur[0] = next_chunk("gu1", i, a)
                        if J >= 2:
                            pe.wait_ge(up_used, 2 * NF + J - 1)
                        if a and i < 2:
                            pe.wait_ge(fsum_ready, 4)
                    w = cur[0]
                    g0 = 4 * fw * o
                    products(PS[0:fw, 2 + 2 * (J % 2) + o, :], ((w[:, 0, g0 + k * fw:g0 + (k + 1) * fw], xnT[:, q, k, tok])
                                                                for k in range(KD) for q in range(2)))
                    if o == 0 and J:
                        pe.wait_ge(lr_copied, 4 + J)
                    ins = pe.matmul(PS[0:fw, 6 + o, :], w[0:LRR, 1, o * fw:(o + 1) * fw], lrx[:, o, tok], start=True, stop=True)
                    if o:
                        ins.then_inc(gu_ready, 1)
                elif kind == "ssm":
                    model(a)
                elif kind == "rd":
                    w = next_chunk("lrd", 0, a)
                    pe.wait_ge(lr_copied, 4 + NF * (a + 1))
                    n = 0
                    for k in range(NF):
                        pe.wait_ge(hid_ready, 2 * NF + NF * a + k + 1)
                        for p, q in PARTS:
                            ins = pe.matmul(PS[0:LRR, 6, :], w[0:FW[k], p, k * LRR:(k + 1) * LRR], hid1[0:FW[k], q, k, :],
                                            start=n == 0, stop=n == 3 * NF - 1)
                            n += 1
                    ins.then_inc(rd_ready, 1)
                elif kind == "dn":
                    w = next_chunk("dn1", i, a)
                    if i == 0:
                        pe.wait_ge(up_used, 2 * NF + NF * (a + 1))
                    for kk in range(2 if i < 5 else 1):
                        k = 2 * i + kk
                        fw = FW[k]
                        for t in range(4):
                            for p in range(2):
                                ins = pe.matmul(PS[:, 2 + t, :], hid1[0:fw, p, k, t * P:(t + 1) * P], w[0:fw, 0, kk * D:(kk + 1) * D],
                                                start=k == 0 and p == 0, stop=k == NF - 1 and p == 1)
                            if k == NF - 1:
                                ins.then_inc(dn_ready, 1)
                    if i < 5:
                        ins.then_inc(chunk_used, 1)
                elif kind == "wout":
                    for t in range(NT):
                        half = t // 4
                        r = slice(CH * half, CH * half + CH)
                        if t == 0:
                            pe.wait_ge(ln_out, 2 * DEPTH + 1)
                        if t >= 2:
                            pe.wait_ge(s_ready, NT + t - 1)
                        pe.matmul(PS[:, t % 2, :], act1[r, (t % 4) * P:(t % 4 + 1) * P], wov[r, :], start=True, stop=True)\
                          .then_inc(wout_ready, 1)
                elif kind == "fin":
                    pe.wait_ge(split_done, chunk_place("lrb", 0, a)[0] + 1)
                    pe.wait_ge(rd_split, a + 1)
                    for t in range(4):
                        if t >= 2:
                            pe.wait_ge(fsum_ready, 4 * a + t - 1)
                        pe.matmul(PS[:, 6 + t % 2, :], lrh[:, t * P:(t + 1) * P], lrdb[:], start=True, stop=True)\
                          .then_inc(lrd_ready, 1)


_NEEDED = ("x", "wq", "wk", "wv", "wo", "gu0", "dn0", "winT", "lra", "gu1", "lrb", "lrd", "lrdb", "dn1", "cols", "bv", "bo",
           "bout", "dscale", "ssmw")


def packed_gate_up(gate, up, np):
    blocks = []
    for i in range(NF):
        o = slice(i * P, i * P + FW[i])
        for w in (gate, up):
            blocks.append(w[o, :].T.reshape(KD, P, FW[i]).transpose(1, 0, 2).reshape(P, KD * FW[i]))
    return np.ascontiguousarray(np.concatenate(blocks, axis=1))


def kernel(**inputs):
    import numpy as np
    import concourse.bacc as bacc
    from concourse.bass_utils import run_bass_kernel_spmd

    v = {k: np.asarray(a) for k, a in inputs.items()}
    l0 = {k[3:]: a for k, a in v.items() if k.startswith("L0_")}
    l1 = {k[3:]: a for k, a in v.items() if k.startswith("L1_")}
    twice = lambda a: np.concatenate([a, a], axis=0)
    at = lambda n: l1["attn_" + n]

    def tiles(a):
        return np.concatenate([a, a[:NF * P - F]]).reshape(NF, P).T

    columns = {
        "bq": l0["attn_bq"].reshape(4, P).T, "bk": l0["attn_bk"].reshape(P, 1),
        "ln1_w": twice(at("ln1_w").T), "ln1_b": twice(at("ln1_b").T), "scl": twice(at("sc_lin").T),
        "ln2_w": twice(at("ln2_w").T), "ln2_b": twice(at("ln2_b").T), "b2": twice(at("b2").T),
        "b1": at("b1").reshape(DEPTH * 2, P).T,
        "lnl_w": twice(at("lnl_w").reshape(CH, 1)), "lnl_b": twice(at("lnl_b").reshape(CH, 1)),
        "bin": twice(at("bin").reshape(CH, 1)),
        "lc_a": np.concatenate([at("lc_re").T, at("lc_im").T]), "lc_b": np.concatenate([at("lc_im").T, at("lc_re").T]),
        "ph_re": twice(at("phz_re").T), "ph_im": twice(at("phz_im").T),
        "gate_s": tiles(l1["ffn_gate_scale"]), "up_s": tiles(l1["ffn_up_scale"]),
    }
    w1 = twice(at("W1").transpose(2, 0, 1).reshape(CH, DEPTH * 256))
    w2 = at("W2").reshape(DEPTH, CH, 2, P).transpose(3, 0, 2, 1).reshape(P, DEPTH * 2 * CH)
    low_rank = lambda a: np.concatenate([a, a, a], axis=1)
    lra = np.concatenate([low_rank(l1[n]).reshape(KD, P, LRR).transpose(1, 0, 2).reshape(P, KD * LRR)
                          for n in ("ffn_gate_A", "ffn_up_A")], axis=1)
    b_blocks = []
    for i in range(NF):
        for n in ("ffn_gate_B", "ffn_up_B"):
            b_blocks.append(l1[n][:, i * P:i * P + FW[i]])
    lrb = np.concatenate(b_blocks, axis=1)
    down_a = low_rank(l1["ffn_down_A"])
    down_a = np.concatenate([down_a, down_a[:NF * P - F]])
    arrays = {
        "x": l0["attn_x"].reshape(TOK, D), "wq": l0["attn_Wq"], "wk": l0["attn_Wk"], "wv": l0["attn_Wv"], "wo": l0["attn_Wo"],
        "gu0": packed_gate_up(l0["ffn_W_gate"], l0["ffn_W_up"], np), "dn0": l0["ffn_W_down"].T,
        "winT": at("Win").T, "lra": lra, "gu1": packed_gate_up(l1["ffn_gate_q"], l1["ffn_up_q"], np),
        "lrb": np.concatenate([lrb, lrb, lrb]), "lrd": down_a.reshape(NF, P, LRR).transpose(1, 0, 2).reshape(P, NF * LRR),
        "lrdb": np.concatenate([l1["ffn_down_B"]] * 3), "dn1": l1["ffn_down_q"].T,
        "cols": np.concatenate([columns[n] for n in COLS], axis=1),
        "bv": l0["attn_bv"].reshape(1, P), "bo": l0["attn_bo"].reshape(1, D), "bout": at("bout").reshape(1, D),
        "dscale": l1["ffn_down_scale"].reshape(1, D),
        "ssmw": np.concatenate([w1, w2, twice(at("Wout").T)], axis=1),
    }
    arrays = {n: np.ascontiguousarray(arrays[n]) for n in _NEEDED}
    nc = bacc.Bacc("TRN2", target_bir_lowering=False, num_devices=1)
    A = {n: nc.dram_tensor("in_" + n, a.shape, mybir.dt.from_np(a.dtype), kind="ExternalInput").ap()
         for n, a in arrays.items()}
    A["out"] = nc.dram_tensor("out", (TOK, D), F32, kind="ExternalOutput").ap()
    build(nc, A)
    r = run_bass_kernel_spmd(nc, [{"in_" + n: a for n, a in arrays.items()}], core_ids=[0])
    return r.results[0]["out"].reshape(4, SEQ, D)
```

```python
from contextlib import ExitStack

import concourse.bass as bass
from concourse import mybir

F32 = mybir.dt.float32
F32R = mybir.dt.float32r
BF16 = mybir.dt.bfloat16
I32 = mybir.dt.int32
ALU = mybir.AluOpType
ACT = mybir.ActivationFunctionType
AX_X = mybir.AxisListType.X

P = 128
TOK = 1024
SEQ = 256
D = 512
KD = D // P
NT = TOK // P
HALF = 512
NKV = 8
GRP = 4
DH = 16
F = 1376
NF = 11
FW = [P] * (NF - 1) + [F - (NF - 1) * P]
DEPTH = 4
CH = 64
RANK = 32
LRR = 3 * RANK
SW = 1312
RW = 1056
EPS = 1e-5
MASKED = -1e30

COLS = {}
_at = 0
for _name, _n in (("bq", 4), ("bk", 1), ("ln1_w", 4), ("ln1_b", 4), ("scl", 4), ("ln2_w", 4), ("ln2_b", 4),
                  ("b2", 4), ("b1", 8), ("lnl_w", 1), ("lnl_b", 1), ("bin", 1), ("lc_a", 4), ("lc_b", 4),
                  ("ph_re", 4), ("ph_im", 4), ("gate_s", NF), ("up_s", NF)):
    COLS[_name] = (_at, _at + _n)
    _at += _n
NCOLS = _at


def weight_chunks():
    chunks = [("qkv", 0), ("qkv", 1), ("qkv", 2), ("wo", 0), ("wo", 1)]
    chunks += [("gu0", i) for i in range(NF)] + [("dn0", i) for i in range(6)]
    chunks += [("win", 0), ("lra", 0)]
    for _ in range(2):
        chunks += [("gu1", i) for i in range(NF)] + [("lrd", 0), ("lrb", 0)] + [("dn1", i) for i in range(6)]
    return chunks


CHUNKS = weight_chunks()
IN_RING = ("wo", "gu0", "dn0", "lra", "gu1", "lrd", "dn1")
N_STAGE = 2
N_RING = 2


def chunk_place(kind, index, half=0):
    seen = -1
    ring = 0
    for c, (k, i) in enumerate(CHUNKS):
        if (k, i) == (kind, index):
            seen += 1
            if seen == half:
                return c, ring
        ring += k in IN_RING
    raise ValueError(kind)


def chunk_dmas(kind):
    return {"qkv": 1, "gu1": 2}.get(kind, 1)


def stage_value(c):
    return 16 * sum(chunk_dmas(CHUNKS[x][0]) + (CHUNKS[x] == ("qkv", 2)) for x in range(c % N_STAGE, c + 1, N_STAGE))


LN_STEPS = ("mean", "var", "rstd")
SSM_STEPS = [(l, s) for l in range(DEPTH) for s in
             ("mean1", "var1", "rstd1", "sel", "comb", "mean2", "var2", "rstd2", "w1a", "w1b", "w2")]
SSM_STEPS += [(DEPTH, s) for s in ("mean1", "var1", "rstd1")]


def layer1_order():
    order = [("lowrank", 0, 0)]
    n = 0
    for half in range(2):
        for i in range(NF):
            for kind in ("gate", "up"):
                order.append((kind, half, i))
                if n < len(SSM_STEPS):
                    order.append(("ssm", n, 0))
                    n += 1
        order.append(("flush", half, 0))
        order.append(("rd", half, 0))
        for i in range(6):
            order.append(("dn", half, i))
            if n < len(SSM_STEPS):
                order.append(("ssm", n, 0))
                n += 1
        if half == 1:
            order.append(("wout", 0, 0))
        order.append(("fin", half, 0))
    assert n == len(SSM_STEPS)
    return order


ORDER1 = layer1_order()


def build(nc, A):
    ctx = ExitStack()
    with ctx:
        def common(name, shape, dt=F32):
            return ctx.enter_context(nc.sbuf_tensor(name, shape, dt))

        def sem(name):
            return ctx.enter_context(nc.semaphore(name))

        x = common("x_sb", [P, NT, D])
        xnT = common("xnT", [P, 2, KD, TOK], F32R)
        stage = common("stage", [P, N_STAGE, SW])
        ring = common("ring", [P, N_RING, 2, RW], F32R)
        xn = common("xn", [P, 2, D])
        ident = common("ident", [P, P])
        cols = common("cols", [P, NCOLS])
        row_b = common("row_b", [P, D])
        bn6 = common("bn6", [P, NT, 6])
        mv = common("mv", [P, NT, 2])
        ve = common("ve", [P, NT])
        rstd = common("rstd", [P, NT])
        nhalf = common("nhalf", [P, 8])
        PS = ctx.enter_context(nc.psum_tensor("PS", [P, 8, 512], F32))

        with nc.sbuf_tensor("wqkv", [P, 2, KD, 768], F32R) as wqkv:
            pass
        s_sb = common("s_sb", [P, NT, D])
        with ExitStack() as scope:
            def att(name, shape, dt=F32):
                return scope.enter_context(nc.sbuf_tensor(name, shape, dt))

            probs = att("probs", [P, 8, GRP * P])
            qs = att("qs", [P, 2, 4, GRP, SEQ], F32R)
            ks = att("ks", [P, 2, 2, 4, SEQ], F32R)
            v_sb = att("v_sb", [P, NT, NKV, 2 * DH])
            proj = att("proj", [P, HALF])
            proj_hl = att("proj_hl", [P, 2, 2, HALF], F32R)
            att_tok = att("att_tok", [P, 2, D])
            attT = att("attT", [P, 2, 2, KD, P], F32R)
            max_hl = att("max_hl", [32, 2, SEQ], F32R)
            negmax = att("negmax", [P, 4, 2, 32])
            maskA = att("maskA", [P, 4, P], BF16)
            identb = att("identb", [P, P], BF16)
            bv_b = att("bv_b", [P, P])
            bq4 = att("bq4", [P, 4])
            rden = att("rden", [P, 2, 16])
            outT = xn
        def late(name, shape, dt=F32):
            return ctx.enter_context(nc.sbuf_tensor(name, shape, dt))

        rot = late("rot", [P, DEPTH, SEQ])
        decay = late("decay", [P, DEPTH])
        first = late("first", [P, DEPTH])
        win_hl = late("win_hl", [P, 2, KD, 3 * CH], F32R)
        with ExitStack() as scope:
            def ff0(name, shape, dt=F32):
                return scope.enter_context(nc.sbuf_tensor(name, shape, dt))

            hid0 = ff0("hid0", [P, 2, NF, TOK], F32R)
            sg0 = ff0("sg0", [P, 2, HALF])
            ht0 = ff0("ht0", [P, 2, HALF])
            rotb = ff0("rotb", [P, DEPTH, SEQ // 2])
            cs = ff0("cs", [P, 12, DEPTH])
        rtmp = xn[:].rearrange("p a (l t) -> p a l t", l=DEPTH)
        hid1 = late("hid1", [P, 2, NF, HALF], F32R)
        lrx = late("lrx", [LRR, 2, TOK], F32R)
        lrh = late("lrh", [LRR, HALF], F32R)
        lrdb = late("lrdb", [LRR, D], F32R)
        dscale_b = late("dscale_b", [P, D])
        ssmw = late("ssmw", [P, DEPTH * 256 + DEPTH * 2 * CH + D])
        gs = late("gs", [P, 2, NF])
        e_lr = late("e_lr", [P, 2, HALF])
        e_gu = late("e_gu", [P, 2, HALF])
        e_h = xn[:, 1, :]
        h = late("h", [P, HALF])
        cen = late("cen", [P, HALF])
        tmp1 = late("tmp1", [P, HALF])
        act1 = late("act1", [P, HALF])
        dz = late("dz", [P, 2, HALF])
        sv = late("sv", [P, 2, 2, HALF])
        dmat = xn[:, 0, :]
        sel = late("sel", [P, 2, P])
        comb = late("comb", [P, 2, P])
        bd = late("bd", [P, P])
        bdc = late("bdc", [P, 2])
        tstat = late("tstat", [P, 8])
        trs = late("trs", [P, 8])

        w1v = ssmw[:, 0:DEPTH * 256].rearrange("p (l f) -> p l f", l=DEPTH)
        w2v = ssmw[:, DEPTH * 256:DEPTH * 256 + DEPTH * 2 * CH].rearrange("p (l t c) -> p l t c", l=DEPTH, t=2)
        wov = ssmw[:, DEPTH * 256 + DEPTH * 2 * CH:]

        def col(name, i=0, n=1):
            return cols[:, COLS[name][0] + i:COLS[name][0] + i + n]

        q_bounce = nc.dram_tensor("q_bounce", [2, 5 * P, TOK], F32).ap()
        m_bounce = nc.dram_tensor("m_bounce", [4, 2, 2, 16, SEQ], F32).ap()

        x_loaded = [sem(f"x_loaded{t}") for t in range(NT)]
        cols_loaded = sem("cols_loaded")
        bv_loaded = sem("bv_loaded")
        bo_loaded = sem("bo_loaded")
        late_loaded = sem("late_loaded")
        stage_loaded = [sem(f"stage_loaded{i}") for i in range(N_STAGE)]
        split_done = sem("split_done")
        chunk_used = sem("chunk_used")
        ident_ready = sem("ident_ready")
        consts_ready = sem("consts_ready")
        var_ready = sem("var_ready")
        rstd_ready = sem("rstd_ready")
        xn_ready = sem("xn_ready")
        xt_ready = sem("xt_ready")
        xh_ready = sem("xh_ready")
        xl_ready = sem("xl_ready")
        qkv_ready = sem("qkv_ready")
        proj_ready = sem("proj_ready")
        proj_split = sem("proj_split")
        v_ready = sem("v_ready")
        q_out = [sem(f"q_out{i}") for i in range(2)]
        qs_loaded = [sem(f"qs_loaded{i}") for i in range(2)]
        s1_ready = sem("s1_ready")
        max_ready = sem("max_ready")
        mt_ready = sem("mt_ready")
        mh_ready = sem("mh_ready")
        ml_ready = sem("ml_ready")
        ks_zeroed = sem("ks_zeroed")
        m_out = sem("m_out")
        m_loaded = [sem(f"m_loaded{i}") for i in range(2)]
        s2_ready = sem("s2_ready")
        exp_ready = sem("exp_ready")
        masked = sem("masked")
        pv_ready = sem("pv_ready")
        ot_ready = sem("ot_ready")
        tt_ready = sem("tt_ready")
        att_ready = sem("att_ready")
        at_ready = sem("at_ready")
        ah_ready = sem("ah_ready")
        al_ready = sem("al_ready")
        wo_ready = sem("wo_ready")
        s_ready = sem("s_ready")
        gu_ready = sem("gu_ready")
        gate_used = sem("gate_used")
        up_used = sem("up_used")
        hid_ready = sem("hid_ready")
        dn_ready = sem("dn_ready")
        g_ready = sem("g_ready")
        x1_ready = sem("x1_ready")
        lr_ready = sem("lr_ready")
        lr_copied = sem("lr_copied")
        lr_split = sem("lr_split")
        phasor_scaled = sem("phasor_scaled")
        polar_ready = sem("polar_ready")
        decay_ready = sem("decay_ready")
        rot_ready = sem("rot_ready")
        late_consts = sem("late_consts")
        gsum_ready = sem("gsum_ready")
        silu_ready = sem("silu_ready")
        fsum_ready = sem("fsum_ready")
        fg_ready = sem("fg_ready")
        rd_ready = sem("rd_ready")
        rd_copied = sem("rd_copied")
        rd_split = sem("rd_split")
        h0_ready = sem("h0_ready")
        h_ready = sem("h_ready")
        ln_mean = sem("ln_mean")
        ln_cen = sem("ln_cen")
        ln_sq = sem("ln_sq")
        ln_var = sem("ln_var")
        ln_stat = sem("ln_stat")
        ln_pow = sem("ln_pow")
        ln_spread = sem("ln_spread")
        ln_rstd = sem("ln_rstd")
        ln_norm = sem("ln_norm")
        ln_out = sem("ln_out")
        cv_sel = sem("cv_sel")
        cv_mod = sem("cv_mod")
        cv_comb = sem("cv_comb")
        w1_ready = sem("w1_ready")
        w1_act = sem("w1_act")
        w2_ready = sem("w2_ready")
        lrd_ready = sem("lrd_ready")
        win_ready = sem("win_ready")
        wout_ready = sem("wout_ready")
        out_ready = sem("out_ready")
        stored = sem("stored")
        dve_chain = sem("dve_chain")
        pool_chain = sem("pool_chain")
        act_chain = sem("act_chain")

        block = ctx.enter_context(nc.Block())

        @block.sync
        def _(sp):
            xd = A["x"].rearrange("(t p) d -> t p d", p=P)

            def chunk_load(c):
                kind, i = CHUNKS[c]
                if c >= N_STAGE:
                    sp.wait_ge(split_done, c - N_STAGE + 1)
                slot = stage[:, c % N_STAGE, :]
                done = stage_loaded[c % N_STAGE]
                if kind == "qkv" and i < 2:
                    sp.dma_start(slot[:, 0:1024].rearrange("p (k n) -> p k n", k=KD),
                                 A["wq"].rearrange("(k p) n -> p k n", p=P)[:, :, 256 * i:256 * i + 256]).then_inc(done, 16)
                elif kind == "qkv":
                    v = slot[:, 0:1024].rearrange("p (k n) -> p k n", k=KD)
                    sp.dma_start(v[:, :, 0:128], A["wk"].rearrange("(k p) n -> p k n", p=P)).then_inc(done, 16)
                    sp.dma_start(v[:, :, 128:256], A["wv"].rearrange("(k p) n -> p k n", p=P)).then_inc(done, 16)
                elif kind == "wo":
                    sp.dma_start(slot[:, 0:1024].rearrange("p (k n) -> p k n", k=2),
                                 A["wo"].rearrange("(k p) n -> p k n", p=P)[:, 2 * i:2 * i + 2, :]).then_inc(done, 16)
                elif kind == "gu0":
                    sp.dma_start(slot[:, 0:8 * FW[i]], A["gu0"][:, 1024 * i:1024 * i + 8 * FW[i]]).then_inc(done, 16)
                elif kind == "gu1":
                    sp.dma_start(slot[:, 0:8 * FW[i]].bitcast(I32), A["gu1"][:, 1024 * i:1024 * i + 8 * FW[i]]).then_inc(done, 16)
                    sp.dma_start(slot[0:LRR, 1024:1024 + 2 * FW[i]], A["lrb"][:, 256 * i:256 * i + 2 * FW[i]]).then_inc(done, 16)
                elif kind in ("dn0", "dn1"):
                    w = A[kind]
                    if i < 5:
                        to = slot[:, 0:1024].rearrange("p (k n) -> p k n", k=2)
                        of = w[256 * i:256 * i + 256, :].rearrange("(k p) n -> p k n", p=P)
                    else:
                        to = slot[0:FW[-1], 0:512]
                        of = w[1280:F, :]
                    sp.dma_start(to if kind == "dn0" else to.bitcast(I32), of).then_inc(done, 16)
                elif kind == "win":
                    sp.dma_start(slot[:, 0:256].rearrange("p (k n) -> p k n", k=KD),
                                 A["winT"].rearrange("(k p) n -> p k n", p=P)).then_inc(done, 16)
                elif kind == "lra":
                    sp.dma_start(slot[:, 0:768], A["lra"]).then_inc(done, 16)
                elif kind == "lrd":
                    sp.dma_start(slot[:, 0:1056], A["lrd"]).then_inc(done, 16)
                elif kind == "lrb":
                    sp.dma_start(slot[0:LRR, 0:512], A["lrdb"]).then_inc(done, 16)

            for t in range(2):
                sp.dma_start(x[:, t, :], xd[t]).then_inc(x_loaded[t], 16)
            for c in range(2):
                chunk_load(c)
            for t in range(2, NT):
                sp.dma_start(x[:, t, :], xd[t]).then_inc(x_loaded[t], 16)
            sp.dma_start(cols[:], A["cols"]).then_inc(cols_loaded, 16)
            sp.dma_start(bv_b[:], A["bv"].to_broadcast([P, P])).then_inc(bv_loaded, 16)
            sp.dma_start(row_b[:], A["bo"].to_broadcast([P, D])).then_inc(bo_loaded, 16)
            for c in range(2, 5):
                chunk_load(c)

            def projections_out(half):
                for u in range(5):
                    n = 5 * half + u
                    sp.wait_ge(proj_split, n + 1)
                    for part in range(2):
                        sp.dma_start(q_bounce[part, u * P:(u + 1) * P, half * HALF:(half + 1) * HALF],
                                     proj_hl[:, n % 2, part, :].bitcast(F32)).then_inc(q_out[n % 2], 16)

            def stacks_in(b):
                for i in range(2):
                    units = (3 - i, 5)[b // 2]
                    sp.wait_ge(q_out[i], 32 * units)
                if b == 0:
                    sp.wait_ge(ks_zeroed, 1)
                if b >= 2:
                    sp.wait_ge(s2_ready, 24 * (b - 1))
                t = slice(b * SEQ, (b + 1) * SEQ)
                for j in range(2):
                    for row, (qpart, kpart) in enumerate(((0, 0), (0, 1), (1, 0))):
                        r = slice(3 * DH * j + DH * row, 3 * DH * j + DH * (row + 1))
                        src = q_bounce[qpart, 256 * j:256 * (j + 1), t].rearrange("(a r) t -> r a t", r=DH)
                        sp.dma_start(qs[r, b % 2, :, :, :].rearrange("p m g t -> p (m g) t").bitcast(F32), src)\
                          .then_inc(qs_loaded[b % 2], 16)
                        src = q_bounce[kpart, 512 + 64 * j:512 + 64 * (j + 1), t].rearrange("(a r) t -> r a t", r=DH)
                        sp.dma_start(ks[r, b % 2, j, :, :].bitcast(F32), src).then_inc(qs_loaded[b % 2], 16)

            def maxima(b):
                sp.wait_ge(ml_ready, b + 1)
                for part in range(2):
                    sp.dma_start(m_bounce[b, :, part, :, :].rearrange("j a t -> j a t"),
                                 max_hl[:, part, :].bitcast(F32)).then_inc(m_out, 16)
                sp.wait_ge(m_out, 32 * (b + 1))
                sp.dma_start(qs[96:100, b % 2, :, :, :].rearrange("p m g t -> p (m g t)").bitcast(F32),
                             m_bounce[b].rearrange("j p a t -> (j p) (a t)")).then_inc(m_loaded[b % 2], 16)

            projections_out(0)
            stacks_in(0)
            stacks_in(1)
            projections_out(1)
            maxima(0)
            maxima(1)
            stacks_in(2)
            maxima(2)
            stacks_in(3)
            maxima(3)
            for c in range(5, 22):
                chunk_load(c)
            sp.wait_ge(s_ready, NT)
            sp.wait_ge(dn_ready, NT)
            sp.wait_ge(hid_ready, 2 * NF)
            sp.dma_start(row_b[:], A["bout"].to_broadcast([P, D])).then_inc(late_loaded, 16)
            sp.dma_start(dscale_b[:], A["dscale"].to_broadcast([P, D])).then_inc(late_loaded, 16)
            sp.dma_start(ssmw[:], A["ssmw"]).then_inc(late_loaded, 16)
            for c in range(22, len(CHUNKS)):
                chunk_load(c)
            od = A["out"].rearrange("(t p) d -> t p d", p=P)
            for t in range(NT):
                sp.wait_ge(out_ready, t + 1)
                sp.dma_start(od[t], x[:, t, :]).then_inc(stored, 16)
            sp.wait_ge(stored, 16 * NT)

        @block.gpsimd
        def _(pool):
            chain = [0]

            def link(ins):
                chain[0] += 1
                ins.then_inc(pool_chain, 1)
                pool.wait_ge(pool_chain, chain[0])

            signals = {}

            def signal(ins, done):
                signals[done.name] = signals.get(done.name, 0) + 1
                ins.then_inc(done, 1)
                pool.wait_ge(done, signals[done.name])

            def split(dst_hi, dst_lo, src, wait=True):
                link(pool.tensor_copy(dst_hi, src))
                return pool.tensor_tensor(dst_lo, src, dst_hi.bitcast(F32), ALU.subtract)

            def last_use(c):
                before = [x for x in range(c) if CHUNKS[x][0] in IN_RING][-N_RING]
                kind, i = CHUNKS[before]
                half = CHUNKS[:before].count(CHUNKS[before])
                if kind == "wo":
                    return wo_ready, NT
                if kind == "gu0":
                    return gu_ready, 2 * i + 2
                if kind == "gu1":
                    return gu_ready, 2 * NF + NF * half + i + 1
                if kind == "lra":
                    return lr_ready, 4
                if kind == "lrd":
                    return rd_ready, half + 1
                if i == 5:
                    return dn_ready, NT if kind == "dn0" else NT + 4 * half + 4
                return chunk_used, i + 1 if kind == "dn0" else 5 + 5 * half + i + 1

            def chunk_split(c):
                kind, i = CHUNKS[c]
                slot = stage[:, c % N_STAGE, :]
                pool.wait_ge(stage_loaded[c % N_STAGE], stage_value(c))
                rc = sum(k in IN_RING for k, _ in CHUNKS[:c])
                w = ring[:, rc % N_RING, :, :]
                if kind in IN_RING and rc >= N_RING:
                    pool.wait_ge(*last_use(c))
                if kind == "qkv":
                    to = wqkv[:, :, :, 256 * i:256 * i + 256]
                    of = slot[:, 0:1024].rearrange("p (k n) -> p k n", k=KD)
                    signal(split(to[:, 0], to[:, 1], of), split_done)
                elif kind in ("wo", "gu0", "dn0", "lra", "lrd"):
                    n = {"wo": 1024, "gu0": 8 * FW[i % NF], "dn0": 1024, "lra": 768, "lrd": 1056}[kind]
                    rows = P
                    if kind == "dn0" and i == 5:
                        n, rows = 512, FW[-1]
                    signal(split(w[0:rows, 0, 0:n], w[0:rows, 1, 0:n], slot[0:rows, 0:n]), split_done)
                elif kind == "win":
                    link(pool.memset(win_hl[:].bitcast(F32), 0.0))
                    of = slot[:, 0:256].rearrange("p (k n) -> p k n", k=KD)
                    signal(split(win_hl[:, 0, :, CH:2 * CH], win_hl[:, 1, :, CH:2 * CH], of), split_done)
                elif kind == "gu1":
                    link(pool.tensor_scalar(w[:, 0, 0:8 * FW[i]], slot[:, 0:8 * FW[i]].bitcast(I32), -7.5, None, ALU.add))
                    of = slot[0:LRR, 1024:1024 + 2 * FW[i]]
                    to = w[0:LRR, 1, 0:2 * FW[i]]
                    link(pool.tensor_copy(to, of))
                    mid = slice(RANK, 2 * RANK)
                    signal(pool.tensor_tensor(to[mid], of[mid], to[mid].bitcast(F32), ALU.subtract), split_done)
                elif kind == "dn1":
                    n, rows = (1024, P) if i < 5 else (512, FW[-1])
                    signal(pool.tensor_scalar(w[0:rows, 0, 0:n], slot[0:rows, 0:n].bitcast(I32), -7.5, None, ALU.add), split_done)
                elif kind == "lrb":
                    of = slot[0:LRR, 0:512]
                    if CHUNKS[:c].count(("lrb", 0)):
                        pool.wait_ge(dn_ready, NT + 4)
                    link(pool.tensor_copy(lrdb[:], of))
                    mid = slice(RANK, 2 * RANK)
                    signal(pool.tensor_tensor(lrdb[mid, :], of[mid], lrdb[mid, :].bitcast(F32), ALU.subtract), split_done)

            def rsqrt_pair(n, g):
                pool.wait_ge(var_ready, 4 * n + g + 1)
                signal(pool.tensor_tensor(rstd[:, 2 * g:2 * g + 2], ve[:, 2 * g:2 * g + 2], nhalf[:, 0:2], ALU.pow), rstd_ready)

            link(pool.memset(nhalf[:], -0.5))
            link(pool.memset(ident[:], 0.0))
            signal(pool.affine_select(out=ident[:], in_=ident[:], compare_op=ALU.not_equal, fill=1.0, base=0,
                               pattern=[[-1, P]], channel_multiplier=1), ident_ready)
            pool.wait_ge(ident_ready, 1)
            for g in range(4):
                rsqrt_pair(0, g)
            link(pool.memset(ks[:].bitcast(F32), 0.0))
            link(pool.memset(ks[96:98, :, 0, :, :].bitcast(F32), 1.0))
            link(pool.memset(ks[96:100, :, 1, :, :].bitcast(F32), 1.0))
            signal(pool.memset(ks[96:98, :, 1, :, :].bitcast(F32), 0.0), ks_zeroed)
            link(pool.memset(v_sb[:], 1.0))
            link(pool.memset(maskA[:], 0.0))
            link(pool.affine_select(out=maskA[:], in_=maskA[:], compare_op=ALU.is_ge, fill=MASKED, base=0,
                                    pattern=[[0, 4], [-1, P]], channel_multiplier=1))
            signal(pool.tensor_copy(identb[:], ident[:]), consts_ready)
            for c in range(5):
                chunk_split(c)
            for G in range(24):
                for kv in range(4 if G % 3 != 1 else 0):
                    n = 4 * G + kv
                    pool.wait_ge(exp_ready, n + 1)
                    pt = probs[:, n % 8, :].rearrange("p (g q) -> p g q", g=GRP)
                    pool.affine_select(out=pt, in_=pt, compare_op=ALU.is_ge, fill=0.0, base=0,
                                       pattern=[[0, GRP], [1, P]], channel_multiplier=-1).then_inc(masked, 1)
            pool.wait_ge(masked, 64)

            def rot_start():
                pool.wait_ge(phasor_scaled, 1)
                link(pool.memset(cs[0:64, 5, :], 1.0))
                link(pool.memset(cs[64:128, 5, :], -1.0))
                link(pool.tensor_tensor(cs[:, 8, :], cs[:, 3, :], nhalf[:, 0:DEPTH], ALU.pow))
                link(pool.tensor_tensor(cs[:, 6, :], cs[:, 0, :], cs[:, 8, :], ALU.mult))
                link(pool.tensor_tensor(cs[:, 7, :], cs[:, 1, :], cs[:, 8, :], ALU.mult))
                link(pool.tensor_tensor(cs[:, 9, :], cs[:, 3, :], cs[:, 8, :], ALU.mult))
                signal(pool.tensor_tensor(cs[:, 4, :], cs[:, 9, :], cs[:, 2, :], ALU.mult), polar_ready)
                link(pool.tensor_tensor(cs[:, 10, :], cs[:, 6, :], cs[:, 5, :], ALU.mult))
                link(pool.tensor_tensor(cs[:, 10, :], cs[:, 10, :], col("lc_a", 0, 4), ALU.mult))
                link(pool.tensor_tensor(cs[:, 11, :], cs[:, 7, :], col("lc_b", 0, 4), ALU.mult))
                link(pool.tensor_tensor(cs[:, 10, :], cs[:, 10, :], cs[:, 11, :], ALU.subtract))
                pool.wait_ge(decay_ready, 1)
                link(pool.tensor_tensor(first[:], cs[:, 10, :], decay[:], ALU.mult))
                link(pool.memset(rot[0:64, :, 0:1], 1.0))
                link(pool.memset(rot[64:128, :, 0:1], 0.0))
                link(pool.memset(rotb[0:64, :, 0:1], 0.0))
                link(pool.memset(rotb[64:128, :, 0:1], 1.0))

            def rot_step(k):
                n = 1 << k
                link(pool.tensor_tensor(cs[:, 8, :], cs[:, 6, :], cs[:, 6, :], ALU.mult))
                link(pool.tensor_tensor(cs[:, 9, :], cs[:, 7, :], cs[:, 7, :], ALU.mult))
                link(pool.tensor_tensor(cs[:, 8, :], cs[:, 8, :], cs[:, 9, :], ALU.add))
                link(pool.tensor_scalar(cs[:, 8, :], cs[:, 8, :], -0.5, 1.5, ALU.mult, ALU.add))
                link(pool.tensor_tensor(cs[:, 6, :], cs[:, 6, :], cs[:, 8, :], ALU.mult))
                link(pool.tensor_tensor(cs[:, 7, :], cs[:, 7, :], cs[:, 8, :], ALU.mult))
                c = cs[:, 6, :].unsqueeze(2).to_broadcast([P, DEPTH, n])
                s = cs[:, 7, :].unsqueeze(2).to_broadcast([P, DEPTH, n])
                a, b = rot[:, :, 0:n], rotb[:, :, 0:n]
                link(pool.tensor_tensor(rtmp[:, 0, :, 0:n], a, c, ALU.mult))
                link(pool.tensor_tensor(rtmp[:, 1, :, 0:n], b, s, ALU.mult))
                if k == 7:
                    signal(pool.tensor_tensor(rot[:, :, n:2 * n], rtmp[:, 0, :, 0:n], rtmp[:, 1, :, 0:n], ALU.add), rot_ready)
                    return
                link(pool.tensor_tensor(rot[:, :, n:2 * n], rtmp[:, 0, :, 0:n], rtmp[:, 1, :, 0:n], ALU.add))
                link(pool.tensor_tensor(rtmp[:, 0, :, 0:n], b, c, ALU.mult))
                link(pool.tensor_tensor(rtmp[:, 1, :, 0:n], a, s, ALU.mult))
                link(pool.tensor_tensor(rotb[:, :, n:2 * n], rtmp[:, 0, :, 0:n], rtmp[:, 1, :, 0:n], ALU.subtract))
                link(pool.tensor_tensor(cs[:, 8, :], cs[:, 6, :], cs[:, 6, :], ALU.mult))
                link(pool.tensor_tensor(cs[:, 9, :], cs[:, 7, :], cs[:, 7, :], ALU.mult))
                link(pool.tensor_tensor(cs[:, 10, :], cs[:, 6, :], cs[:, 7, :], ALU.mult))
                link(pool.tensor_tensor(cs[:, 6, :], cs[:, 8, :], cs[:, 9, :], ALU.subtract))
                link(pool.tensor_tensor(cs[:, 7, :], cs[:, 10, :], cs[:, 10, :], ALU.add))

            for c in range(5, 22):
                chunk_split(c)
                if c == 7:
                    rot_start()
                if 8 <= c < 16:
                    rot_step(c - 8)
            for g in range(4):
                rsqrt_pair(1, g)
            chunk_split(22)
            pool.wait_ge(dn_ready, NT)
            pool.wait_ge(x1_ready, NT)
            link(pool.memset(sel[:], 0.0))
            link(pool.memset(comb[:], 0.0))
            link(pool.memset(bd[:], 0.0))
            link(pool.memset(bdc[:], 0.0))
            for j in range(2):
                r = slice(CH * j, CH * j + CH)
                for i in range(2):
                    link(pool.tensor_copy(sel[r, j, CH * i:CH * i + CH], ident[r, r]))
                link(pool.tensor_tensor(comb[:, j, r], ident[:, 0:CH], ident[:, CH:P], ALU.add))
                link(pool.memset(bd[r, r], 1.0 / CH))
                ins = pool.memset(bdc[r, j:j + 1], 1.0 / CH)
                if j == 0:
                    link(ins)
                else:
                    signal(ins, late_consts)
            c = 23
            for kind, a, i in ORDER1:
                if kind == "ssm":
                    l, step = SSM_STEPS[a]
                    if step in ("var1", "var2"):
                        nth = 2 * l + (step == "var2")
                        pool.wait_ge(ln_stat, nth + 1)
                        signal(pool.tensor_tensor(trs[:], tstat[:], nhalf[:], ALU.pow), ln_pow)
                    continue
                ahead = {"lowrank": 2, "gate": 1, "rd": 3, "dn": 1}.get(kind, 0)
                for _ in range(ahead):
                    if c < len(CHUNKS):
                        chunk_split(c)
                        c += 1
            assert c == len(CHUNKS)

        @block.scalar
        def _(act):
            chain = [0]

            def link(ins):
                chain[0] += 1
                ins.then_inc(act_chain, 1)
                act.wait_ge(act_chain, chain[0])

            def ln_hi(n, t):
                act.wait_ge(xt_ready, NT * n + t + 1)
                act.activation(xnT[:, 0, :, t * P:(t + 1) * P], PS[:, t % 2, :].rearrange("p (k q) -> p k q", k=KD),
                               ACT.Copy).then_inc(xh_ready, 1)

            for t in range(NT):
                ln_hi(0, t)

            def projection(n):
                half, u = n // 5, n % 5
                act.wait_ge(qkv_ready, 6 * half + u + 1)
                if n:
                    act.wait_ge(proj_split, n)
                if n == 0:
                    act.wait_ge(dve_chain, 1)
                bias, scale = (bq4[:, u:u + 1], 0.25) if u < 4 else (col("bk"), 1.0)
                act.activation(proj[:], PS[:, u % 2, :], ACT.Identity, bias=bias, scale=scale).then_inc(proj_ready, 1)

            def max_hi(b):
                act.wait_ge(mt_ready, b + 1)
                if b:
                    act.wait_ge(m_out, 32 * b)
                act.activation(max_hl[:, 0, :], PS[0:32, 2, 0:SEQ], ACT.Copy).then_inc(mh_ready, 1)

            def exps(G):
                for kv in range(4):
                    n = 4 * G + kv
                    act.wait_ge(s2_ready, n + 1)
                    if G >= 2:
                        act.wait_ge(pv_ready, G - 1)
                    act.activation(probs[:, n % 8, :], PS[:, n % 2, :], ACT.Exp).then_inc(exp_ready, 1)

            def outputs(b, quad):
                act.wait_ge(pv_ready, 6 * b + 3 * quad + 3)
                for qt in range(2):
                    n = 4 * b + 2 * quad + qt
                    if n >= 2:
                        act.wait_ge(tt_ready, n - 1)
                    act.activation(outT[:, qt, :], PS[:, 5 + qt, :], ACT.Copy).then_inc(ot_ready, 1)

            def attT_hi(b):
                for qt in range(2):
                    t = 2 * b + qt
                    act.wait_ge(at_ready, t + 1)
                    if t >= 2:
                        act.wait_ge(wo_ready, t - 1)
                    act.activation(attT[:, qt, 0, :, :], PS[:, 5 + qt, :].rearrange("p (k q) -> p k q", k=KD), ACT.Copy)\
                       .then_inc(ah_ready, 1)

            for n in range(10):
                projection(n)
            max_hi(0)
            exps(0)
            for b in range(4):
                for g in range(6):
                    if g < 5:
                        exps(6 * b + g + 1)
                    if g == 2:
                        outputs(b, 0)
                    if g == 4 and b < 3:
                        max_hi(b + 1)
                outputs(b, 1)
                if b < 3:
                    exps(6 * b + 6)
                attT_hi(b)
            act.wait_ge(polar_ready, 1)
            act.activation(decay[:], cs[:, 4, :], ACT.Tanh).then_inc(decay_ready, 1)
            for job in range(2 * NF):
                i = job // 2
                act.wait_ge(gu_ready, job + 1)
                if job >= 2:
                    act.wait_ge(up_used, job - 1)
                act.activation(sg0[0:FW[i], job % 2, :], PS[0:FW[i], 2 + 2 * (job % 3), :], ACT.Silu).then_inc(gate_used, 1)
            for t in range(NT):
                act.wait_ge(dn_ready, t + 1)
                if t < 2:
                    act.wait_ge(up_used, 2 * NF)
                else:
                    act.wait_ge(x1_ready, t - 1)
                act.activation(sg0[:, t % 2, :], PS[:, t, :], ACT.Silu).then_inc(g_ready, 1)
            for t in range(NT):
                ln_hi(1, t)
            act.wait_ge(win_ready, 1)
            act.activation(h[:], PS[:, 2, :], ACT.Identity, bias=col("bin"), scale=1.0).then_inc(h0_ready, 1)

            def copies(J):
                fw = FW[J % NF]
                act.wait_ge(gu_ready, 2 * NF + J + 1)
                if J:
                    act.wait_ge(up_used, 2 * NF + J)
                for o in range(2):
                    ins = act.activation(e_lr[0:fw, o, :], PS[0:fw, 6 + o, :], ACT.Copy)
                ins.then_inc(lr_copied, 1)

            def silu(J):
                fw = FW[J % NF]
                act.wait_ge(gsum_ready, J + 1)
                if J:
                    act.wait_ge(hid_ready, 2 * NF + J)
                act.activation(e_h[0:fw, :], e_gu[0:fw, 0, :], ACT.Silu).then_inc(silu_ready, 1)

            def model(n):
                l, step = SSM_STEPS[n]
                nth = 2 * l + (step[-1] == "2")
                if step in ("mean1", "mean2"):
                    act.wait_ge(ln_cen, nth + 1)
                    act.activation(tmp1[:], cen[:], ACT.Square).then_inc(ln_sq, 1)
                elif step in ("rstd1", "rstd2"):
                    act.wait_ge(ln_norm, nth + 1)
                    if l == DEPTH:
                        f, w, b = ACT.Identity, col("lnl_w"), col("lnl_b")
                    elif step == "rstd1":
                        f, w, b = ACT.Silu, col("ln1_w", l), col("ln1_b", l)
                    else:
                        f, w, b = ACT.Identity, col("ln2_w", l), col("ln2_b", l)
                    act.activation(act1[:], cen[:], f, bias=b, scale=w).then_inc(ln_out, 1)
                elif step in ("w1a", "w1b"):
                    ft = int(step == "w1b")
                    act.wait_ge(w1_ready, 2 * l + ft + 1)
                    for half in range(2):
                        ins = act.activation(sv[:, ft, half, :], PS[:, half, :], ACT.Silu, bias=col("b1", 2 * l + ft))
                    ins.then_inc(w1_act, 1)

            for kind, a, i in ORDER1:
                J = NF * a + i
                if kind == "lowrank":
                    for o in range(4):
                        act.wait_ge(lr_ready, o + 1)
                        if o >= 2:
                            act.wait_ge(lr_split, o - 1)
                        act.activation(e_lr[0:LRR, o % 2, :], PS[0:LRR, 3 + o, :], ACT.Copy, scale=0.02).then_inc(lr_copied, 1)
                    act.wait_ge(lr_split, 4)
                elif kind == "gate" and i:
                    copies(J - 1)
                elif kind == "up" and i:
                    silu(J - 1)
                elif kind == "flush":
                    copies(NF * a + NF - 1)
                    silu(NF * a + NF - 1)
                elif kind == "ssm":
                    model(a)
                elif kind == "rd":
                    act.wait_ge(rd_ready, a + 1)
                    act.wait_ge(up_used, 2 * NF + NF * (a + 1))
                    act.activation(e_lr[0:LRR, 0, :], PS[0:LRR, 6, :], ACT.Copy, scale=0.02).then_inc(rd_copied, 1)
                elif kind == "fin":
                    for t in range(4):
                        act.wait_ge(fsum_ready, 4 * a + t + 1)
                        if a == 0:
                            act.activation(s_sb[:, t, :], e_gu[:, t % 2, :], ACT.Silu).then_inc(fg_ready, 1)
                        else:
                            if t >= 2:
                                act.wait_ge(out_ready, 4 + t - 1)
                            act.activation(e_lr[:, t % 2, :], e_gu[:, t % 2, :], ACT.Silu).then_inc(fg_ready, 1)

        @block.vector
        def _(dve):
            chain = [0]

            def link(ins):
                chain[0] += 1
                ins.then_inc(dve_chain, 1)
                dve.wait_ge(dve_chain, chain[0])

            dve.wait_ge(cols_loaded, 16)
            link(dve.tensor_scalar(bq4[:], col("bq", 0, 4), 0.25, None, ALU.mult))

            def layernorm(n):
                for g in range(5):
                    if g < 4:
                        for t in (2 * g, 2 * g + 1):
                            if n == 0:
                                dve.wait_ge(x_loaded[t], 16)
                            link(dve.bn_stats(bn6[:, t, :], x[:, t, :]))
                            link(dve.bn_aggr(mv[:, t, :], bn6[:, t, :]))
                        dve.tensor_scalar(ve[:, 2 * g:2 * g + 2], mv[:, 2 * g:2 * g + 2, 1], EPS, None, ALU.add)\
                           .then_inc(var_ready, 1)
                    if g:
                        dve.wait_ge(rstd_ready, 4 * n + g)
                        for t in (2 * g - 2, 2 * g - 1):
                            if NT * n + t >= 2:
                                dve.wait_ge(xt_ready, NT * n + t - 1)
                            dve.tensor_scalar(xn[:, t % 2, :], x[:, t, :], mv[:, t, 0:1], rstd[:, t:t + 1],
                                              ALU.subtract, ALU.mult).then_inc(xn_ready, 1)
                        for t in (2 * g - 2, 2 * g - 1):
                            dve.wait_ge(xh_ready, NT * n + t + 1)
                            o = slice(t * P, (t + 1) * P)
                            dve.tensor_tensor(xnT[:, 1, :, o], PS[:, t % 2, :].rearrange("p (k q) -> p k q", k=KD),
                                              xnT[:, 0, :, o].bitcast(F32), ALU.subtract).then_inc(xl_ready, 1)

            layernorm(0)

            def projection_split(n):
                dve.wait_ge(proj_ready, n + 1)
                if n >= 2:
                    dve.wait_ge(q_out[n % 2], 32 * (n // 2))
                link(dve.tensor_copy(proj_hl[:, n % 2, 0, :], proj[:]))
                dve.tensor_tensor(proj_hl[:, n % 2, 1, :], proj[:], proj_hl[:, n % 2, 0, :].bitcast(F32),
                                  ALU.subtract).then_inc(proj_split, 1)

            def values_in(half):
                dve.wait_ge(qkv_ready, 6 * half + 6)
                if half == 0:
                    dve.wait_ge(consts_ready, 1)
                    dve.wait_ge(bv_loaded, 16)
                for q in range(4):
                    ins = dve.tensor_tensor(v_sb[:, 4 * half + q, :, 0:DH],
                                            PS[:, 1, q * P:(q + 1) * P].rearrange("p (h e) -> p h e", h=NKV),
                                            bv_b[:].rearrange("p (h e) -> p h e", h=NKV), ALU.add)
                ins.then_inc(v_ready, 1)

            def maximum(b, unit):
                m, gp = unit // 2, unit % 2
                dve.wait_ge(s1_ready, 8 * b + unit + 1)
                for qt in range(2):
                    to = negmax[:, b, qt, :].rearrange("p (j m g) -> p m g j", j=2, m=4)[:, m, 2 * gp:2 * gp + 2, :]
                    if qt == 0:
                        of = PS[:, 2, :].rearrange("p (g j k) -> p g j k", g=2, j=2)
                    else:
                        of = PS[:, 3:5, :].rearrange("p g (j k) -> p g j k", j=2)
                    ins = dve.tensor_reduce(to, of, AX_X, ALU.max, negate=True)
                ins.then_inc(max_ready, 1)

            def max_lo(b):
                dve.wait_ge(mh_ready, b + 1)
                dve.tensor_tensor(max_hl[:, 1, :], PS[0:32, 2, 0:SEQ], max_hl[:, 0, :].bitcast(F32), ALU.subtract)\
                   .then_inc(ml_ready, 1)

            def normalise(b, quad):
                for qt in range(2):
                    n = 4 * b + 2 * quad + qt
                    dve.wait_ge(tt_ready, n + 1)
                    if b and quad == 0:
                        dve.wait_ge(at_ready, 2 * b)
                    if n >= 2:
                        dve.wait_ge(att_ready, n - 1)
                    o = PS[:, 7, :].rearrange("p (g k e) -> p g k e", g=GRP, k=4)
                    den = rden[:, qt, :].rearrange("p (g k) -> p g k", g=GRP)
                    link(dve.reciprocal(den, o[:, :, :, DH]))
                    to = att_tok[:, qt, 256 * quad:256 * (quad + 1)].rearrange("p (k g e) -> p g k e", k=4, g=GRP)
                    dve.tensor_tensor(to, o[:, :, :, 0:DH], den.unsqueeze(3).to_broadcast([P, GRP, 4, DH]), ALU.mult)\
                       .then_inc(att_ready, 1)

            def attT_lo(b):
                for qt in range(2):
                    dve.wait_ge(ah_ready, 2 * b + qt + 1)
                    dve.tensor_tensor(attT[:, qt, 1, :, :], PS[:, 5 + qt, :].rearrange("p (k q) -> p k q", k=KD),
                                      attT[:, qt, 0, :, :].bitcast(F32), ALU.subtract).then_inc(al_ready, 1)

            def s_out(b):
                for qt in range(2):
                    t = 2 * b + qt
                    dve.wait_ge(wo_ready, t + 1)
                    if t == 0:
                        dve.wait_ge(bo_loaded, 16)
                    dve.tensor_tensor(s_sb[:, t, :], PS[:, 7, :], row_b[:], ALU.add).then_inc(s_ready, 1)

            for n in range(5):
                projection_split(n)
            values_in(0)
            for u in range(3):
                projection_split(5 + u)
            for unit in range(8):
                maximum(0, unit)
                if unit in (1, 3):
                    projection_split(8 + unit // 2)
                if unit == 5:
                    values_in(1)
            max_lo(0)
            for b in range(4):
                for g in range(6):
                    if b < 3 and g < 4:
                        maximum(b + 1, 2 * g)
                        maximum(b + 1, 2 * g + 1)
                    if g == 3:
                        normalise(b, 0)
                    if b < 3 and g == 4:
                        max_lo(b + 1)
                normalise(b, 1)
                attT_lo(b)
                s_out(b)
            re, im = col("ph_re", 0, 4), col("ph_im", 0, 4)
            dve.wait_ge(s_ready, NT)
            link(dve.tensor_scalar(cs[:, 8, :], re, -1.0, None, ALU.mult))
            link(dve.tensor_scalar(cs[:, 9, :], im, -1.0, None, ALU.mult))
            link(dve.tensor_tensor(cs[:, 8, :], cs[:, 8, :], re, ALU.max))
            link(dve.tensor_tensor(cs[:, 9, :], cs[:, 9, :], im, ALU.max))
            link(dve.tensor_tensor(cs[:, 2, :], cs[:, 8, :], cs[:, 9, :], ALU.max))
            link(dve.tensor_scalar(cs[:, 10, :], cs[:, 2, :], 0.0, None, ALU.is_equal))
            link(dve.tensor_scalar(cs[:, 8, :], cs[:, 2, :], 1.2e-38, None, ALU.max))
            link(dve.reciprocal(cs[:, 9, :], cs[:, 8, :]))
            link(dve.tensor_tensor(cs[:, 0, :], re, cs[:, 9, :], ALU.mult))
            link(dve.tensor_tensor(cs[:, 0, :], cs[:, 0, :], cs[:, 10, :], ALU.add))
            link(dve.tensor_tensor(cs[:, 1, :], im, cs[:, 9, :], ALU.mult))
            link(dve.tensor_tensor(cs[:, 8, :], cs[:, 0, :], cs[:, 0, :], ALU.mult))
            link(dve.tensor_tensor(cs[:, 9, :], cs[:, 1, :], cs[:, 1, :], ALU.mult))
            dve.tensor_tensor(cs[:, 3, :], cs[:, 8, :], cs[:, 9, :], ALU.add).then_inc(phasor_scaled, 1)
            for job in range(2 * NF):
                i, half = job // 2, job % 2
                fw = FW[i]
                hs = slice(half * HALF, (half + 1) * HALF)
                dve.wait_ge(gate_used, job + 1)
                hid = ht0[0:fw, job % 2, :]
                dve.tensor_tensor(hid, sg0[0:fw, job % 2, :], PS[0:fw, 3 + 2 * (job % 3), :], ALU.mult).then_inc(up_used, 1)
                dve.wait_ge(up_used, job + 1)
                link(dve.tensor_copy(hid0[0:fw, 0, i, hs], hid))
                dve.tensor_tensor(hid0[0:fw, 1, i, hs], hid, hid0[0:fw, 0, i, hs].bitcast(F32), ALU.subtract)\
                   .then_inc(hid_ready, 1)
            for t in range(NT):
                dve.wait_ge(g_ready, t + 1)
                link(dve.tensor_tensor(ht0[:, t % 2, :], sg0[:, t % 2, :], s_sb[:, t, :], ALU.mult))
                dve.tensor_tensor(x[:, t, :], x[:, t, :], ht0[:, t % 2, :], ALU.add).then_inc(x1_ready, 1)
            dve.wait_ge(x1_ready, NT)
            dve.wait_ge(rot_ready, 1)
            layernorm(1)
            dve.wait_ge(late_loaded, 48)
            for o, name in ((0, "gate_s"), (1, "up_s")):
                link(dve.tensor_scalar(gs[:, o, :], col(name, 0, NF), 0.005, None, ALU.mult))
            link(dve.tensor_scalar(dscale_b[:], dscale_b[:], 0.005, None, ALU.mult))

            def sums(J):
                i = J % NF
                fw = FW[i]
                dve.wait_ge(lr_copied, 4 + J + 1)
                for o in range(2):
                    dve.scalar_tensor_tensor(e_gu[0:fw, o, :], PS[0:fw, 2 + 2 * (J % 2) + o, :], gs[0:fw, o, i:i + 1],
                                             e_lr[0:fw, o, :], ALU.mult, ALU.add).then_inc((gsum_ready, up_used)[o], 1)

            def hidden(J):
                half, i = J // NF, J % NF
                fw = FW[i]
                if half == 1 and i == 0:
                    dve.wait_ge(dn_ready, NT + 4)
                dve.wait_ge(silu_ready, J + 1)
                dve.wait_ge(up_used, 2 * NF + J + 1)
                hid = e_gu[0:fw, 1, :]
                link(dve.tensor_tensor(hid, hid, e_h[0:fw, :], ALU.mult))
                link(dve.tensor_copy(hid1[0:fw, 0, i, :], hid))
                dve.tensor_tensor(hid1[0:fw, 1, i, :], hid, hid1[0:fw, 0, i, :].bitcast(F32), ALU.subtract).then_inc(hid_ready, 1)
                dve.wait_ge(hid_ready, 2 * NF + J + 1)

            def model(n):
                l, step = SSM_STEPS[n]
                nth = 2 * l + (step[-1] == "2")
                if step in ("mean1", "mean2"):
                    dve.wait_ge(ln_mean, nth + 1)
                    dve.tensor_tensor(cen[:], h[:], PS[:, 0, :], ALU.subtract).then_inc(ln_cen, 1)
                elif step in ("var1", "var2"):
                    dve.wait_ge(ln_var, nth + 1)
                    dve.tensor_scalar(tstat[:], PS[:, 1, 0:8], EPS, None, ALU.add).then_inc(ln_stat, 1)
                    dve.wait_ge(ln_pow, nth + 1)
                    dve.tensor_copy(tmp1[:].rearrange("p (c e) -> p c e", c=8),
                                    trs[:].unsqueeze(2).to_broadcast([P, 8, CH])).then_inc(ln_spread, 1)
                elif step in ("rstd1", "rstd2"):
                    dve.wait_ge(ln_rstd, nth + 1)
                    dve.tensor_tensor(cen[:], cen[:], PS[:, 0, :], ALU.mult).then_inc(ln_norm, 1)
                elif step == "sel":
                    link(dve.tensor_copy(dmat[:], decay[:, l:l + 1].to_broadcast([P, HALF])))
                    link(dve.memset(dmat[:, 0:HALF:SEQ], 0.0))
                    dve.wait_ge(cv_sel, l + 1)
                    r = rot[:, l, :].unsqueeze(1).to_broadcast([P, 2, SEQ])
                    for j in range(2):
                        link(dve.tensor_tensor(dz[:, j, :].rearrange("p (s t) -> p s t", s=2),
                                               PS[:, j, :].rearrange("p (s t) -> p s t", s=2), r, ALU.mult))
                    for j in range(2):
                        link(dve.tensor_scalar(dz[:, j, 0:HALF:SEQ], dz[:, j, 0:HALF:SEQ], first[:, l:l + 1], None, ALU.add))
                    for j in range(2):
                        link(dve.tensor_tensor_scan(sv[:, 0, j, :], dmat[:], dz[:, j, :], 0.0, ALU.mult, ALU.add))
                    for j in range(2):
                        ins = dve.tensor_tensor(dz[:, j, :].rearrange("p (s t) -> p s t", s=2),
                                                sv[:, 0, j, :].rearrange("p (s t) -> p s t", s=2), r, ALU.mult)
                    ins.then_inc(cv_mod, 1)
                elif step == "comb":
                    dve.wait_ge(cv_comb, l + 1)
                    dve.scalar_tensor_tensor(h[:], PS[:, 0, :], col("scl", l), h[:], ALU.mult, ALU.add).then_inc(h_ready, 1)
                    dve.wait_ge(h_ready, 2 * l + 1)
                elif step == "w2":
                    dve.wait_ge(w2_ready, l + 1)
                    dve.scalar_tensor_tensor(h[:], PS[:, 0, :], col("b2", l), h[:], ALU.add, ALU.add).then_inc(h_ready, 1)
                    dve.wait_ge(h_ready, 2 * l + 2)

            def down_sum(n):
                t = n % 4
                dve.wait_ge(lrd_ready, n + 1)
                if n % 4 >= 2:
                    dve.wait_ge(fg_ready, n - 1)
                link(dve.tensor_tensor(e_gu[:, t % 2, :], PS[:, 2 + t, :], dscale_b[:], ALU.mult))
                dve.tensor_tensor(e_gu[:, t % 2, :], e_gu[:, t % 2, :], PS[:, 6 + t % 2, :], ALU.add).then_inc(fsum_ready, 1)

            def gated(n):
                dve.wait_ge(fg_ready, n + 1)
                link(dve.tensor_tensor(s_sb[:, n, :], s_sb[:, n, :], e_lr[:, n % 2, :], ALU.mult))
                dve.tensor_tensor(x[:, n, :], x[:, n, :], s_sb[:, n, :], ALU.add).then_inc(out_ready, 1)

            for kind, a, i in ORDER1:
                J = NF * a + i
                if kind == "lowrank":
                    for o in range(4):
                        dve.wait_ge(lr_copied, o + 1)
                        to = lrx[:, o // 2, (o % 2) * HALF:(o % 2 + 1) * HALF]
                        of = e_lr[0:LRR, o % 2, :]
                        low = slice(2 * RANK, LRR)
                        link(dve.tensor_copy(to, of))
                        dve.tensor_tensor(to[low], of[low], to[low].bitcast(F32), ALU.subtract).then_inc(lr_split, 1)
                elif kind == "gate" and i:
                    sums(J - 1)
                elif kind == "up" and i:
                    hidden(J - 1)
                elif kind == "flush":
                    sums(NF * a + NF - 1)
                    hidden(NF * a + NF - 1)
                elif kind == "ssm":
                    model(a)
                elif kind == "rd":
                    dve.wait_ge(rd_copied, a + 1)
                    if a:
                        dve.wait_ge(lrd_ready, 4)
                    low = slice(2 * RANK, LRR)
                    link(dve.tensor_copy(lrh[:], e_lr[0:LRR, 0, :]))
                    dve.tensor_tensor(lrh[low, :], e_lr[low, 0, :], lrh[low, :].bitcast(F32), ALU.subtract).then_inc(rd_split, 1)
                elif kind == "wout":
                    for t in range(NT):
                        dve.wait_ge(wout_ready, t + 1)
                        if t < 4:
                            link(dve.tensor_tensor(dz[:, 0, :], PS[:, t % 2, :], row_b[:], ALU.add))
                            s_taken = dve.tensor_tensor(dz[:, 1, :], dz[:, 0, :], s_sb[:, t, :], ALU.mult)
                            s_taken.then_inc(s_ready, 1)
                            dve.wait_ge(s_ready, NT + t + 1)
                            dve.tensor_tensor(x[:, t, :], x[:, t, :], dz[:, 1, :], ALU.add).then_inc(out_ready, 1)
                            dve.wait_ge(out_ready, t + 1)
                        else:
                            dve.tensor_tensor(s_sb[:, t, :], PS[:, t % 2, :], row_b[:], ALU.add).then_inc(s_ready, 1)
                            dve.wait_ge(s_ready, NT + t + 1)
                elif kind == "fin":
                    for t in range(5):
                        if t < 4:
                            down_sum(4 * a + t)
                        if t and a:
                            gated(4 * a + t - 1)

        @block.tensor
        def _(pe):
            def products(out, pairs):
                pairs = list(pairs)
                for n, (w, m) in enumerate(pairs):
                    ins = pe.matmul(out, w, m, start=n == 0, stop=n == len(pairs) - 1)
                return ins

            PARTS = ((0, 0), (0, 1), (1, 0))

            def transposes(n):
                for t in range(NT):
                    pe.wait_ge(xn_ready, NT * n + t + 1)
                    if t >= 2:
                        pe.wait_ge(xl_ready, NT * n + t - 1)
                    if n == 1 and t < 2:
                        pe.wait_ge(x1_ready, t + 1)
                    for k in range(KD):
                        ins = pe.transpose(PS[:, t % 2, k * P:(k + 1) * P], xn[:, t % 2, k * P:(k + 1) * P], ident[:])
                    ins.then_inc(xt_ready, 1)

            pe.wait_ge(ident_ready, 1)
            transposes(0)

            def qkv(half, u):
                tok = slice(half * HALF, (half + 1) * HALF)
                if half == 0 and u == 0:
                    pe.wait_ge(xl_ready, NT)
                if half or u >= 2:
                    if half and u == 1:
                        pe.wait_ge(v_ready, 1)
                    else:
                        pe.wait_ge(proj_ready, 5 * half + max(u - 1, 0))
                if half == 0 and u in (0, 2, 4):
                    pe.wait_ge(split_done, u // 2 + 1)
                if u < 5:
                    products(PS[:, u % 2, :], ((wqkv[:, a, k, u * P:(u + 1) * P], xnT[:, b, k, tok])
                                               for k in range(KD) for a, b in PARTS)).then_inc(qkv_ready, 1)
                else:
                    for q in range(4):
                        t = slice((4 * half + q) * P, (4 * half + q + 1) * P)
                        ins = products(PS[:, 1, q * P:(q + 1) * P], ((xnT[:, b, k, t], wqkv[:, a, k, 640:768])
                                                                    for k in range(KD) for a, b in PARTS))
                    ins.then_inc(qkv_ready, 1)

            K1 = 6 * DH
            K2 = K1 + 4

            def score_max(b, unit):
                m, gp, buf = unit // 2, unit % 2, b % 2
                if unit == 0:
                    pe.wait_ge(qs_loaded[buf], 192 * (b // 2 + 1))
                    if b:
                        pe.wait_ge(ml_ready, b)
                    if b == 0:
                        pe.wait_ge(consts_ready, 1)
                if 8 * b + unit:
                    pe.wait_ge(max_ready, 8 * b + unit)
                pe.matmul(PS[:, 2, :], identb[:], maskA[:].rearrange("p g k -> p (g k)"), start=True, stop=False)
                for g in range(2):
                    pe.matmul(PS[:, 2, 256 * g:256 * (g + 1)], qs[0:K1, buf, m, 2 * gp + g, 0:P], ks[0:K1, buf, :, m, 0:P],
                              start=False, stop=g == 1)
                for g in range(2):
                    pe.matmul(PS[:, 3 + g, :].rearrange("p (j k) -> p j k", j=2)[:, :, P:SEQ], identb[:], maskA[:, 0:2, :],
                              start=True, stop=False, skip_group_check=True)
                    ins = pe.matmul(PS[:, 3 + g, :], qs[0:K1, buf, m, 2 * gp + g, P:SEQ], ks[0:K1, buf, :, m, :],
                                    start=False, stop=True, skip_group_check=True)
                ins.then_inc(s1_ready, 1)

            def max_transposed(b):
                pe.wait_ge(max_ready, 8 * (b + 1))
                for qt in range(2):
                    ins = pe.transpose(PS[0:32, 2, qt * P:(qt + 1) * P], negmax[:, b, qt, :], ident[:])
                ins.then_inc(mt_ready, 1)

            TILES = ((0, 0), (0, 1), (1, 1))

            def scores(G, kv):
                b, quad, (kt, qt) = G // 6, G // 3 % 2, TILES[G % 3]
                m, j, buf, n = 2 * quad + kv // 2, kv % 2, b % 2, 4 * G + kv
                if G % 6 == 0 and kv == 0:
                    pe.wait_ge(m_loaded[buf], 16 * (b // 2 + 1))
                if n < 2:
                    pe.wait_ge((proj_ready, v_ready)[n], (10, 2)[n])
                else:
                    pe.wait_ge(exp_ready, n - 1)
                pe.matmul(PS[:, n % 2, :], ks[0:K2, buf, j, m, kt * P:(kt + 1) * P],
                          qs[0:K2, buf, m, :, qt * P:(qt + 1) * P], start=True, stop=True).then_inc(s2_ready, 1)

            def values(G):
                b, quad, c = G // 6, G // 3 % 2, G % 3
                kt, qt = TILES[c]
                if c < 2:
                    if G >= 3:
                        pe.wait_ge(ot_ready, 2 * (G // 3) - 1 + c)
                    if G % 6 < 3 and b:
                        pe.wait_ge(al_ready, 2 * b - 1 + c)
                for kv in range(4):
                    n = 4 * G + kv
                    if c == 1:
                        pe.wait_ge(exp_ready, n + 1)
                    else:
                        pe.wait_ge(masked, 8 * (G // 3) + 4 * (c // 2) + kv + 1)
                    ins = pe.matmul(PS[32 * kv:32 * kv + 32, 5 + qt, :], v_sb[:, 2 * b + kt, 4 * quad + kv, :], probs[:, n % 8, :],
                                    start=c < 2, stop=c != 1)
                ins.then_inc(pv_ready, 1)

            def tokens_back(b, quad):
                for qt in range(2):
                    n = 4 * b + 2 * quad + qt
                    pe.wait_ge(ot_ready, n + 1)
                    if n:
                        pe.wait_ge(att_ready, n)
                    if quad == 0 and b and qt == 0:
                        pe.wait_ge(s_ready, 2 * b)
                    for g in range(GRP):
                        ins = pe.transpose(PS[:, 7, g * P:(g + 1) * P], outT[:, qt, g * P:(g + 1) * P], ident[:])
                    ins.then_inc(tt_ready, 1)

            def project_out(b):
                pe.wait_ge(att_ready, 4 * b + 4)
                for qt in range(2):
                    for k in range(KD):
                        ins = pe.transpose(PS[:, 5 + qt, k * P:(k + 1) * P], att_tok[:, qt, k * P:(k + 1) * P], ident[:])
                    ins.then_inc(at_ready, 1)
                for qt in range(2):
                    t = 2 * b + qt
                    pe.wait_ge(al_ready, t + 1)
                    if b == 0:
                        pe.wait_ge(split_done, 5)
                    if qt:
                        pe.wait_ge(s_ready, t)
                    ins = products(PS[:, 7, :], ((attT[:, qt, a, k, :], ring[:, k // 2, w, (k % 2) * D:(k % 2 + 1) * D])
                                                 for k in range(KD) for a, w in PARTS))
                    ins.then_inc(wo_ready, 1)

            for u in range(6):
                qkv(0, u)
            for u in range(3):
                qkv(1, u)
            for unit in range(8):
                score_max(0, unit)
                if unit in (1, 3, 5):
                    qkv(1, 3 + unit // 2)
            max_transposed(0)
            for kv in range(4):
                scores(0, kv)
            for b in range(4):
                for g in range(6):
                    G = 6 * b + g
                    for kv in range(4):
                        if g < 5:
                            scores(G + 1, kv)
                        if b < 3 and g < 4 and kv % 2 == 0:
                            score_max(b + 1, 2 * g + kv // 2)
                    values(G)
                    if g == 3:
                        tokens_back(b, 0)
                    if b < 3 and g == 4:
                        max_transposed(b + 1)
                if b < 3:
                    for kv in range(4):
                        scores(G + 1, kv)
                tokens_back(b, 1)
                project_out(b)

            used = [2]

            def next_chunk(kind, index, half=0):
                c, rc = chunk_place(kind, index, half)
                assert rc == used[0], (kind, index, rc, used)
                used[0] += 1
                pe.wait_ge(split_done, c + 1)
                return ring[:, rc % N_RING, :, :]

            pe.wait_ge(al_ready, NT)
            pe.wait_ge(s_ready, NT)
            for i in range(NF):
                w = next_chunk("gu0", i)
                fw = FW[i]
                for half in range(2):
                    job = 2 * i + half
                    tok = slice(half * HALF, (half + 1) * HALF)
                    if job >= 3:
                        pe.wait_ge(up_used, job - 2)
                    for o in range(2):
                        g0 = 4 * fw * o
                        ins = products(PS[0:fw, 2 + 2 * (job % 3) + o, :],
                                       ((w[:, a, g0 + k * fw:g0 + (k + 1) * fw], xnT[:, b, k, tok])
                                        for k in range(KD) for a, b in PARTS))
                    ins.then_inc(gu_ready, 1)
            pe.wait_ge(up_used, 2 * NF)
            pe.wait_ge(s_ready, NT)
            for i in range(6):
                w = next_chunk("dn0", i)
                for kk in range(2 if i < 5 else 1):
                    k = 2 * i + kk
                    fw = FW[k]
                    pe.wait_ge(hid_ready, 2 * k + 2)
                    for t in range(NT):
                        for n, (a, b) in enumerate(PARTS):
                            ins = pe.matmul(PS[:, t, :], hid0[0:fw, a, k, t * P:(t + 1) * P], w[0:fw, b, kk * D:(kk + 1) * D],
                                            start=k == 0 and n == 0, stop=k == NF - 1 and n == 2)
                        if k == NF - 1:
                            ins.then_inc(dn_ready, 1)
                if i < 5:
                    ins.then_inc(chunk_used, 1)
            transposes(1)

            pe.wait_ge(xl_ready, 2 * NT)
            pe.wait_ge(g_ready, NT)
            pe.wait_ge(split_done, 23)
            products(PS[:, 2, :], ((win_hl[:, a, k, (CH, 0)[half]:(CH, 0)[half] + P], xnT[:, b, k, half * HALF:(half + 1) * HALF])
                                   for half in range(2) for k in range(KD) for a, b in PARTS)).then_inc(win_ready, 1)

            def model(n):
                l, step = SSM_STEPS[n]
                nth = 2 * l + (step[-1] == "2")
                if step in ("mean1", "mean2"):
                    if nth == 0:
                        pe.wait_ge(h0_ready, 1)
                        pe.wait_ge(late_consts, 1)
                    else:
                        pe.wait_ge(h_ready, nth)
                    pe.matmul(PS[:, 0, :], bd[:], h[:], start=True, stop=True).then_inc(ln_mean, 1)
                elif step in ("var1", "var2"):
                    pe.wait_ge(ln_sq, nth + 1)
                    for c in range(4):
                        ins = pe.matmul(PS[:, 1, 2 * c:2 * c + 2], tmp1[:, c * P:(c + 1) * P], bdc[:], start=True, stop=True)
                    ins.then_inc(ln_var, 1)
                elif step in ("rstd1", "rstd2"):
                    pe.wait_ge(ln_spread, nth + 1)
                    for c in range(4):
                        ins = pe.transpose(PS[:, 0, c * P:(c + 1) * P], tmp1[:, c * P:(c + 1) * P], ident[:])
                    ins.then_inc(ln_rstd, 1)
                elif step == "sel":
                    pe.wait_ge(ln_out, nth + 1)
                    for j in range(2):
                        ins = pe.matmul(PS[:, j, :], sel[:, j, :], act1[:], start=True, stop=True)
                    ins.then_inc(cv_sel, 1)
                elif step == "comb":
                    pe.wait_ge(cv_mod, l + 1)
                    products(PS[:, 0, :], ((comb[:, j, :], dz[:, j, :]) for j in range(2))).then_inc(cv_comb, 1)
                elif step in ("w1a", "w1b"):
                    ft = int(step == "w1b")
                    pe.wait_ge(late_loaded, 48)
                    pe.wait_ge(ln_out, 2 * l + 2)
                    if ft:
                        pe.wait_ge(w1_act, 2 * l + 1)
                    for half in range(2):
                        r = slice(CH * half, CH * half + CH)
                        ins = pe.matmul(PS[:, half, :], w1v[r, l, ft * P:(ft + 1) * P], act1[r, :], start=True, stop=True)
                    ins.then_inc(w1_ready, 1)
                elif step == "w2":
                    pe.wait_ge(w1_act, 2 * l + 2)
                    for half in range(2):
                        r = slice(CH * half, CH * half + CH)
                        ins = products(PS[r, 0, :], ((w2v[:, l, ft, :], sv[:, ft, half, :]) for ft in range(2)))
                    ins.then_inc(w2_ready, 1)

            cur = [None]
            for kind, a, i in ORDER1:
                J = NF * a + i
                tok = slice(a * HALF, (a + 1) * HALF)
                if kind == "lowrank":
                    w = next_chunk("lra", 0)
                    for o in range(4):
                        g0 = LRR * KD * (o // 2)
                        ins = products(PS[0:LRR, 3 + o, :], ((w[:, p, g0 + k * LRR:g0 + (k + 1) * LRR],
                                                        xnT[:, q, k, (o % 2) * HALF:(o % 2 + 1) * HALF])
                                                       for k in range(KD) for p, q in PARTS))
                        ins.then_inc(lr_ready, 1)
                    pe.wait_ge(lr_copied, 4)
                    pe.wait_ge(lr_split, 4)
                    pe.wait_ge(h0_ready, 1)
                elif kind in ("gate", "up"):
                    o = int(kind == "up")
                    fw = FW[i]
                    if o == 0:
                        cur[0] = next_chunk("gu1", i, a)
                        if J >= 2:
                            pe.wait_ge(up_used, 2 * NF + J - 1)
                        if a and i < 2:
                            pe.wait_ge(fsum_ready, 4)
                    w = cur[0]
                    g0 = 4 * fw * o
                    products(PS[0:fw, 2 + 2 * (J % 2) + o, :], ((w[:, 0, g0 + k * fw:g0 + (k + 1) * fw], xnT[:, q, k, tok])
                                                                for k in range(KD) for q in range(2)))
                    if o == 0 and J:
                        pe.wait_ge(lr_copied, 4 + J)
                    ins = pe.matmul(PS[0:fw, 6 + o, :], w[0:LRR, 1, o * fw:(o + 1) * fw], lrx[:, o, tok], start=True, stop=True)
                    if o:
                        ins.then_inc(gu_ready, 1)
                elif kind == "ssm":
                    model(a)
                elif kind == "rd":
                    w = next_chunk("lrd", 0, a)
                    pe.wait_ge(lr_copied, 4 + NF * (a + 1))
                    n = 0
                    for k in range(NF):
                        pe.wait_ge(hid_ready, 2 * NF + NF * a + k + 1)
                        for p, q in PARTS:
                            ins = pe.matmul(PS[0:LRR, 6, :], w[0:FW[k], p, k * LRR:(k + 1) * LRR], hid1[0:FW[k], q, k, :],
                                            start=n == 0, stop=n == 3 * NF - 1)
                            n += 1
                    ins.then_inc(rd_ready, 1)
                elif kind == "dn":
                    w = next_chunk("dn1", i, a)
                    if i == 0:
                        pe.wait_ge(up_used, 2 * NF + NF * (a + 1))
                    for kk in range(2 if i < 5 else 1):
                        k = 2 * i + kk
                        fw = FW[k]
                        for t in range(4):
                            for p in range(2):
                                ins = pe.matmul(PS[:, 2 + t, :], hid1[0:fw, p, k, t * P:(t + 1) * P], w[0:fw, 0, kk * D:(kk + 1) * D],
                                                start=k == 0 and p == 0, stop=k == NF - 1 and p == 1)
                            if k == NF - 1:
                                ins.then_inc(dn_ready, 1)
                    if i < 5:
                        ins.then_inc(chunk_used, 1)
                elif kind == "wout":
                    for t in range(NT):
                        half = t // 4
                        r = slice(CH * half, CH * half + CH)
                        if t == 0:
                            pe.wait_ge(ln_out, 2 * DEPTH + 1)
                        if t >= 2:
                            pe.wait_ge(s_ready, NT + t - 1)
                        pe.matmul(PS[:, t % 2, :], act1[r, (t % 4) * P:(t % 4 + 1) * P], wov[r, :], start=True, stop=True)\
                          .then_inc(wout_ready, 1)
                elif kind == "fin":
                    pe.wait_ge(split_done, chunk_place("lrb", 0, a)[0] + 1)
                    pe.wait_ge(rd_split, a + 1)
                    for t in range(4):
                        if t >= 2:
                            pe.wait_ge(fsum_ready, 4 * a + t - 1)
                        pe.matmul(PS[:, 6 + t % 2, :], lrh[:, t * P:(t + 1) * P], lrdb[:], start=True, stop=True)\
                          .then_inc(lrd_ready, 1)


_NEEDED = ("x", "wq", "wk", "wv", "wo", "gu0", "dn0", "winT", "lra", "gu1", "lrb", "lrd", "lrdb", "dn1", "cols", "bv", "bo",
           "bout", "dscale", "ssmw")


def packed_gate_up(gate, up, np):
    blocks = []
    for i in range(NF):
        o = slice(i * P, i * P + FW[i])
        for w in (gate, up):
            blocks.append(w[o, :].T.reshape(KD, P, FW[i]).transpose(1, 0, 2).reshape(P, KD * FW[i]))
    return np.ascontiguousarray(np.concatenate(blocks, axis=1))


def kernel(**inputs):
    import numpy as np
    import concourse.bacc as bacc
    from concourse.bass_utils import run_bass_kernel_spmd

    v = {k: np.asarray(a) for k, a in inputs.items()}
    l0 = {k[3:]: a for k, a in v.items() if k.startswith("L0_")}
    l1 = {k[3:]: a for k, a in v.items() if k.startswith("L1_")}
    twice = lambda a: np.concatenate([a, a], axis=0)
    at = lambda n: l1["attn_" + n]

    def tiles(a):
        return np.concatenate([a, a[:NF * P - F]]).reshape(NF, P).T

    by_pair = lambda a, g: a.reshape(a.shape[0], 4, 2, g * DH).transpose(0, 2, 1, 3).reshape(a.shape)
    columns = {
        "bq": by_pair(l0["attn_bq"][None], GRP).reshape(4, P).T, "bk": by_pair(l0["attn_bk"][None], 1).reshape(P, 1),
        "ln1_w": twice(at("ln1_w").T), "ln1_b": twice(at("ln1_b").T), "scl": twice(at("sc_lin").T),
        "ln2_w": twice(at("ln2_w").T), "ln2_b": twice(at("ln2_b").T), "b2": twice(at("b2").T),
        "b1": at("b1").reshape(DEPTH * 2, P).T,
        "lnl_w": twice(at("lnl_w").reshape(CH, 1)), "lnl_b": twice(at("lnl_b").reshape(CH, 1)),
        "bin": twice(at("bin").reshape(CH, 1)),
        "lc_a": np.concatenate([at("lc_re").T, at("lc_im").T]), "lc_b": np.concatenate([at("lc_im").T, at("lc_re").T]),
        "ph_re": twice(at("phz_re").T), "ph_im": twice(at("phz_im").T),
        "gate_s": tiles(l1["ffn_gate_scale"]), "up_s": tiles(l1["ffn_up_scale"]),
    }
    w1 = twice(at("W1").transpose(2, 0, 1).reshape(CH, DEPTH * 256))
    w2 = at("W2").reshape(DEPTH, CH, 2, P).transpose(3, 0, 2, 1).reshape(P, DEPTH * 2 * CH)
    low_rank = lambda a: np.concatenate([a, a, a], axis=1)
    lra = np.concatenate([low_rank(l1[n]).reshape(KD, P, LRR).transpose(1, 0, 2).reshape(P, KD * LRR)
                          for n in ("ffn_gate_A", "ffn_up_A")], axis=1)
    b_blocks = []
    for i in range(NF):
        for n in ("ffn_gate_B", "ffn_up_B"):
            b_blocks.append(l1[n][:, i * P:i * P + FW[i]])
    lrb = np.concatenate(b_blocks, axis=1)
    down_a = low_rank(l1["ffn_down_A"])
    down_a = np.concatenate([down_a, down_a[:NF * P - F]])
    arrays = {
        "x": l0["attn_x"].reshape(TOK, D), "wq": by_pair(l0["attn_Wq"], GRP), "wk": by_pair(l0["attn_Wk"], 1), "wv": l0["attn_Wv"], "wo": l0["attn_Wo"],
        "gu0": packed_gate_up(l0["ffn_W_gate"], l0["ffn_W_up"], np), "dn0": l0["ffn_W_down"].T,
        "winT": at("Win").T, "lra": lra, "gu1": packed_gate_up(l1["ffn_gate_q"], l1["ffn_up_q"], np),
        "lrb": np.concatenate([lrb, lrb, lrb]), "lrd": down_a.reshape(NF, P, LRR).transpose(1, 0, 2).reshape(P, NF * LRR),
        "lrdb": np.concatenate([l1["ffn_down_B"]] * 3), "dn1": l1["ffn_down_q"].T,
        "cols": np.concatenate([columns[n] for n in COLS], axis=1),
        "bv": l0["attn_bv"].reshape(1, P), "bo": l0["attn_bo"].reshape(1, D), "bout": at("bout").reshape(1, D),
        "dscale": l1["ffn_down_scale"].reshape(1, D),
        "ssmw": np.concatenate([w1, w2, twice(at("Wout").T)], axis=1),
    }
    arrays = {n: np.ascontiguousarray(arrays[n]) for n in _NEEDED}
    nc = bacc.Bacc("TRN2", target_bir_lowering=False, num_devices=1)
    A = {n: nc.dram_tensor("in_" + n, a.shape, mybir.dt.from_np(a.dtype), kind="ExternalInput").ap()
         for n, a in arrays.items()}
    A["out"] = nc.dram_tensor("out", (TOK, D), F32, kind="ExternalOutput").ap()
    build(nc, A)
    r = run_bass_kernel_spmd(nc, [{"in_" + n: a for n, a in arrays.items()}], core_ids=[0])
    return r.results[0]["out"].reshape(4, SEQ, D)
```

```python
from contextlib import ExitStack

import concourse.bass as bass
from concourse import mybir

F32 = mybir.dt.float32
F32R = mybir.dt.float32r
BF16 = mybir.dt.bfloat16
I32 = mybir.dt.int32
ALU = mybir.AluOpType
ACT = mybir.ActivationFunctionType
AX_X = mybir.AxisListType.X

P = 128
TOK = 1024
SEQ = 256
D = 512
KD = D // P
NT = TOK // P
HALF = 512
NKV = 8
GRP = 4
DH = 16
F = 1376
NF = 11
FW = [P] * (NF - 1) + [F - (NF - 1) * P]
DEPTH = 4
CH = 64
RANK = 32
LRR = 3 * RANK
SW = 1312
RW = 1056
EPS = 1e-5
MASKED = -1e30

COLS = {}
_at = 0
for _name, _n in (("bq", 4), ("bk", 1), ("ln1_w", 4), ("ln1_b", 4), ("scl", 4), ("ln2_w", 4), ("ln2_b", 4),
                  ("b2", 4), ("b1", 8), ("lnl_w", 1), ("lnl_b", 1), ("bin", 1), ("lc_a", 4), ("lc_b", 4),
                  ("ph_re", 4), ("ph_im", 4), ("gate_s", NF), ("up_s", NF)):
    COLS[_name] = (_at, _at + _n)
    _at += _n
NCOLS = _at


def weight_chunks():
    chunks = [("qkv", 0), ("qkv", 1), ("qkv", 2)] + [("gu0", i) for i in range(NF)]
    chunks += [("wo", 0), ("wo", 1)] + [("dn0", i) for i in range(6)]
    chunks += [("win", 0), ("lra", 0)]
    for _ in range(2):
        chunks += [("gu1", i) for i in range(NF)] + [("lrd", 0), ("lrb", 0)] + [("dn1", i) for i in range(6)]
    return chunks


CHUNKS = weight_chunks()
GU0, WO, DN0, WIN, LRA, GU1 = (CHUNKS.index((kind, 0)) for kind in ("gu0", "wo", "dn0", "win", "lra", "gu1"))
IN_RING = ("gu0", "dn0", "gu1", "lrd", "dn1")
N_STAGE = 2
N_RING = 2
LN_BANK = (2, 0)
LR_BANK = (3, 5, 1, 1)
N_HID = 5


def chunk_place(kind, index, half=0):
    seen = -1
    ring = 0
    for c, (k, i) in enumerate(CHUNKS):
        if (k, i) == (kind, index):
            seen += 1
            if seen == half:
                return c, ring
        ring += k in IN_RING
    raise ValueError(kind)


def stage_value(c):
    return 16 * sum(2 if k == "gu1" or (k, i) == ("qkv", 2) else 1 for k, i in CHUNKS[c % N_STAGE:c + 1:N_STAGE])


def hi_value(c):
    return sum(k not in ("win", "lrb") for k, _ in CHUNKS[:c + 1])


def lo_value(c):
    return sum(k != "dn1" for k, _ in CHUNKS[:c + 1])


def attention_order():
    order = [("tr", t, 0) for t in range(4)] + [("qkv", 0, 0), ("tr", 4, 0), ("tr", 5, 0)]
    order += [("qkv", 0, 1), ("tr", 6, 0), ("tr", 7, 0)] + [("qkv", 0, u) for u in range(2, 6)]
    pieces = [("ffn", job, piece) for job in range(2 * NF) for piece in range(4)]

    def feed(n):
        order.extend(pieces[:n])
        del pieces[:n]

    for u in range(6):
        order.append(("qkv", 1, u))
        feed(2)
    for i in range(24):
        order.append(("max", 0, i))
        if i % 3 == 2:
            feed(1)
    order.append(("maxT", 0, 0))
    feed(4)
    order.extend(("scores", 0, kv) for kv in range(4))
    main = len(pieces) - AFTER
    fed = 0
    for G in range(24):
        b, g = G // 6, G % 6
        items = []
        if g % 3 == 0 and G:
            items += [("back", G // 3 - 1, qt) for qt in range(2)]
        if b < 3 and 1 <= g < 4:
            items += [("max", b + 1, 8 * (g - 1) + i) for i in range(8)]
        if b < 3 and g == 4:
            items.append(("maxT", b + 1, 0))
        if g == 5:
            feed(2)
            fed += 2
        for kv in range(4):
            if G < 23:
                order.append(("scores", G + 1, kv))
            n = max(main * (4 * G + kv + 1) // 96 - fed, 0)
            feed(n)
            fed += n
            order.extend(items[:3])
            del items[:3]
        order.append(("values", G, 0))
    feed(4)
    order.extend(("back", 7, qt) for qt in range(2))
    feed(len(pieces))
    return order


AFTER = 8
ATT = attention_order()
TURNS = [s for s in ATT if s[0] in ("max", "maxT", "back")]


SSM_STEPS = [(l, s, c) for l in range(DEPTH) for s in
             ("cen1", "var1", "rstd1", "sel", "comb", "cen2", "var2", "rstd2", "w1a", "w1b", "w2") for c in range(2)]
SSM_STEPS += [(DEPTH, s, c) for s in ("cen1", "var1", "rstd1") for c in range(2)]


def layer1_order():
    tr = lambda *tiles: [("tr", t, 0) for t in tiles]
    down = lambda *tiles: [("dl", t, 0) for t in tiles]
    order = down(0, 1, 2, 3, 4) + tr(0, 1) + down(5) + tr(2, 3) + down(6, 7)
    order += [("lr", 0, 0), ("lr", 0, 1)] + tr(4, 5) + [("gate", 0, 0), ("up", 0, 0)] + tr(6, 7)
    order += [("gate", 0, 1), ("win", 0, 0), ("lr", 1, 0), ("up", 0, 1), ("lr", 1, 1)]
    fill = []
    for half in range(2):
        for i in range(0 if half else 2, NF):
            fill += [("gate", half, i), ("up", half, i)]
        fill += [("rd", half, i) for i in range(4)] + [("dn", half, k) for k in range(8 if half else NF)]
        if half == 0:
            fill += [("fin", half, t) for t in range(4)]
    steps = list(range(len(SSM_STEPS)))
    out_tiles = list(range(NT))
    now, ready = 0.0, [0.0, 0.0]
    while fill or steps:
        chain = steps[0] % 2 if steps else 0
        if steps and (ready[chain] <= now or not fill):
            held, after = MODEL_LENGTHS[SSM_STEPS[steps[0]][1]]
            order.append(("ssm", steps.pop(0), 0))
            now += held
            ready[chain] = now + after + MARGIN
        else:
            order.append(fill.pop(0))
            now += FILL_LENGTHS[order[-1][0]]
            if not steps and ("fin", 0, 3) in order and out_tiles:
                order.append(("wout", out_tiles.pop(0), 0))
    order += [("wout", t, 0) for t in out_tiles]
    order += [("end", 1, t) for t in range(4)]
    out, due = [], []
    for step in order:
        due = [(n - 1, what) for n, what in due]
        while due and (due[0][0] <= 0 or step[0] == "rd" and step[2] == 3):
            out.append(due.pop(0)[1])
        out.append(step)
        if step[0] == "up":
            due += [(n, (what,) + step[1:]) for n, what in AFTER_UP]
        elif step[0] == "ssm" and SSM_STEPS[step[1]][1] in ("var1", "var2"):
            due.append((2, ("spread", step[1], 0)))
        due.sort(key=lambda x: x[0])
    return out


MODEL_LENGTHS = {"cen1": (.5, .5), "var1": (.2, 1.9), "rstd1": (.3, 1.3), "sel": (1.0, 5.5), "comb": (1.0, .6),
               "cen2": (.5, .5), "var2": (.2, 1.9), "rstd2": (.3, 1.3), "w1a": (1.0, 1.1), "w1b": (1.0, 1.1),
               "w2": (2.0, .6)}
MARGIN = 0.45
AFTER_UP = ((1, "copies"), (2, "sums"), (3, "silu"), (4, "hidden"))
FILL_LENGTHS = {"gate": 1.9, "up": 1.9, "rd": 1.8, "dn": 1.7, "fin": 1.3}
ORDER1 = layer1_order()


def ahead_of(order):
    c = GU1 + 1
    for kind, a, i in order:
        yield None, (kind, a, i)
        chunks = {"gate": 1, "rd": (2, 0, 0, 1)[i % 4], "dn": i % 2 == 1}.get(kind, 0)
        for _ in range(chunks):
            yield c, (kind, a, i)
            c += 1
    assert c == len(CHUNKS)


def build(nc, A):
    ctx = ExitStack()
    with ctx:
        def common(name, shape, dt=F32):
            return ctx.enter_context(nc.sbuf_tensor(name, shape, dt))

        def sem(name):
            return ctx.enter_context(nc.semaphore(name))

        xnT = common("xnT", [P, 2, KD, TOK], F32R)
        stage = common("stage", [P, N_STAGE, SW])
        ring = common("ring", [P, N_RING, 2, RW], F32R)
        xn = common("xn", [P, 2, D])
        ident = common("ident", [P, P])
        cols = common("cols", [P, NCOLS])
        row_b = common("row_b", [P, D])
        bn6 = common("bn6", [P, NT, 6])
        mv = common("mv", [P, NT, 2])
        ve = common("ve", [P, NT])
        rstd = common("rstd", [P, NT])
        cs = common("cs", [P, 12, DEPTH])
        trig = common("trig", [P, 8, 2, DEPTH])
        decay = common("decay", [P, DEPTH])
        start = common("start", [P, DEPTH])
        nhalf = common("nhalf", [P, 8])
        PS = ctx.enter_context(nc.psum_tensor("PS", [P, 8, 512], F32))

        sg0 = common("sg0", [P, 2, HALF])
        with ExitStack() as scope:
            def early(name, shape, dt=F32):
                return scope.enter_context(nc.sbuf_tensor(name, shape, dt))

            wqkv = early("wqkv", [P, 2, KD, 768], F32R)
            proj = early("proj", [P, HALF])
            proj_hl = early("proj_hl", [P, 2, 2, HALF], F32R)
            bv_b = early("bv_b", [P, P])
            bq4 = early("bq4", [P, 4])
            x0 = early("x0", [P, NT, D])
        s_sb = common("s_sb", [P, NT, D])
        with ExitStack() as scope:
            def att(name, shape, dt=F32):
                return scope.enter_context(nc.sbuf_tensor(name, shape, dt))

            hidf = att("hidf", [P, 2 * NF, HALF])
            probs = att("probs", [P, 8, GRP * P])
            qs = att("qs", [P, 2, 4, GRP, SEQ], F32R)
            ks = att("ks", [P, 2, 2, 4, SEQ], F32R)
            v_sb = att("v_sb", [P, NT, NKV, 2 * DH])
            max_hl = att("max_hl", [32, 2, SEQ], F32R)
            negmax = att("negmax", [P, 4, 2, 32])
            maskA = att("maskA", [P, 4, P], BF16)
            identb = att("identb", [P, P], BF16)
            rden = att("rden", [P, 2, 16])
            outT = xn
        def late(name, shape, dt=F32):
            return ctx.enter_context(nc.sbuf_tensor(name, shape, dt))

        hid1 = late("hid1", [P, 2, NF, HALF], F32R)
        x = late("x_sb", [P, NT, D])
        rot = late("rot", [P, DEPTH, SEQ])
        win_hl = late("win_hl", [P, 2, KD, 3 * CH], F32R)
        with ExitStack() as scope:
            def ff0(name, shape, dt=F32):
                return scope.enter_context(nc.sbuf_tensor(name, shape, dt))

            hid0 = ff0("hid0", [P, N_HID, 2, TOK], F32R)
            ht0 = ff0("ht0", [P, 4, HALF])
            rotb = ff0("rotb", [P, DEPTH, SEQ // 2])
            rtmp = ht0[:, 2:4, :].rearrange("p a (l t) -> p a l t", l=DEPTH)
        wo_hl = hid0[:, 1:3, :, :].rearrange("p s a (k n) -> p s a k n", k=2)
        attT = hid0[:, 3:5, :, 0:KD * P].rearrange("p t a (k q) -> p t a k q", k=KD)
        lra_hl = hid1[:, 1, 7:10, :].rearrange("p s (h n) -> p (s h) n", h=2).rearrange("p (a s) n -> p a (s n)", a=2)
        lrx = late("lrx", [LRR, 2, TOK], F32R)
        lrh = late("lrh", [LRR, HALF], F32R)
        lrdb = late("lrdb", [LRR, D], F32R)
        dscale_b = late("dscale_b", [P, D])
        ssmw = late("ssmw", [P, DEPTH * 512 + DEPTH * 2 * CH + D])
        gs = late("gs", [P, 2, NF])
        e_lr = sg0
        e_gu = late("e_gu", [P, 2, HALF])
        h = late("h", [P, HALF])
        tmp1 = late("tmp1", [P, HALF])
        act1 = late("act1", [P, HALF])
        dz = late("dz", [P, 2, HALF])
        sv = late("sv", [P, 2, 2, HALF])
        tstat = late("tstat", [P, 2, 4])
        trs = late("trs", [P, 2, 4])
        sel = late("sel", [P, 2, P])
        comb = late("comb", [P, 2, P])
        center = late("center", [P, P])
        bdc = late("bdc", [P, 2])

        w1v = ssmw[:, 0:DEPTH * 512].rearrange("p (l h f) -> p l h f", l=DEPTH, h=2)
        w2v = ssmw[:, DEPTH * 512:DEPTH * 512 + DEPTH * 2 * CH].rearrange("p (l t c) -> p l t c", l=DEPTH, t=2)
        wov = ssmw[:, DEPTH * 512 + DEPTH * 2 * CH:]

        def col(name, i=0, n=1):
            return cols[:, COLS[name][0] + i:COLS[name][0] + i + n]

        q_bounce = nc.dram_tensor("q_bounce", [2, 3, DH, 4 * GRP, TOK], F32).ap()
        k_bounce = nc.dram_tensor("k_bounce", [2, 3, DH, 4, TOK], F32).ap()
        m_bounce = nc.dram_tensor("m_bounce", [4, 2, 2, 16, SEQ], F32).ap()

        x_loaded = [sem(f"x_loaded{t}") for t in range(NT)]
        cols_loaded = sem("cols_loaded")
        bv_loaded = sem("bv_loaded")
        bq_ready = sem("bq_ready")
        bo_loaded = sem("bo_loaded")
        late_loaded = sem("late_loaded")
        stage_loaded = [sem(f"stage_loaded{i}") for i in range(N_STAGE)]
        hi_done = sem("hi_done")
        lo_done = sem("lo_done")
        x_back = sem("x_back")
        chunk_used = sem("chunk_used")
        ident_ready = sem("ident_ready")
        consts_ready = sem("consts_ready")
        var_ready = sem("var_ready")
        rstd_ready = sem("rstd_ready")
        xn_ready = sem("xn_ready")
        xt_ready = sem("xt_ready")
        xh_ready = sem("xh_ready")
        xl_ready = sem("xl_ready")
        qkv_ready = sem("qkv_ready")
        proj_ready = sem("proj_ready")
        proj_split = sem("proj_split")
        v_ready = sem("v_ready")
        q_out = [sem(f"q_out{i}") for i in range(2)]
        qs_loaded = [sem(f"qs_loaded{i}") for i in range(2)]
        turn_ready = sem("turn_ready")
        turn_read = sem("turn_read")
        mh_ready = sem("mh_ready")
        ks_zeroed = sem("ks_zeroed")
        m_out = sem("m_out")
        m_loaded = [sem(f"m_loaded{i}") for i in range(2)]
        s2_ready = sem("s2_ready")
        exp_ready = sem("exp_ready")
        masked = sem("masked")
        pv_ready = sem("pv_ready")
        ot_ready = sem("ot_ready")
        at_ready = sem("at_ready")
        ah_ready = sem("ah_ready")
        al_ready = sem("al_ready")
        wo_ready = sem("wo_ready")
        s_ready = sem("s_ready")
        gu_ready = sem("gu_ready")
        tanh_ready = sem("tanh_ready")
        gate_used = sem("gate_used")
        up_used = sem("up_used")
        hid_ready = sem("hid_ready")
        hid_used = sem("hid_used")
        dn_ready = sem("dn_ready")
        g_ready = sem("g_ready")
        gs_ready = sem("gs_ready")
        x1_ready = sem("x1_ready")
        lr_ready = sem("lr_ready")
        lr_inner = sem("lr_inner")
        lr_copied = sem("lr_copied")
        lr_split = sem("lr_split")
        phasor_scaled = sem("phasor_scaled")
        polar_ready = sem("polar_ready")
        decay_ready = sem("decay_ready")
        rot_ready = sem("rot_ready")
        late_consts = sem("late_consts")
        gsum_ready = sem("gsum_ready")
        silu_ready = sem("silu_ready")
        fsum_ready = sem("fsum_ready")
        fg_ready = sem("fg_ready")
        rd_ready = sem("rd_ready")
        rd_copied = sem("rd_copied")
        rd_split = sem("rd_split")
        h0_ready = sem("h0_ready")
        h_ready = sem("h_ready")
        ln_cen = sem("ln_cen")
        ln_sq = sem("ln_sq")
        ln_copied = sem("ln_copied")
        ln_var = sem("ln_var")
        ln_stat = sem("ln_stat")
        ln_pow = sem("ln_pow")
        ln_spread = sem("ln_spread")
        ln_rstd = sem("ln_rstd")
        ln_norm = sem("ln_norm")
        ln_out = sem("ln_out")
        cv_sel = sem("cv_sel")
        cv_mod = sem("cv_mod")
        cv_comb = sem("cv_comb")
        w1_ready = sem("w1_ready")
        w1_act = sem("w1_act")
        w2_ready = sem("w2_ready")
        lrd_ready = sem("lrd_ready")
        win_ready = sem("win_ready")
        wout_ready = sem("wout_ready")
        out_ready = sem("out_ready")
        stored = sem("stored")
        dve_chain = sem("dve_chain")
        pool_chain = sem("pool_chain")
        act_chain = sem("act_chain")

        def out_value(n):
            return 16 * sum(6 if x % 5 == 4 else 3 for x in range(n % 2, n + 1, 2))

        def turn(kind, b, i):
            return TURNS.index((kind, b, i))

        def max_item(i):
            m, r = i // 6, i % 6
            return (m, 0, 2 * r) if r < 2 else (m, 1, r - 2)

        def ring_free(engine, c):
            kind, _ = CHUNKS[c]
            if kind == "lra":
                engine.wait_ge(hid_ready, 2)
                return
            if kind == "wo":
                engine.wait_ge(pv_ready, 24)
                return
            if kind not in IN_RING or chunk_place(*CHUNKS[c])[1] < N_RING:
                return
            before = [x for x in range(c) if CHUNKS[x][0] in IN_RING][-N_RING]
            kind, i = CHUNKS[before]
            half = CHUNKS[:before].count(CHUNKS[before])
            if kind == "gu0":
                engine.wait_ge(gu_ready, 4 * i + 4)
            elif kind == "gu1":
                engine.wait_ge(gu_ready, 4 * NF + NF * half + i + 1)
            elif kind == "lrd":
                engine.wait_ge(rd_ready, half + 1)
            elif kind == "dn0" and i < 4:
                engine.wait_ge(hid_used, 2 * i + 2)
            elif kind == "dn1" and i < 5:
                engine.wait_ge(chunk_used, 5 * half + i + 1)
            else:
                engine.wait_ge(dn_ready, NT if kind == "dn0" else NT + 4 * half + 4)

        def chunk_ready(engine, c):
            if CHUNKS[c][0] == "dn1":
                engine.wait_ge(hi_done, hi_value(c))
            else:
                engine.wait_ge(lo_done, lo_value(c))

        def ring_slot(c):
            return ring[:, sum(k in IN_RING for k, _ in CHUNKS[:c]) % N_RING, :, :]

        def chunk_parts(c):
            kind, i = CHUNKS[c]
            slot = stage[:, c % N_STAGE, :]
            w = ring_slot(c)
            if kind == "qkv":
                to = wqkv[:, :, :, 256 * i:256 * i + 256]
                return to[:, 0], to[:, 1], slot[:, 0:1024].rearrange("p (k n) -> p k n", k=KD)
            if kind == "win":
                to = win_hl[:, :, :, CH:2 * CH]
                return to[:, 0], to[:, 1], slot[:, 0:256].rearrange("p (k n) -> p k n", k=KD)
            if kind == "lra":
                return lra_hl[:, 0, :], lra_hl[:, 1, :], slot[:, 0:768]
            if kind == "wo":
                to = wo_hl[:, i, :, :, :]
                return to[:, 0], to[:, 1], slot[:, 0:1024].rearrange("p (k n) -> p k n", k=2)
            n = {"gu0": 8 * FW[i % NF], "lrd": 1056, "gu1": 8 * FW[i % NF]}.get(kind, 1024)
            rows = P
            if kind in ("dn0", "dn1") and i == 5:
                n, rows = 512, FW[-1]
            return w[0:rows, 0, 0:n], w[0:rows, 1, 0:n], slot[0:rows, 0:n]

        block = ctx.enter_context(nc.Block())

        @block.sync
        def _(sp):
            xd = A["x"].rearrange("(t p) d -> t p d", p=P)

            def chunk_load(c):
                kind, i = CHUNKS[c]
                if c >= N_STAGE:
                    chunk_ready(sp, c - N_STAGE)
                slot = stage[:, c % N_STAGE, :]
                done = stage_loaded[c % N_STAGE]
                if kind == "qkv" and i < 2:
                    sp.dma_start(slot[:, 0:1024].rearrange("p (k n) -> p k n", k=KD),
                                 A["wq"].rearrange("(k p) n -> p k n", p=P)[:, :, 256 * i:256 * i + 256]).then_inc(done, 16)
                elif kind == "qkv":
                    v = slot[:, 0:1024].rearrange("p (k n) -> p k n", k=KD)
                    sp.dma_start(v[:, :, 0:128], A["wk"].rearrange("(k p) n -> p k n", p=P)).then_inc(done, 16)
                    sp.dma_start(v[:, :, 128:256], A["wv"].rearrange("(k p) n -> p k n", p=P)).then_inc(done, 16)
                elif kind == "wo":
                    sp.dma_start(slot[:, 0:1024].rearrange("p (k n) -> p k n", k=2),
                                 A["wo"].rearrange("(k p) n -> p k n", p=P)[:, 2 * i:2 * i + 2, :]).then_inc(done, 16)
                elif kind == "gu0":
                    sp.dma_start(slot[:, 0:8 * FW[i]], A["gu0"][:, 1024 * i:1024 * i + 8 * FW[i]]).then_inc(done, 16)
                elif kind == "gu1":
                    sp.dma_start(slot[:, 0:8 * FW[i]].bitcast(I32), A["gu1"][:, 1024 * i:1024 * i + 8 * FW[i]]).then_inc(done, 16)
                    sp.dma_start(slot[0:LRR, 1024:1024 + 2 * FW[i]], A["lrb"][:, 256 * i:256 * i + 2 * FW[i]]).then_inc(done, 16)
                elif kind in ("dn0", "dn1"):
                    w = A[kind]
                    if i < 5:
                        to = slot[:, 0:1024].rearrange("p (k n) -> p k n", k=2)
                        of = w[256 * i:256 * i + 256, :].rearrange("(k p) n -> p k n", p=P)
                    else:
                        to = slot[0:FW[-1], 0:512]
                        of = w[1280:F, :]
                    sp.dma_start(to if kind == "dn0" else to.bitcast(I32), of).then_inc(done, 16)
                elif kind == "win":
                    sp.dma_start(slot[:, 0:256].rearrange("p (k n) -> p k n", k=KD),
                                 A["winT"].rearrange("(k p) n -> p k n", p=P)).then_inc(done, 16)
                elif kind == "lra":
                    sp.dma_start(slot[:, 0:768], A["lra"]).then_inc(done, 16)
                elif kind == "lrd":
                    sp.dma_start(slot[:, 0:1056], A["lrd"]).then_inc(done, 16)
                elif kind == "lrb":
                    sp.dma_start(slot[0:LRR, 0:512], A["lrdb"]).then_inc(done, 16)

            for t in range(4):
                sp.dma_start(x0[:, t, :], xd[t]).then_inc(x_loaded[t], 16)
            chunk_load(0)
            for t in range(4, NT):
                sp.dma_start(x0[:, t, :], xd[t]).then_inc(x_loaded[t], 16)
            chunk_load(1)
            sp.dma_start(cols[:], A["cols"]).then_inc(cols_loaded, 16)
            sp.dma_start(bv_b[:], A["bv"].to_broadcast([P, P])).then_inc(bv_loaded, 16)
            sp.dma_start(row_b[:], A["bo"].to_broadcast([P, D])).then_inc(bo_loaded, 16)
            chunk_load(2)

            def projections_out(n):
                half, u = n // 5, n % 5
                sp.wait_ge(proj_split, n + 1)
                tok = slice(half * HALF, (half + 1) * HALF)
                for place, part in enumerate((0, 0, 1) if u < 4 else (0, 1, 0)):
                    of = proj_hl[:, n % 2, part, :].bitcast(F32)
                    if u < 4:
                        heads = slice(8 * (u % 2), 8 * (u % 2) + 8)
                        sp.dma_start(q_bounce[u // 2, place, :, heads, tok].rearrange("r a t -> a r t"), of)\
                          .then_inc(q_out[n % 2], 16)
                    else:
                        for j in range(2):
                            sp.dma_start(k_bounce[j, place, :, :, tok].rearrange("r a t -> a r t"),
                                         of[64 * j:64 * (j + 1)]).then_inc(q_out[n % 2], 16)

            def stacks_in(b):
                last = 4 + 5 * (b // 2)
                sp.wait_ge(q_out[0], out_value(last - last % 2))
                sp.wait_ge(q_out[1], out_value(last - 1 + last % 2))
                if b == 0:
                    sp.wait_ge(ks_zeroed, 1)
                if b >= 2:
                    sp.wait_ge(s2_ready, 24 * (b - 1))
                tok = slice(b * SEQ, (b + 1) * SEQ)
                sp.dma_start(qs[0:96, b % 2, :, :, :].rearrange("p m g t -> p (m g) t").bitcast(F32),
                             q_bounce[:, :, :, :, tok].rearrange("j s r a t -> (j s r) a t")).then_inc(qs_loaded[b % 2], 16)
                for j in range(2):
                    sp.dma_start(ks[48 * j:48 * (j + 1), b % 2, j, :, :].bitcast(F32),
                                 k_bounce[j, :, :, :, tok].rearrange("s r a t -> (s r) a t")).then_inc(qs_loaded[b % 2], 16)

            def maxima(b):
                sp.wait_ge(turn_read, turn("maxT", b, 0) + 1)
                for part in range(2):
                    sp.dma_start(m_bounce[b, :, part, :, :],
                                 max_hl[:, part, :].bitcast(F32)).then_inc(m_out, 16)
                sp.wait_ge(m_out, 32 * (b + 1))
                sp.dma_start(qs[96:100, b % 2, :, :, :].rearrange("p m g t -> p (m g t)").bitcast(F32),
                             m_bounce[b].rearrange("j p a t -> (j p) (a t)")).then_inc(m_loaded[b % 2], 16)

            chunk_load(GU0)
            loaded = GU0 + 1
            for kind, a, i in ATT:
                if kind == "qkv" and i < 5:
                    projections_out(5 * a + i)
                    if a == 0 and i == 4:
                        stacks_in(0)
                    if a == 1 and i == 4:
                        stacks_in(1)
                    if (a, i) in ((0, 0), (1, 1), (1, 3)):
                        chunk_load(loaded)
                        loaded += 1
                elif kind == "ffn" and i == 3 and a % 2 == 1 and 3 <= a < 2 * NF - 1:
                    chunk_load(loaded)
                    loaded += 1
                elif kind == "maxT":
                    maxima(a)
                elif kind == "scores" and i == 3 and a in (5, 11):
                    stacks_in(a // 6 + 2)
            sp.wait_ge(pv_ready, 24)
            sp.dma_start(x[:], A["x"].rearrange("(t p) d -> p t d", p=P)).then_inc(x_back, 16)
            for c in range(loaded, GU1 + 2):
                chunk_load(c)
            sp.wait_ge(s_ready, NT)
            sp.wait_ge(dn_ready, NT)
            sp.dma_start(row_b[:], A["bout"].to_broadcast([P, D])).then_inc(late_loaded, 16)
            sp.dma_start(dscale_b[:], A["dscale"].to_broadcast([P, D])).then_inc(late_loaded, 16)
            sp.dma_start(ssmw[:], A["ssmw"]).then_inc(late_loaded, 16)
            for c in range(GU1 + 2, len(CHUNKS)):
                chunk_load(c)
            od = A["out"].rearrange("(t p) d -> t p d", p=P)
            for t in range(NT):
                sp.wait_ge(out_ready, t + 1)
                sp.dma_start(od[t], x[:, t, :]).then_inc(stored, 16)
            sp.wait_ge(stored, 16 * NT)

        @block.gpsimd
        def _(pool):
            chain = [0]

            def link(ins):
                chain[0] += 1
                ins.then_inc(pool_chain, 1)
                pool.wait_ge(pool_chain, chain[0])

            signals = {}

            def signal(ins, done):
                signals[done.name] = signals.get(done.name, 0) + 1
                ins.then_inc(done, 1)
                pool.wait_ge(done, signals[done.name])

            def chunk_lo(c):
                kind, i = CHUNKS[c]
                slot = stage[:, c % N_STAGE, :]
                hi, lo, of = chunk_parts(c)
                if kind == "dn1":
                    return
                if kind in ("win", "lrb"):
                    pool.wait_ge(stage_loaded[c % N_STAGE], stage_value(c))
                else:
                    pool.wait_ge(hi_done, hi_value(c))
                if kind == "win":
                    link(pool.memset(win_hl[:].bitcast(F32), 0.0))
                    link(pool.tensor_copy(hi, of))
                if kind == "gu1":
                    of = slot[0:LRR, 1024:1024 + 2 * FW[i]]
                    to = ring_slot(c)[0:LRR, 1, 0:2 * FW[i]]
                    mid = slice(RANK, 2 * RANK)
                    signal(pool.tensor_tensor(to[mid], of[mid], to[mid].bitcast(F32), ALU.subtract), lo_done)
                elif kind == "lrb":
                    of = slot[0:LRR, 0:512]
                    if CHUNKS[:c].count(("lrb", 0)):
                        pool.wait_ge(dn_ready, NT + 4)
                    link(pool.tensor_copy(lrdb[:], of))
                    mid = slice(RANK, 2 * RANK)
                    signal(pool.tensor_tensor(lrdb[mid, :], of[mid], lrdb[mid, :].bitcast(F32), ALU.subtract), lo_done)
                else:
                    signal(pool.tensor_tensor(lo, of, hi.bitcast(F32), ALU.subtract), lo_done)

            def rsqrt_pair(n, g):
                pool.wait_ge(var_ready, 4 * n + g + 1)
                signal(pool.tensor_tensor(rstd[:, 2 * g:2 * g + 2], ve[:, 2 * g:2 * g + 2], nhalf[:, 0:2], ALU.pow), rstd_ready)

            def rot_start():
                pool.wait_ge(phasor_scaled, 1)
                link(pool.memset(cs[0:64, 5, :], 1.0))
                link(pool.memset(cs[64:128, 5, :], -1.0))
                link(pool.tensor_tensor(cs[:, 8, :], cs[:, 3, :], nhalf[:, 0:DEPTH], ALU.pow))
                link(pool.tensor_tensor(cs[:, 6, :], cs[:, 0, :], cs[:, 8, :], ALU.mult))
                link(pool.tensor_tensor(cs[:, 7, :], cs[:, 1, :], cs[:, 8, :], ALU.mult))
                link(pool.tensor_tensor(cs[:, 9, :], cs[:, 3, :], cs[:, 8, :], ALU.mult))
                signal(pool.tensor_tensor(cs[:, 4, :], cs[:, 9, :], cs[:, 2, :], ALU.mult), polar_ready)
                link(pool.tensor_tensor(cs[:, 10, :], cs[:, 6, :], cs[:, 5, :], ALU.mult))
                link(pool.tensor_tensor(cs[:, 10, :], cs[:, 10, :], col("lc_a", 0, 4), ALU.mult))
                link(pool.tensor_tensor(cs[:, 11, :], cs[:, 7, :], col("lc_b", 0, 4), ALU.mult))
                link(pool.tensor_tensor(start[:], cs[:, 10, :], cs[:, 11, :], ALU.subtract))

            def rot_angle(k):
                link(pool.tensor_tensor(cs[:, 8, :], cs[:, 6, :], cs[:, 6, :], ALU.mult))
                link(pool.tensor_tensor(cs[:, 9, :], cs[:, 7, :], cs[:, 7, :], ALU.mult))
                link(pool.tensor_tensor(cs[:, 8, :], cs[:, 8, :], cs[:, 9, :], ALU.add))
                link(pool.tensor_scalar(cs[:, 8, :], cs[:, 8, :], -0.5, 1.5, ALU.mult, ALU.add))
                c, s = trig[:, k, 0, :], trig[:, k, 1, :]
                link(pool.tensor_tensor(c, cs[:, 6, :], cs[:, 8, :], ALU.mult))
                link(pool.tensor_tensor(s, cs[:, 7, :], cs[:, 8, :], ALU.mult))
                if k < 7:
                    link(pool.tensor_tensor(cs[:, 8, :], c, c, ALU.mult))
                    link(pool.tensor_tensor(cs[:, 9, :], s, s, ALU.mult))
                    link(pool.tensor_tensor(cs[:, 10, :], c, s, ALU.mult))
                    link(pool.tensor_tensor(cs[:, 6, :], cs[:, 8, :], cs[:, 9, :], ALU.subtract))
                    link(pool.tensor_tensor(cs[:, 7, :], cs[:, 10, :], cs[:, 10, :], ALU.add))

            def rot_step(k):
                n = 1 << k
                c = trig[:, k, 0, :].unsqueeze(2).to_broadcast([P, DEPTH, n])
                s = trig[:, k, 1, :].unsqueeze(2).to_broadcast([P, DEPTH, n])
                a, b = rot[:, :, 0:n], rotb[:, :, 0:n]
                link(pool.tensor_tensor(rtmp[:, 0, :, 0:n], a, c, ALU.mult))
                link(pool.tensor_tensor(rtmp[:, 1, :, 0:n], b, s, ALU.mult))
                if k == 7:
                    signal(pool.tensor_tensor(rot[:, :, n:2 * n], rtmp[:, 0, :, 0:n], rtmp[:, 1, :, 0:n], ALU.add), rot_ready)
                    return
                link(pool.tensor_tensor(rot[:, :, n:2 * n], rtmp[:, 0, :, 0:n], rtmp[:, 1, :, 0:n], ALU.add))
                link(pool.tensor_tensor(rtmp[:, 0, :, 0:n], b, c, ALU.mult))
                link(pool.tensor_tensor(rtmp[:, 1, :, 0:n], a, s, ALU.mult))
                link(pool.tensor_tensor(rotb[:, :, n:2 * n], rtmp[:, 0, :, 0:n], rtmp[:, 1, :, 0:n], ALU.subtract))

            link(pool.memset(nhalf[:], -0.5))
            link(pool.memset(ident[:], 0.0))
            signal(pool.affine_select(out=ident[:], in_=ident[:], compare_op=ALU.not_equal, fill=1.0, base=0,
                               pattern=[[-1, P]], channel_multiplier=1), ident_ready)
            pool.wait_ge(ident_ready, 1)
            for g in range(2):
                rsqrt_pair(0, g)
            chunk_lo(0)
            for kind, a, i in ATT:
                if kind == "tr" and a in (1, 3):
                    rsqrt_pair(0, 2 + a // 2)
                elif kind == "qkv" and a == 0 and i < 4:
                    chunk_lo(i + 1)
                    if i == 1:
                        link(pool.memset(ks[:].bitcast(F32), 0.0))
                        link(pool.memset(ks[96:98, :, 0, :, :].bitcast(F32), 1.0))
                        link(pool.memset(ks[96:100, :, 1, :, :].bitcast(F32), 1.0))
                        signal(pool.memset(ks[96:98, :, 1, :, :].bitcast(F32), 0.0), ks_zeroed)
                        link(pool.memset(v_sb[:], 1.0))
                        link(pool.memset(maskA[:], 0.0))
                        link(pool.affine_select(out=maskA[:], in_=maskA[:], compare_op=ALU.is_ge, fill=MASKED, base=0,
                                                pattern=[[0, 4], [-1, P]], channel_multiplier=1))
                        signal(pool.tensor_copy(identb[:], ident[:]), consts_ready)
                elif kind == "qkv" and a == 1 and i == 5:
                    rot_start()
                elif kind == "max" and a == 0 and i % 3 == 2:
                    rot_angle(i // 3)
                elif kind == "ffn" and i == 1 and a % 2 == 0 and 2 <= a < 2 * NF - 2:
                    chunk_lo(GU0 + a // 2 + 1)
                elif kind == "scores" and a % 3 != 1:
                    n = 4 * a + i
                    pool.wait_ge(exp_ready, n + 1)
                    pt = probs[:, n % 8, :].rearrange("p (g q) -> p g q", g=GRP)
                    pool.affine_select(out=pt, in_=pt, compare_op=ALU.is_ge, fill=0.0, base=0,
                                       pattern=[[0, GRP], [1, P]], channel_multiplier=-1).then_inc(masked, 1)
            pool.wait_ge(masked, 64)
            for c in (WO, WO + 1):
                chunk_lo(c)

            link(pool.memset(rot[0:64, :, 0:1], 1.0))
            link(pool.memset(rot[64:128, :, 0:1], 0.0))
            link(pool.memset(rotb[0:64, :, 0:1], 0.0))
            link(pool.memset(rotb[64:128, :, 0:1], 1.0))
            for c in (DN0, DN0 + 1):
                chunk_lo(c)
            for k in range(8):
                rot_step(k)
            chunk_lo(DN0 + 2)
            link(pool.memset(sel[:], 0.0))
            link(pool.memset(comb[:], 0.0))
            link(pool.memset(bdc[:], 0.0))
            link(pool.tensor_copy(center[:], ident[:]))
            for j in range(2):
                r = slice(CH * j, CH * j + CH)
                for i in range(2):
                    link(pool.tensor_copy(sel[r, j, CH * i:CH * i + CH], ident[r, r]))
                link(pool.tensor_tensor(comb[:, j, r], ident[:, 0:CH], ident[:, CH:P], ALU.add))
                link(pool.tensor_scalar(center[r, r], center[r, r], -1.0 / CH, None, ALU.add))
                ins = pool.memset(bdc[r, j:j + 1], 1.0 / CH)
                if j == 0:
                    link(ins)
                else:
                    signal(ins, late_consts)
            for c in range(DN0 + 3, LRA + 1):
                chunk_lo(c)
            for kind, t, _ in ORDER1:
                if kind == "dl":
                    pool.wait_ge(g_ready, t + 1)
                    if t >= 4:
                        pool.wait_ge(x1_ready, t - 3)
                    pool.tensor_tensor(ht0[:, t % 4, :], sg0[:, t % 2, :], s_sb[:, t, :], ALU.mult).then_inc(gs_ready, 1)
                    if t == 2 or t in (3, 5, 7):
                        rsqrt_pair(1, t // 2 - (t == 2))
            chunk_lo(GU1)
            for c, (kind, a, i) in ahead_of(ORDER1):
                if c is not None:
                    chunk_lo(c)
                elif kind == "ssm":
                    l, step, c = SSM_STEPS[a]
                    if step in ("var1", "var2"):
                        nth = 2 * l + (step == "var2")
                        pool.wait_ge(ln_stat, 2 * nth + c + 1)
                        signal(pool.tensor_tensor(trs[:, c, :], tstat[:, c, :], nhalf[:, 0:4], ALU.pow), ln_pow)

        @block.scalar
        def _(act):
            chain = [0]

            def link(ins):
                chain[0] += 1
                ins.then_inc(act_chain, 1)
                act.wait_ge(act_chain, chain[0])

            def ln_hi(n, t):
                act.wait_ge(xt_ready, NT * n + t + 1)
                act.activation(xnT[:, 0, :, t * P:(t + 1) * P], PS[:, LN_BANK[n] + t % 2, :].rearrange("p (k q) -> p k q", k=KD),
                               ACT.Copy).then_inc(xh_ready, 1)

            def chunk_hi(c):
                kind, i = CHUNKS[c]
                if kind in ("win", "lrb"):
                    return
                act.wait_ge(stage_loaded[c % N_STAGE], stage_value(c))
                ring_free(act, c)
                hi, _, of = chunk_parts(c)
                if kind in ("gu1", "dn1"):
                    if kind == "gu1":
                        act.activation(ring_slot(c)[0:LRR, 1, 0:2 * FW[i]],
                                       stage[0:LRR, c % N_STAGE, 1024:1024 + 2 * FW[i]], ACT.Copy)
                    act.activation(hi, of.bitcast(I32), ACT.Copy, bias=-7.5).then_inc(hi_done, 1)
                else:
                    act.activation(hi, of, ACT.Copy).then_inc(hi_done, 1)

            chunk_hi(0)

            def projection(n):
                half, u = n // 5, n % 5
                act.wait_ge(qkv_ready, 6 * half + u + 1)
                if n:
                    act.wait_ge(proj_split, n)
                if n == 0:
                    act.wait_ge(bq_ready, 1)
                bias, scale = (bq4[:, u:u + 1], 0.25) if u < 4 else (col("bk"), 1.0)
                act.activation(proj[:], PS[:, u % 2, :], ACT.Identity, bias=bias, scale=scale).then_inc(proj_ready, 1)

            def max_hi(b):
                n = turn("maxT", b, 0)
                act.wait_ge(turn_ready, n + 1)
                if b:
                    act.wait_ge(m_out, 32 * b)
                act.activation(max_hl[:, 0, :], PS[0:32, 2 + n % 2, 0:SEQ], ACT.Copy).then_inc(mh_ready, 1)

            def exps(G, kv):
                n = 4 * G + kv
                act.wait_ge(s2_ready, n + 1)
                if G >= 2:
                    act.wait_ge(pv_ready, G - 1)
                act.activation(probs[:, n % 8, :], PS[:, n % 2, :], ACT.Exp).then_inc(exp_ready, 1)

            def outputs(bq):
                act.wait_ge(pv_ready, 3 * bq + 3)
                for qt in range(2):
                    if bq:
                        act.wait_ge(turn_ready, turn("back", bq - 1, qt) + 1)
                    act.activation(outT[:, qt, :], PS[:, 5 + qt, :], ACT.Copy).then_inc(ot_ready, 1)

            def gate(job):
                act.wait_ge(gu_ready, 2 * job + 1)
                if job >= 2:
                    act.wait_ge(up_used, job - 1)
                fw = FW[job // 2]
                act.activation(sg0[0:fw, job % 2, :], PS[0:fw, 4, :], ACT.Tanh, scale=0.5).then_inc(tanh_ready, 1)

            for kind, a, i in ATT:
                if kind == "tr":
                    ln_hi(0, a)
                    if a in (1, 3):
                        chunk_hi(1 + a // 2)
                elif kind == "max" and a == 0 and i == 12:
                    act.wait_ge(polar_ready, 1)
                    act.activation(decay[:], cs[:, 4, :], ACT.Tanh).then_inc(decay_ready, 1)
                elif kind == "qkv" and i < 5:
                    projection(5 * a + i)
                    if a == 0 and i in (1, 3):
                        chunk_hi(GU0 + i // 2)
                elif kind == "maxT":
                    max_hi(a)
                elif kind == "scores":
                    exps(a, i)
                elif kind == "values" and a % 3 == 2:
                    outputs(a // 3)
                elif kind == "ffn" and i == 1:
                    if a % 2 == 0 and 2 <= a < 2 * NF - 2:
                        chunk_hi(GU0 + a // 2 + 1)
                    gate(a)
                elif kind == "back" and a == 7 and i == 1:
                    for c in (WO, WO + 1):
                        chunk_hi(c)
            for t in range(NT):
                act.wait_ge(at_ready, t + 1)
                if t >= 2:
                    act.wait_ge(wo_ready, t - 1)
                act.activation(attT[:, t % 2, 0, :, :], PS[:, t % 2, :].rearrange("p (k q) -> p k q", k=KD), ACT.Copy)\
                   .then_inc(ah_ready, 1)
                if t in (1, 3):
                    chunk_hi(DN0 + t // 2)
            for c in range(DN0 + 2, DN0 + 6):
                chunk_hi(c)
            chunk_hi(LRA)

            def down_silu(t):
                act.wait_ge(dn_ready, t + 1)
                if t >= 2:
                    act.wait_ge(gs_ready, t - 1)
                act.activation(sg0[:, t % 2, :], PS[:, t, :], ACT.Silu).then_inc(g_ready, 1)

            def copies(J):
                fw = FW[J % NF]
                act.wait_ge(gu_ready, 4 * NF + J + 1)
                if J:
                    act.wait_ge(up_used, 2 * NF + J)
                else:
                    act.wait_ge(gs_ready, NT)
                for o in range(2):
                    ins = act.activation(e_lr[0:fw, o, :], PS[0:fw, 6 + o, :], ACT.Copy)
                ins.then_inc(lr_copied, 1)

            def silu(J):
                fw = FW[J % NF]
                act.wait_ge(gsum_ready, J + 1)
                act.activation(e_gu[0:fw, 0, :], e_gu[0:fw, 0, :], ACT.Silu).then_inc(silu_ready, 1)

            def model(n):
                l, step, c = SSM_STEPS[n]
                nth = 2 * l + (step[-1] == "2")
                seq = slice(SEQ * c, SEQ * (c + 1))
                if step in ("cen1", "cen2"):
                    act.wait_ge(ln_cen, 2 * nth + c + 1)
                    act.activation(act1[:, seq], PS[:, c, 0:SEQ], ACT.Copy).then_inc(ln_copied, 1)
                    act.activation(tmp1[:, seq], PS[:, c, 0:SEQ], ACT.Square).then_inc(ln_sq, 1)
                elif step in ("rstd1", "rstd2"):
                    act.wait_ge(ln_norm, 2 * nth + c + 1)
                    if l == DEPTH:
                        f, w, b = ACT.Identity, col("lnl_w"), col("lnl_b")
                    elif step == "rstd1":
                        f, w, b = ACT.Silu, col("ln1_w", l), col("ln1_b", l)
                    else:
                        f, w, b = ACT.Identity, col("ln2_w", l), col("ln2_b", l)
                    act.activation(act1[:, seq], act1[:, seq], f, bias=b, scale=w).then_inc(ln_out, 1)
                elif step in ("w1a", "w1b"):
                    ft = int(step == "w1b")
                    act.wait_ge(w1_ready, 4 * l + 2 * ft + c + 1)
                    act.activation(sv[:, ft, :, seq], PS[:, c, :].rearrange("p (h t) -> p h t", h=2), ACT.Silu,
                                   bias=col("b1", 2 * l + ft)).then_inc(w1_act, 1)

            for c, (kind, a, i) in ahead_of(ORDER1):
                J = NF * a + i
                if c is not None:
                    chunk_hi(c)
                elif kind == "dl":
                    down_silu(a)
                    if a == 7:
                        chunk_hi(GU1)
                elif kind == "tr":
                    ln_hi(1, a)
                elif kind == "lr":
                    n = 2 * a + i
                    act.wait_ge(lr_ready, n + 1)
                    if n >= 2:
                        act.wait_ge(lr_split, n - 1)
                    act.activation((act1, tmp1)[n % 2][0:LRR, :], PS[0:LRR, LR_BANK[n], :], ACT.Copy, scale=0.02).then_inc(lr_inner, 1)
                elif kind == "win":
                    act.wait_ge(win_ready, 1)
                    act.activation(h[:], PS[:, 0, :], ACT.Identity, bias=col("bin"), scale=1.0).then_inc(h0_ready, 1)
                elif kind == "copies":
                    copies(J)
                elif kind == "silu":
                    silu(J)
                elif kind == "ssm":
                    model(a)
                elif kind == "rd" and i == 3:
                    act.wait_ge(rd_ready, a + 1)
                    act.wait_ge(up_used, 2 * NF + NF * (a + 1))
                    act.activation(e_lr[0:LRR, 0, :], PS[0:LRR, 6, :], ACT.Copy, scale=0.02).then_inc(rd_copied, 1)
                elif kind == "fin":
                    act.wait_ge(fsum_ready, i + 1)
                    act.activation(s_sb[:, i, :], e_gu[:, i % 2, :], ACT.Silu).then_inc(fg_ready, 1)
                elif kind == "end":
                    act.wait_ge(fsum_ready, 4 + i + 1)
                    if i >= 2:
                        act.wait_ge(out_ready, 4 + i - 1)
                    act.activation(e_lr[:, i % 2, :], e_gu[:, i % 2, :], ACT.Silu).then_inc(fg_ready, 1)

        @block.vector
        def _(dve):
            chain = [0]

            def link(ins):
                chain[0] += 1
                ins.then_inc(dve_chain, 1)
                dve.wait_ge(dve_chain, chain[0])

            def note(ins):
                chain[0] += 1
                ins.then_inc(dve_chain, 1)

            def statistics(n, g):
                xs = (x0, x)[n]
                for t in (2 * g, 2 * g + 1):
                    if n == 0:
                        dve.wait_ge(x_loaded[t], 16)
                    (note, link)[t % 2](dve.bn_stats(bn6[:, t, :], xs[:, t, :]))
                note(dve.bn_aggr(mv[:, 2 * g, :], bn6[:, 2 * g, :]))
                link(dve.bn_aggr(mv[:, 2 * g + 1, :], bn6[:, 2 * g + 1, :]))
                dve.tensor_scalar(ve[:, 2 * g:2 * g + 2], mv[:, 2 * g:2 * g + 2, 1], EPS, None, ALU.add).then_inc(var_ready, 1)

            def normalised(n, g):
                xs = (x0, x)[n]
                dve.wait_ge(rstd_ready, 4 * n + g + 1)
                for t in (2 * g, 2 * g + 1):
                    if NT * n + t >= 2:
                        dve.wait_ge(xt_ready, NT * n + t - 1)
                    dve.tensor_scalar(xn[:, t % 2, :], xs[:, t, :], mv[:, t, 0:1], rstd[:, t:t + 1],
                                      ALU.subtract, ALU.mult).then_inc(xn_ready, 1)

            def ln_tiles(n, g):
                if n == 0 and g < 2:
                    statistics(0, g + 2)
                if g < 3:
                    normalised(n, g + 1)
                for t in (2 * g, 2 * g + 1):
                    dve.wait_ge(xh_ready, NT * n + t + 1)
                    o = slice(t * P, (t + 1) * P)
                    dve.tensor_tensor(xnT[:, 1, :, o], PS[:, LN_BANK[n] + t % 2, :].rearrange("p (k q) -> p k q", k=KD),
                                      xnT[:, 0, :, o].bitcast(F32), ALU.subtract).then_inc(xl_ready, 1)

            statistics(0, 0)
            normalised(0, 0)
            statistics(0, 1)

            def projection_split(n):
                dve.wait_ge(proj_ready, n + 1)
                if n >= 2:
                    dve.wait_ge(q_out[n % 2], out_value(n - 2))
                link(dve.tensor_copy(proj_hl[:, n % 2, 0, :], proj[:]))
                dve.tensor_tensor(proj_hl[:, n % 2, 1, :], proj[:], proj_hl[:, n % 2, 0, :].bitcast(F32),
                                  ALU.subtract).then_inc(proj_split, 1)

            def values_in(half):
                dve.wait_ge(qkv_ready, 6 * half + 6)
                if half == 0:
                    dve.wait_ge(consts_ready, 1)
                    dve.wait_ge(bv_loaded, 16)
                for q in range(4):
                    ins = dve.tensor_tensor(v_sb[:, 4 * half + q, :, 0:DH],
                                            PS[:, 1, q * P:(q + 1) * P].rearrange("p (h e) -> p h e", h=NKV),
                                            bv_b[:].rearrange("p (h e) -> p h e", h=NKV), ALU.add)
                ins.then_inc(v_ready, 1)

            def s_out(t):
                dve.wait_ge(wo_ready, t + 1)
                if t == 0:
                    dve.wait_ge(bo_loaded, 16)
                dve.tensor_tensor(s_sb[:, t, :], PS[:, 2 + t % 2, :], row_b[:], ALU.add).then_inc(s_ready, 1)

            def maximum(b, i):
                n, (m, qt, g) = turn("max", b, i), max_item(i)
                dve.wait_ge(turn_ready, n + 1)
                to = negmax[:, b, qt, :].rearrange("p (j m g) -> p m g j", j=2, m=4)
                if qt == 0:
                    to = to[:, m, g:g + 2, :]
                    of = PS[:, 2 + n % 2, :].rearrange("p (g j k) -> p g j k", g=2, j=2)
                else:
                    to = to[:, m, g, :]
                    of = PS[:, 2 + n % 2, :].rearrange("p (j k) -> p j k", j=2)
                dve.tensor_reduce(to, of, AX_X, ALU.max, negate=True).then_inc(turn_read, 1)

            def max_lo(b):
                n = turn("maxT", b, 0)
                dve.wait_ge(mh_ready, b + 1)
                dve.tensor_tensor(max_hl[:, 1, :], PS[0:32, 2 + n % 2, 0:SEQ], max_hl[:, 0, :].bitcast(F32), ALU.subtract)\
                   .then_inc(turn_read, 1)

            def normalise(bq, qt):
                n, t = turn("back", bq, qt), 2 * (bq // 2) + qt
                dve.wait_ge(turn_ready, n + 1)
                o = PS[:, 2 + n % 2, :].rearrange("p (g k e) -> p g k e", g=GRP, k=4)
                den = rden[:, qt, :].rearrange("p (g k) -> p g k", g=GRP)
                link(dve.reciprocal(den, o[:, :, :, DH]))
                to = s_sb[:, t, 256 * (bq % 2):256 * (bq % 2 + 1)].rearrange("p (k g e) -> p g k e", k=4, g=GRP)
                dve.tensor_tensor(to, o[:, :, :, 0:DH], den.unsqueeze(3).to_broadcast([P, GRP, 4, DH]), ALU.mult)\
                   .then_inc(turn_read, 1)

            def gated(job):
                fw, sg = FW[job // 2], sg0[0:FW[job // 2], job % 2, :]
                dve.wait_ge(tanh_ready, job + 1)
                dve.scalar_tensor_tensor(sg, sg, 1.0, PS[0:fw, 4, :], ALU.add, ALU.mult).then_inc(gate_used, 1)

            def gate_up(job):
                fw, sg = FW[job // 2], sg0[0:FW[job // 2], job % 2, :]
                dve.wait_ge(gate_used, job + 1)
                dve.wait_ge(gu_ready, 2 * job + 2)
                dve.scalar_tensor_tensor(hidf[0:fw, 2 * NF - 1 - job, :], sg, 0.5, PS[0:fw, 7, :], ALU.mult, ALU.mult)\
                   .then_inc(up_used, 1)

            def phasors():
                re, im = col("ph_re", 0, 4), col("ph_im", 0, 4)
                link(dve.tensor_scalar(cs[:, 8, :], re, -1.0, None, ALU.mult))
                link(dve.tensor_scalar(cs[:, 9, :], im, -1.0, None, ALU.mult))
                link(dve.tensor_tensor(cs[:, 8, :], cs[:, 8, :], re, ALU.max))
                link(dve.tensor_tensor(cs[:, 9, :], cs[:, 9, :], im, ALU.max))
                link(dve.tensor_tensor(cs[:, 2, :], cs[:, 8, :], cs[:, 9, :], ALU.max))
                link(dve.tensor_scalar(cs[:, 10, :], cs[:, 2, :], 0.0, None, ALU.is_equal))
                link(dve.tensor_scalar(cs[:, 8, :], cs[:, 2, :], 1.2e-38, None, ALU.max))
                link(dve.reciprocal(cs[:, 9, :], cs[:, 8, :]))
                link(dve.tensor_tensor(cs[:, 0, :], re, cs[:, 9, :], ALU.mult))
                link(dve.tensor_tensor(cs[:, 0, :], cs[:, 0, :], cs[:, 10, :], ALU.add))
                link(dve.tensor_tensor(cs[:, 1, :], im, cs[:, 9, :], ALU.mult))
                link(dve.tensor_tensor(cs[:, 8, :], cs[:, 0, :], cs[:, 0, :], ALU.mult))
                link(dve.tensor_tensor(cs[:, 9, :], cs[:, 1, :], cs[:, 1, :], ALU.mult))
                dve.tensor_tensor(cs[:, 3, :], cs[:, 8, :], cs[:, 9, :], ALU.add).then_inc(phasor_scaled, 1)

            for kind, a, i in ATT:
                if kind == "tr" and a % 2:
                    ln_tiles(0, a // 2)
                elif kind == "qkv" and i < 5:
                    if a == 0 and i == 0:
                        dve.wait_ge(cols_loaded, 16)
                        dve.tensor_scalar(bq4[:], col("bq", 0, 4), 0.25, None, ALU.mult).then_inc(bq_ready, 1)
                    projection_split(5 * a + i)
                elif kind == "qkv":
                    values_in(a)
                    if a:
                        phasors()
                elif kind == "max":
                    maximum(a, i)
                elif kind == "maxT":
                    max_lo(a)
                elif kind == "back":
                    normalise(a, i)
                elif kind == "ffn" and i == 2:
                    gated(a)
                elif kind == "ffn" and i == 3:
                    gate_up(a)

            def hidden_split(k):
                if k == 1:
                    dve.wait_ge(wo_ready, NT)
                if k >= N_HID:
                    dve.wait_ge(hid_used, k - N_HID + 1)
                fw = FW[k]
                to = hid0[0:fw, k % N_HID, :, :].rearrange("p a (h t) -> p a h t", h=2)
                of = hidf[0:fw, 2 * NF - 2 - 2 * k:2 * NF - 2 * k, :]
                for half in range(2):
                    link(dve.tensor_copy(to[:, 0, half, :], of[:, 1 - half, :]))
                    ins = dve.tensor_tensor(to[:, 1, half, :], of[:, 1 - half, :], to[:, 0, half, :].bitcast(F32), ALU.subtract)
                ins.then_inc(hid_ready, 1)

            dve.wait_ge(up_used, 2 * NF)
            for t in range(NT):
                dve.wait_ge(ah_ready, t + 1)
                dve.tensor_tensor(attT[:, t % 2, 1, :, :], PS[:, t % 2, :].rearrange("p (k q) -> p k q", k=KD),
                                  attT[:, t % 2, 0, :, :].bitcast(F32), ALU.subtract).then_inc(al_ready, 1)
                if t:
                    s_out(t - 1)
            hidden_split(0)
            s_out(NT - 1)
            for k in range(1, NF):
                hidden_split(k)
            dve.wait_ge(x_back, 16)

            def sums(J):
                i = J % NF
                fw = FW[i]
                dve.wait_ge(lr_copied, J + 1)
                for o in range(2):
                    dve.scalar_tensor_tensor(e_gu[0:fw, o, :], PS[0:fw, 2 + 2 * (J % 2) + o, :], gs[0:fw, o, i:i + 1],
                                             e_lr[0:fw, o, :], ALU.mult, ALU.add).then_inc((gsum_ready, up_used)[o], 1)

            def hidden(J):
                half, i = J // NF, J % NF
                fw = FW[i]
                if half == 1 and i == 0:
                    dve.wait_ge(dn_ready, NT + 4)
                dve.wait_ge(silu_ready, J + 1)
                dve.wait_ge(up_used, 2 * NF + J + 1)
                hid = e_gu[0:fw, 1, :]
                link(dve.tensor_tensor(hid, hid, e_gu[0:fw, 0, :], ALU.mult))
                link(dve.tensor_copy(hid1[0:fw, 0, i, :], hid))
                dve.tensor_tensor(hid1[0:fw, 1, i, :], hid, hid1[0:fw, 0, i, :].bitcast(F32), ALU.subtract).then_inc(hid_ready, 1)
                dve.wait_ge(hid_ready, NF + J + 1)

            def model(n):
                l, step, c = SSM_STEPS[n]
                nth = 2 * l + (step[-1] == "2")
                seq = slice(SEQ * c, SEQ * (c + 1))
                if step in ("var1", "var2"):
                    dve.wait_ge(ln_var, 2 * nth + c + 1)
                    dve.tensor_scalar(tstat[:, c, :], PS[:, c, SEQ:SEQ + 4], EPS, None, ALU.add).then_inc(ln_stat, 1)
                elif step in ("rstd1", "rstd2"):
                    dve.wait_ge(ln_copied, 2 * nth + c + 1)
                    dve.wait_ge(ln_rstd, 2 * nth + c + 1)
                    dve.tensor_tensor(act1[:, seq], act1[:, seq], PS[:, c, SEQ:2 * SEQ], ALU.mult).then_inc(ln_norm, 1)
                elif step == "sel":
                    dve.wait_ge(cv_sel, 2 * l + c + 1)
                    dve.wait_ge(rot_ready, 1)
                    dve.wait_ge(decay_ready, 1)
                    r = rot[:, l, :].unsqueeze(1).to_broadcast([P, 2, SEQ])
                    link(dve.tensor_tensor(dz[:, :, seq], PS[:, c, :].rearrange("p (j t) -> p j t", j=2), r, ALU.mult))
                    for j in range(2):
                        (note, link)[j](dve.tensor_tensor_scan(sv[:, 0, j, seq], decay[:, l:l + 1].to_broadcast([P, SEQ]), dz[:, j, seq],
                                                    start[:, l:l + 1], ALU.mult, ALU.add))
                    dve.tensor_tensor(dz[:, :, seq], sv[:, 0, :, seq], r, ALU.mult).then_inc(cv_mod, 1)
                elif step == "comb":
                    dve.wait_ge(cv_comb, 2 * l + c + 1)
                    dve.scalar_tensor_tensor(h[:, seq], PS[:, c, 0:SEQ], col("scl", l), h[:, seq], ALU.mult, ALU.add)\
                       .then_inc(h_ready, 1)
                    dve.wait_ge(h_ready, 4 * l + c + 1)
                elif step == "w2":
                    dve.wait_ge(w2_ready, 2 * l + c + 1)
                    dve.scalar_tensor_tensor(h[:, seq], PS[:, c, 0:SEQ], col("b2", l), h[:, seq], ALU.add, ALU.add)\
                       .then_inc(h_ready, 1)
                    dve.wait_ge(h_ready, 4 * l + 2 + c + 1)

            def spread(n):
                l, step, c = SSM_STEPS[n]
                nth = 2 * l + (step[-1] == "2")
                dve.wait_ge(ln_pow, 2 * nth + c + 1)
                dve.tensor_copy(tmp1[:, SEQ * c:SEQ * (c + 1)].rearrange("p (k e) -> p k e", k=4),
                                trs[:, c, :].unsqueeze(2).to_broadcast([P, 4, CH])).then_inc(ln_spread, 1)

            def down_sum(n):
                t = n % 4
                dve.wait_ge(lrd_ready, n + 1)
                dve.wait_ge(dn_ready, NT + n + 1)
                if n % 4 >= 2:
                    dve.wait_ge(fg_ready, n - 1)
                link(dve.tensor_tensor(e_gu[:, t % 2, :], PS[:, 2 + t, :], dscale_b[:], ALU.mult))
                dve.tensor_tensor(e_gu[:, t % 2, :], e_gu[:, t % 2, :], PS[:, 6 + t % 2, :], ALU.add).then_inc(fsum_ready, 1)

            def residual(n):
                dve.wait_ge(fg_ready, n + 1)
                link(dve.tensor_tensor(s_sb[:, n, :], s_sb[:, n, :], e_lr[:, n % 2, :], ALU.mult))
                dve.tensor_tensor(x[:, n, :], x[:, n, :], s_sb[:, n, :], ALU.add).then_inc(out_ready, 1)

            for kind, a, i in ORDER1:
                J = NF * a + i
                if kind == "dl":
                    dve.wait_ge(gs_ready, a + 1)
                    dve.tensor_tensor(x[:, a, :], x[:, a, :], ht0[:, a % 4, :], ALU.add).then_inc(x1_ready, 1)
                    if a % 2:
                        dve.wait_ge(x1_ready, a + 1)
                        statistics(1, a // 2)
                    if a == 2:
                        normalised(1, 0)
                elif kind == "tr" and a % 2:
                    ln_tiles(1, a // 2)
                elif kind == "lr":
                    n = 2 * a + i
                    dve.wait_ge(lr_inner, n + 1)
                    to = lrx[:, i, a * HALF:(a + 1) * HALF]
                    of = (act1, tmp1)[n % 2][0:LRR, :]
                    low = slice(2 * RANK, LRR)
                    link(dve.tensor_copy(to, of))
                    dve.tensor_tensor(to[low], of[low], to[low].bitcast(F32), ALU.subtract).then_inc(lr_split, 1)
                    if n == 1:
                        for o, name in ((0, "gate_s"), (1, "up_s")):
                            link(dve.tensor_scalar(gs[:, o, :], col(name, 0, NF), 0.005, None, ALU.mult))
                    if n == 3:
                        dve.wait_ge(late_loaded, 48)
                        link(dve.tensor_scalar(dscale_b[:], dscale_b[:], 0.005, None, ALU.mult))
                elif kind == "sums":
                    sums(J)
                elif kind == "hidden":
                    hidden(J)
                elif kind == "spread":
                    spread(a)
                elif kind == "ssm":
                    model(a)
                elif kind == "rd" and i == 3:
                    dve.wait_ge(rd_copied, a + 1)
                    if a:
                        dve.wait_ge(lrd_ready, 4)
                    low = slice(2 * RANK, LRR)
                    link(dve.tensor_copy(lrh[:], e_lr[0:LRR, 0, :]))
                    dve.tensor_tensor(lrh[low, :], e_lr[low, 0, :], lrh[low, :].bitcast(F32), ALU.subtract).then_inc(rd_split, 1)
                elif kind == "wout":
                    t = a
                    dve.wait_ge(wout_ready, t + 1)
                    if t < 4:
                        link(dve.tensor_tensor(dz[:, 0, :], PS[:, t % 2, :], row_b[:], ALU.add))
                        dve.tensor_tensor(dz[:, 1, :], dz[:, 0, :], s_sb[:, t, :], ALU.mult).then_inc(s_ready, 1)
                        dve.wait_ge(s_ready, NT + t + 1)
                        dve.tensor_tensor(x[:, t, :], x[:, t, :], dz[:, 1, :], ALU.add).then_inc(out_ready, 1)
                        dve.wait_ge(out_ready, t + 1)
                    else:
                        dve.tensor_tensor(s_sb[:, t, :], PS[:, t % 2, :], row_b[:], ALU.add).then_inc(s_ready, 1)
                        dve.wait_ge(s_ready, NT + t + 1)
                elif kind == "fin":
                    down_sum(i)
                elif kind == "end":
                    down_sum(4 + i)
                    if i:
                        residual(4 + i - 1)
                    if i == 3:
                        residual(7)

        @block.tensor
        def _(pe):
            def products(out, pairs):
                pairs = list(pairs)
                for n, (w, m) in enumerate(pairs):
                    ins = pe.matmul(out, w, m, start=n == 0, stop=n == len(pairs) - 1)
                return ins

            PARTS = ((0, 0), (0, 1), (1, 0))

            def transposes(n, t):
                pe.wait_ge(xn_ready, NT * n + t + 1)
                if t >= 2:
                    pe.wait_ge(xl_ready, NT * n + t - 1)
                bank = PS[:, LN_BANK[n] + t % 2, :]
                for k in range(KD):
                    ins = pe.transpose(bank[:, k * P:(k + 1) * P], xn[:, t % 2, k * P:(k + 1) * P], ident[:])
                ins.then_inc(xt_ready, 1)

            pe.wait_ge(ident_ready, 1)

            def qkv(half, u):
                tok = slice(half * HALF, (half + 1) * HALF)
                if u == 0:
                    pe.wait_ge(xl_ready, 4 * half + 4)
                if half or u >= 2:
                    if half and u == 1:
                        pe.wait_ge(v_ready, 1)
                    else:
                        pe.wait_ge(proj_ready, 5 * half + max(u - 1, 0))
                if half == 0 and u in (0, 2, 4):
                    chunk_ready(pe, u // 2)
                if u < 5:
                    products(PS[:, u % 2, :], ((wqkv[:, a, k, u * P:(u + 1) * P], xnT[:, b, k, tok])
                                               for k in range(KD) for a, b in PARTS)).then_inc(qkv_ready, 1)
                else:
                    for q in range(4):
                        t = slice((4 * half + q) * P, (4 * half + q + 1) * P)
                        ins = products(PS[:, 1, q * P:(q + 1) * P], ((xnT[:, b, k, t], wqkv[:, a, k, 640:768])
                                                                    for k in range(KD) for a, b in PARTS))
                    ins.then_inc(qkv_ready, 1)

            K1 = 6 * DH
            K2 = K1 + 4

            def turn_bank(n):
                if n >= 2:
                    pe.wait_ge(turn_read, n - 1)
                return PS[:, 2 + n % 2, :]

            def score_max(b, i):
                (m, qt, g), buf, n = max_item(i), b % 2, turn("max", b, i)
                if i == 0:
                    pe.wait_ge(qs_loaded[buf], 48 * (b // 2 + 1))
                    if b == 0:
                        pe.wait_ge(consts_ready, 1)
                        pe.wait_ge(xl_ready, NT)
                bank = turn_bank(n)
                if qt == 0:
                    pe.matmul(bank, identb[:], maskA[:].rearrange("p g k -> p (g k)"), start=True, stop=False)
                    for o in range(2):
                        ins = pe.matmul(bank[:, 256 * o:256 * (o + 1)], qs[0:K1, buf, m, g + o, 0:P], ks[0:K1, buf, :, m, 0:P],
                                        start=False, stop=o == 1)
                else:
                    pe.matmul(bank.rearrange("p (j k) -> p j k", j=2)[:, :, P:SEQ], identb[:], maskA[:, 0:2, :],
                              start=True, stop=False, skip_group_check=True)
                    ins = pe.matmul(bank, qs[0:K1, buf, m, g, P:SEQ], ks[0:K1, buf, :, m, :],
                                    start=False, stop=True, skip_group_check=True)
                ins.then_inc(turn_ready, 1)

            def max_transposed(b):
                n = turn("maxT", b, 0)
                pe.wait_ge(turn_read, n)
                for qt in range(2):
                    ins = pe.transpose(PS[0:32, 2 + n % 2, qt * P:(qt + 1) * P], negmax[:, b, qt, :], ident[:])
                ins.then_inc(turn_ready, 1)

            TILES = ((0, 0), (0, 1), (1, 1))

            def scores(G, kv):
                b, quad, (kt, qt) = G // 6, G // 3 % 2, TILES[G % 3]
                m, j, buf, n = 2 * quad + kv // 2, kv % 2, b % 2, 4 * G + kv
                if G % 6 == 0 and kv == 0:
                    pe.wait_ge(m_loaded[buf], 16 * (b // 2 + 1))
                if n < 2:
                    pe.wait_ge((proj_ready, v_ready)[n], (10, 2)[n])
                else:
                    pe.wait_ge(exp_ready, n - 1)
                pe.matmul(PS[:, n % 2, :], ks[0:K2, buf, j, m, kt * P:(kt + 1) * P],
                          qs[0:K2, buf, m, :, qt * P:(qt + 1) * P], start=True, stop=True).then_inc(s2_ready, 1)

            def values(G):
                b, quad, c = G // 6, G // 3 % 2, G % 3
                kt, qt = TILES[c]
                if c < 2 and G >= 3:
                    pe.wait_ge(ot_ready, 2 * (G // 3) - 1 + c)
                for kv in range(4):
                    n = 4 * G + kv
                    if c == 1:
                        pe.wait_ge(exp_ready, n + 1)
                    else:
                        pe.wait_ge(masked, 8 * (G // 3) + 4 * (c // 2) + kv + 1)
                    ins = pe.matmul(PS[32 * kv:32 * kv + 32, 5 + qt, :], v_sb[:, 2 * b + kt, 4 * quad + kv, :], probs[:, n % 8, :],
                                    start=c < 2, stop=c != 1)
                ins.then_inc(pv_ready, 1)

            def tokens_back(bq, qt):
                n = turn("back", bq, qt)
                pe.wait_ge(ot_ready, 2 * bq + qt + 1)
                bank = turn_bank(n)
                for g in range(GRP):
                    ins = pe.transpose(bank[:, g * P:(g + 1) * P], outT[:, qt, g * P:(g + 1) * P], ident[:])
                ins.then_inc(turn_ready, 1)

            used = [0]

            def next_chunk(kind, index, half=0):
                c, rc = chunk_place(kind, index, half)
                assert rc == used[0], (kind, index, rc, used)
                used[0] += 1
                chunk_ready(pe, c)
                return ring[:, rc % N_RING, :, :]

            slot = [None]

            def gate_up(job, piece):
                i, half, o = job // 2, job % 2, piece // 2
                if piece == 0 and half == 0:
                    slot[0] = next_chunk("gu0", i)
                if piece == 0 and job:
                    pe.wait_ge(gate_used, job)
                if piece == 2 and job:
                    pe.wait_ge(up_used, job)
                fw, w = FW[i], slot[0]
                tok = slice(half * HALF, (half + 1) * HALF)
                for k in (0, 1) if piece % 2 == 0 else (2, 3):
                    at = 4 * fw * o + k * fw
                    for n, (a, b) in enumerate(PARTS):
                        ins = pe.matmul(PS[0:fw, 4 + 3 * o, :], w[:, a, at:at + fw], xnT[:, b, k, tok],
                                        start=k == 0 and n == 0, stop=k == 3 and n == 2)
                if piece % 2:
                    ins.then_inc(gu_ready, 1)

            for kind, a, i in ATT:
                if kind == "tr":
                    transposes(0, a)
                elif kind == "qkv":
                    qkv(a, i)
                elif kind == "max":
                    score_max(a, i)
                elif kind == "maxT":
                    max_transposed(a)
                elif kind == "scores":
                    scores(a, i)
                elif kind == "values":
                    values(a)
                elif kind == "back":
                    tokens_back(a, i)
                elif kind == "ffn":
                    gate_up(a, i)

            pe.wait_ge(turn_read, len(TURNS))
            for t in range(NT + 1):
                if t < NT:
                    if t >= 2:
                        pe.wait_ge(al_ready, t - 1)
                    for k in range(KD):
                        ins = pe.transpose(PS[:, t % 2, k * P:(k + 1) * P], s_sb[:, t, k * P:(k + 1) * P], ident[:])
                    ins.then_inc(at_ready, 1)
                if t == 0:
                    chunk_ready(pe, WO + 1)
                    continue
                pe.wait_ge(al_ready, t)
                if t >= 3:
                    pe.wait_ge(s_ready, t - 2)
                products(PS[:, 2 + (t - 1) % 2, :],
                         ((attT[:, (t - 1) % 2, a, k, :], wo_hl[:, k // 2, w, k % 2, :])
                          for k in range(KD) for a, w in PARTS)).then_inc(wo_ready, 1)

            pe.wait_ge(up_used, 2 * NF)
            pe.wait_ge(s_ready, NT)
            def down(t, k, w):
                for n, (a, b) in enumerate(PARTS):
                    ins = pe.matmul(PS[:, t, :], hid0[0:FW[k], k % N_HID, a, t * P:(t + 1) * P],
                                    w[0:FW[k], b, k % 2 * D:(k % 2 + 1) * D],
                                    start=k == 0 and n == 0, stop=k == NF - 1 and n == 2)
                return ins

            for k in range(8):
                if k % 2 == 0:
                    w = next_chunk("dn0", k // 2)
                pe.wait_ge(hid_ready, k + 1)
                for t in range(NT):
                    ins = down(t, k, w)
                ins.then_inc(hid_used, 1)
            last_chunks = [None, None]

            def model(n):
                l, step, c = SSM_STEPS[n]
                nth = 2 * l + (step[-1] == "2")
                seq = slice(SEQ * c, SEQ * (c + 1))
                lower, upper = PS[:, c, 0:SEQ], PS[:, c, SEQ:2 * SEQ]
                if step in ("cen1", "cen2"):
                    if nth == 0:
                        pe.wait_ge(h0_ready, 1)
                        pe.wait_ge(lr_split, 4)
                        pe.wait_ge(late_consts, 1)
                    else:
                        pe.wait_ge(h_ready, 2 * (nth - 1) + c + 1)
                    pe.matmul(lower, center[:], h[:, seq], start=True, stop=True).then_inc(ln_cen, 1)
                elif step in ("var1", "var2"):
                    pe.wait_ge(ln_sq, 2 * nth + c + 1)
                    for k in range(2):
                        ins = pe.matmul(upper[:, 2 * k:2 * k + 2], tmp1[:, c * SEQ + k * P:c * SEQ + (k + 1) * P], bdc[:],
                                        start=True, stop=True)
                    ins.then_inc(ln_var, 1)
                elif step in ("rstd1", "rstd2"):
                    pe.wait_ge(ln_spread, 2 * nth + c + 1)
                    for k in range(2):
                        ins = pe.transpose(upper[:, k * P:(k + 1) * P], tmp1[:, c * SEQ + k * P:c * SEQ + (k + 1) * P], ident[:])
                    ins.then_inc(ln_rstd, 1)
                elif step == "sel":
                    pe.wait_ge(ln_out, 2 * nth + c + 1)
                    for j, bank in enumerate((lower, upper)):
                        ins = pe.matmul(bank, sel[:, j, :], act1[:, seq], start=True, stop=True)
                    ins.then_inc(cv_sel, 1)
                elif step == "comb":
                    pe.wait_ge(cv_mod, 2 * l + c + 1)
                    products(lower, ((comb[:, j, :], dz[:, j, seq]) for j in range(2))).then_inc(cv_comb, 1)
                elif step in ("w1a", "w1b"):
                    ft = int(step == "w1b")
                    if ft == 0:
                        pe.wait_ge(ln_out, 2 * (2 * l + 1) + c + 1)
                    else:
                        pe.wait_ge(w1_act, 4 * l + c + 1)
                    for half, bank in enumerate((lower, upper)):
                        ins = pe.matmul(bank, w1v[:, l, half, ft * P:(ft + 1) * P], act1[:, seq], start=True, stop=True)
                    ins.then_inc(w1_ready, 1)
                elif step == "w2":
                    pe.wait_ge(w1_act, 4 * l + 2 + c + 1)
                    for half in range(2):
                        r = slice(CH * half, CH * half + CH)
                        ins = products(PS[r, c, 0:SEQ], ((w2v[:, l, ft, :], sv[:, ft, half, seq]) for ft in range(2)))
                    ins.then_inc(w2_ready, 1)

            def low_rank_down(half, t):
                if t >= 2:
                    pe.wait_ge(fsum_ready, 4 * half + t - 1)
                pe.matmul(PS[:, 6 + t % 2, :], lrh[:, t * P:(t + 1) * P], lrdb[:], start=True, stop=True)\
                  .then_inc(lrd_ready, 1)

            def down1(t, k, w):
                for p in range(2):
                    ins = pe.matmul(PS[:, 2 + t, :], hid1[0:FW[k], p, k, t * P:(t + 1) * P],
                                    w[0:FW[k], 0, k % 2 * D:(k % 2 + 1) * D],
                                    start=k == 0 and p == 0, stop=k == NF - 1 and p == 1)
                return ins

            cur = [None]
            for kind, a, i in ORDER1:
                J = NF * a + i
                tok = slice(a * HALF, (a + 1) * HALF)
                if kind == "dl":
                    if a == 0:
                        last_chunks[0] = next_chunk("dn0", 4)
                        pe.wait_ge(hid_ready, NF)
                    for t in (0, 1) if a == 0 else (a + 1,) if a < NT - 1 else ():
                        for k in (8, 9):
                            down(t, k, last_chunks[0])
                    if a == 0:
                        last_chunks[1] = next_chunk("dn0", 5)
                    down(a, NF - 1, last_chunks[1]).then_inc(dn_ready, 1)
                elif kind == "tr":
                    transposes(1, a)
                elif kind == "lr":
                    n = 2 * a + i
                    if n == 0:
                        pe.wait_ge(xl_ready, NT + 4)
                        pe.wait_ge(g_ready, 6)
                        chunk_ready(pe, LRA)
                    if n == 3:
                        pe.wait_ge(lr_inner, 3)
                    g0 = LRR * KD * i
                    products(PS[0:LRR, LR_BANK[n], :], ((lra_hl[:, p, g0 + k * LRR:g0 + (k + 1) * LRR],
                                                         xnT[:, q, k, a * HALF:(a + 1) * HALF])
                                                        for k in range(KD) for p, q in PARTS)).then_inc(lr_ready, 1)
                elif kind == "win":
                    pe.wait_ge(xl_ready, 2 * NT)
                    chunk_ready(pe, WIN)
                    products(PS[:, 0, :], ((win_hl[:, b, k, (CH, 0)[half]:(CH, 0)[half] + P], xnT[:, c, k, half * HALF:(half + 1) * HALF])
                                           for half in range(2) for k in range(KD) for b, c in PARTS)).then_inc(win_ready, 1)
                elif kind in ("gate", "up"):
                    o = int(kind == "up")
                    fw = FW[i]
                    if o == 0:
                        cur[0] = next_chunk("gu1", i, a)
                        if J >= 2:
                            pe.wait_ge(up_used, 2 * NF + J - 1)
                        elif J == 0:
                            pe.wait_ge(g_ready, NT)
                            pe.wait_ge(lr_inner, 1)
                        else:
                            pe.wait_ge(lr_inner, 2)
                        if a and i < 2:
                            pe.wait_ge(fsum_ready, 4)
                    w = cur[0]
                    g0 = 4 * fw * o
                    products(PS[0:fw, 2 + 2 * (J % 2) + o, :], ((w[:, 0, g0 + k * fw:g0 + (k + 1) * fw], xnT[:, q, k, tok])
                                                                for k in range(KD) for q in range(2)))
                    if o == 0 and J:
                        pe.wait_ge(lr_copied, J)
                    if i == 0 and o == 0:
                        pe.wait_ge(lr_split, 2 * a + 2)
                    ins = pe.matmul(PS[0:fw, 6 + o, :], w[0:LRR, 1, o * fw:(o + 1) * fw], lrx[:, o, tok], start=True, stop=True)
                    if o:
                        ins.then_inc(gu_ready, 1)
                elif kind == "ssm":
                    model(a)
                elif kind == "rd":
                    if i == 0:
                        cur[0] = next_chunk("lrd", 0, a)
                        pe.wait_ge(lr_copied, NF * (a + 1))
                    w = cur[0]
                    for k in range(3 * i, min(3 * i + 3, NF)):
                        pe.wait_ge(hid_ready, NF + NF * a + k + 1)
                        for n, (p, q) in enumerate(PARTS):
                            ins = pe.matmul(PS[0:LRR, 6, :], w[0:FW[k], p, k * LRR:(k + 1) * LRR], hid1[0:FW[k], q, k, :],
                                            start=k == 0 and n == 0, stop=k == NF - 1 and n == 2)
                    if i == 3:
                        ins.then_inc(rd_ready, 1)
                elif kind == "dn":
                    if i % 2 == 0:
                        cur[0] = next_chunk("dn1", i // 2, a)
                    if i == 0:
                        pe.wait_ge(up_used, 2 * NF + NF * (a + 1))
                    for t in range(4):
                        ins = down1(t, i, cur[0])
                        if i == NF - 1:
                            ins.then_inc(dn_ready, 1)
                    if i % 2:
                        ins.then_inc(chunk_used, 1)
                elif kind == "wout":
                    t = a
                    half = t // 4
                    r = slice(CH * half, CH * half + CH)
                    if t == 0:
                        pe.wait_ge(ln_out, 4 * DEPTH + 2)
                    if t >= 2:
                        pe.wait_ge(s_ready, NT + t - 1)
                    pe.matmul(PS[:, t % 2, :], act1[r, (t % 4) * P:(t % 4 + 1) * P], wov[r, :], start=True, stop=True)\
                      .then_inc(wout_ready, 1)
                elif kind == "fin":
                    if i == 0:
                        chunk_ready(pe, chunk_place("lrb", 0, a)[0])
                        pe.wait_ge(rd_split, a + 1)
                    low_rank_down(a, i)
                elif kind == "end":
                    if i == 0:
                        last_chunks[0] = next_chunk("dn1", 4, a)
                        chunk_ready(pe, chunk_place("lrb", 0, a)[0])
                        pe.wait_ge(rd_split, a + 1)
                    low_rank_down(a, i)
                    for t in (0, 1) if i == 0 else (i + 1,) if i < 3 else ():
                        for k in (8, 9):
                            down1(t, k, last_chunks[0])
                    if i == 0:
                        last_chunks[1] = next_chunk("dn1", 5, a)
                    down1(i, NF - 1, last_chunks[1]).then_inc(dn_ready, 1)


_NEEDED = ("x", "wq", "wk", "wv", "wo", "gu0", "dn0", "winT", "lra", "gu1", "lrb", "lrd", "lrdb", "dn1", "cols", "bv", "bo",
           "bout", "dscale", "ssmw")


def packed_gate_up(gate, up, np):
    blocks = []
    for i in range(NF):
        o = slice(i * P, i * P + FW[i])
        for w in (gate, up):
            blocks.append(w[o, :].T.reshape(KD, P, FW[i]).transpose(1, 0, 2).reshape(P, KD * FW[i]))
    return np.ascontiguousarray(np.concatenate(blocks, axis=1))


def kernel(**inputs):
    import numpy as np
    import concourse.bacc as bacc
    from concourse.bass_utils import run_bass_kernel_spmd

    v = {k: np.asarray(a) for k, a in inputs.items()}
    l0 = {k[3:]: a for k, a in v.items() if k.startswith("L0_")}
    l1 = {k[3:]: a for k, a in v.items() if k.startswith("L1_")}
    twice = lambda a: np.concatenate([a, a], axis=0)
    at = lambda n: l1["attn_" + n]

    def tiles(a):
        return np.concatenate([a, a[:NF * P - F]]).reshape(NF, P).T

    by_pair = lambda a, g: a.reshape(a.shape[0], 4, 2, g * DH).transpose(0, 2, 1, 3).reshape(a.shape)
    columns = {
        "bq": by_pair(l0["attn_bq"][None], GRP).reshape(4, P).T, "bk": by_pair(l0["attn_bk"][None], 1).reshape(P, 1),
        "ln1_w": twice(at("ln1_w").T), "ln1_b": twice(at("ln1_b").T), "scl": twice(at("sc_lin").T),
        "ln2_w": twice(at("ln2_w").T), "ln2_b": twice(at("ln2_b").T), "b2": twice(at("b2").T),
        "b1": at("b1").reshape(DEPTH * 2, P).T,
        "lnl_w": twice(at("lnl_w").reshape(CH, 1)), "lnl_b": twice(at("lnl_b").reshape(CH, 1)),
        "bin": twice(at("bin").reshape(CH, 1)),
        "lc_a": np.concatenate([at("lc_re").T, at("lc_im").T]), "lc_b": np.concatenate([at("lc_im").T, at("lc_re").T]),
        "ph_re": twice(at("phz_re").T), "ph_im": twice(at("phz_im").T),
        "gate_s": tiles(l1["ffn_gate_scale"]), "up_s": tiles(l1["ffn_up_scale"]),
    }
    w1 = np.zeros((2, CH, DEPTH, 2, 256), np.float32)
    for half in range(2):
        w1[half, :, :, half, :] = at("W1").transpose(2, 0, 1)
    w1 = w1.reshape(P, DEPTH * 512)
    w2 = at("W2").reshape(DEPTH, CH, 2, P).transpose(3, 0, 2, 1).reshape(P, DEPTH * 2 * CH)
    low_rank = lambda a: np.concatenate([a, a, a], axis=1)
    lra = np.concatenate([low_rank(l1[n]).reshape(KD, P, LRR).transpose(1, 0, 2).reshape(P, KD * LRR)
                          for n in ("ffn_gate_A", "ffn_up_A")], axis=1)
    b_blocks = []
    for i in range(NF):
        for n in ("ffn_gate_B", "ffn_up_B"):
            b_blocks.append(l1[n][:, i * P:i * P + FW[i]])
    lrb = np.concatenate(b_blocks, axis=1)
    down_a = low_rank(l1["ffn_down_A"])
    down_a = np.concatenate([down_a, down_a[:NF * P - F]])
    arrays = {
        "x": l0["attn_x"].reshape(TOK, D), "wq": by_pair(l0["attn_Wq"], GRP), "wk": by_pair(l0["attn_Wk"], 1), "wv": l0["attn_Wv"], "wo": l0["attn_Wo"],
        "gu0": packed_gate_up(l0["ffn_W_gate"], l0["ffn_W_up"], np), "dn0": l0["ffn_W_down"].T,
        "winT": at("Win").T, "lra": lra, "gu1": packed_gate_up(l1["ffn_gate_q"], l1["ffn_up_q"], np),
        "lrb": np.concatenate([lrb, lrb, lrb]), "lrd": down_a.reshape(NF, P, LRR).transpose(1, 0, 2).reshape(P, NF * LRR),
        "lrdb": np.concatenate([l1["ffn_down_B"]] * 3), "dn1": l1["ffn_down_q"].T,
        "cols": np.concatenate([columns[n] for n in COLS], axis=1),
        "bv": l0["attn_bv"].reshape(1, P), "bo": l0["attn_bo"].reshape(1, D), "bout": at("bout").reshape(1, D),
        "dscale": l1["ffn_down_scale"].reshape(1, D),
        "ssmw": np.concatenate([w1, w2, twice(at("Wout").T)], axis=1),
    }
    arrays = {n: np.ascontiguousarray(arrays[n]) for n in _NEEDED}
    nc = bacc.Bacc("TRN2", target_bir_lowering=False, num_devices=1)
    A = {n: nc.dram_tensor("in_" + n, a.shape, mybir.dt.from_np(a.dtype), kind="ExternalInput").ap()
         for n, a in arrays.items()}
    A["out"] = nc.dram_tensor("out", (TOK, D), F32, kind="ExternalOutput").ap()
    build(nc, A)
    r = run_bass_kernel_spmd(nc, [{"in_" + n: a for n, a in arrays.items()}], core_ids=[0])
    return r.results[0]["out"].reshape(4, SEQ, D)
```
